# Optimizing a Trainium2 kernel written in Bass

```python
import numpy as np
import jax
import jax.numpy as jnp

def _softmax(x, axis=-1):
    return jax.nn.softmax(x, axis=axis)

def _gelu(x):
    return jax.nn.gelu(x, approximate=True)

def _silu(x):
    return jax.nn.silu(x)

def _sigmoid(x):
    return jax.nn.sigmoid(x)

def _layernorm(x, axis=-1, eps=1e-05):
    m = jnp.mean(x, axis=axis, keepdims=True)
    v = jnp.var(x, axis=axis, keepdims=True)
    return (x - m) / jnp.sqrt(v + eps)

def _scatter_add(tgt, idx, src, axis=0):
    return tgt.at[idx].add(src)

def _segment_sum(src, seg, n):
    return jax.ops.segment_sum(src, seg, n)
kernel_name = 'mk_adaln_attn_ffn_d1_seqx_r4_ddde0f'

def setup_inputs(seed: int=0):
    np.random.seed(seed)
    _w = jnp.asarray

    def _rec_inputs():
        import jax
        import jax.numpy as jnp
        _rk = jax.random.key(seed)
        x = 7.22e-05 + 1 * jax.random.normal(jax.random.fold_in(_rk, 1), (8, 256, 256), jnp.float32)
        _lenS = 256 - jax.random.randint(jax.random.fold_in(_rk, 7), (8,), 0, max(1, 256 // 4) + 1, jnp.int32)
        _lenS2 = 256 - jax.random.randint(jax.random.fold_in(_rk, 8), (8,), 0, max(1, 256 // 4) + 1, jnp.int32)
        cond_8 = -0.104238 + 1.01173 * jax.random.normal(jax.random.fold_in(_rk, 11), (8, 8), jnp.float32)
        return (x, cond_8)
    x, cond_8 = _rec_inputs()

    def _L0_cond_setup():
        import jax, jax.numpy as jnp
        import numpy as np
        TOP_K = 2
        NUM_MOE_LAYERS = 12

        def _gemma_mlp(x, gate_w, up_w, down_w):
            g = jnp.einsum('bsh,hi->bsi', x, gate_w)
            u = jnp.einsum('bsh,hi->bsi', x, up_w)
            return jnp.einsum('bsi,ih->bsh', jax.nn.gelu(g, approximate=True) * u, down_w)
        key = jax.random.key(seed)
        ks = jax.random.split(key, 8)
        B, S, H, I, E = (32, 64, 256, 1024, 8)
        std = 0.02
        return {'x': jax.random.normal(ks[0], (B, S, H), jnp.float32), 'router_logits': jax.random.normal(ks[1], (B, E), jnp.float32), 'skill_gate': jax.random.normal(ks[2], (E, H, I), jnp.float32) * std, 'skill_up': jax.random.normal(ks[3], (E, H, I), jnp.float32) * std, 'skill_down': jax.random.normal(ks[4], (E, I, H), jnp.float32) * std, 'shared_gate': jax.random.normal(ks[5], (H, I), jnp.float32) * std, 'shared_up': jax.random.normal(ks[6], (H, I), jnp.float32) * std, 'shared_down': jax.random.normal(ks[7], (I, H), jnp.float32) * std}
    _L0_cond_all = _L0_cond_setup()
    _L0_cond_in = {k: v for k, v in _L0_cond_all.items() if k in ('skill_gate', 'skill_up', 'skill_down', 'shared_gate', 'shared_up', 'shared_down')}
    del _L0_cond_all

    def _L0_attn_setup():
        import jax, jax.numpy as jnp
        import numpy as np
        L, B, E, H = (512, 8, 256, 16)
        D = E // H
        EPS = 0.001
        key = jax.random.key(seed)
        k1, k2, k3 = jax.random.split(key, 3)
        scale_in = (2.0 / (3 * E + E)) ** 0.5
        scale_out = (2.0 / (E + E)) ** 0.5
        return {'query': jax.random.normal(k1, (L, B, E), dtype=jnp.float32), 'in_proj_weight': jax.random.normal(k2, (3 * E, E), dtype=jnp.float32) * scale_in, 'in_proj_bias': jnp.zeros((3 * E,), dtype=jnp.float32), 'out_w': jax.random.normal(k3, (E, E), dtype=jnp.float32) * scale_out, 'out_b': jnp.zeros((E,), dtype=jnp.float32)}
    _L0_attn_all = _L0_attn_setup()
    _L0_attn_in = {k: v for k, v in _L0_attn_all.items() if k in ('in_proj_weight', 'in_proj_bias', 'out_w', 'out_b')}
    del _L0_attn_all

    def _L0_cond2_setup():
        import jax, jax.numpy as jnp
        import numpy as np
        R = 16
        ALPHA = 32.0
        SCALING = ALPHA / R
        key = jax.random.key(seed)
        ks = jax.random.split(key, 6)
        B, T, C, O, E = (16, 375, 256, 256, 8)
        x = jax.random.normal(ks[0], (B, T, C), dtype=jnp.float32)
        w = jax.random.uniform(ks[1], (B, E), dtype=jnp.float32)
        W_base = jax.random.normal(ks[2], (O, C), dtype=jnp.float32) * 0.02
        b_base = jax.random.normal(ks[3], (O,), dtype=jnp.float32) * 0.02
        As = jax.random.normal(ks[4], (E, R, C), dtype=jnp.float32) * 0.02
        Bs = jax.random.normal(ks[5], (E, O, R), dtype=jnp.float32) * 0.02
        return {'x': x, 'w': w, 'W_base': W_base, 'b_base': b_base, 'As': As, 'Bs': Bs}
    _L0_cond2_all = _L0_cond2_setup()
    _L0_cond2_in = {k: v for k, v in _L0_cond2_all.items() if k in ('W_base', 'b_base', 'As', 'Bs')}
    del _L0_cond2_all

    def _L0_ffn_setup():
        import jax, jax.numpy as jnp
        import numpy as np
        D = 256
        E = 12
        HS = 2 * D
        HR = 3 * D
        TAU = 1.5

        def _geglu(h):
            a, g = jnp.split(h, 2, axis=-1)
            return a * jax.nn.gelu(g, approximate=False)
        key = jax.random.key(seed)
        ks = jax.random.split(key, 12)

        def xavier(k, shape):
            fan_in, fan_out = (shape[-2], shape[-1])
            lim = jnp.sqrt(6.0 / (fan_in + fan_out))
            return jax.random.uniform(k, shape, jnp.float32, -lim, lim)
        x = jax.random.normal(ks[0], (2, 256, D), jnp.float32)
        Ws1 = xavier(ks[1], (D, 2 * HS))
        bs1 = jnp.zeros((2 * HS,), jnp.float32)
        Ws2 = xavier(ks[2], (HS, D))
        bs2 = jnp.zeros((D,), jnp.float32)
        We1 = xavier(ks[3], (E, D, 2 * HR))
        be1 = jnp.zeros((E, 2 * HR), jnp.float32)
        We2 = xavier(ks[4], (E, HR, D))
        be2 = jnp.zeros((E, D), jnp.float32)
        Wr = xavier(ks[5], (D, E))
        br = jnp.zeros((E,), jnp.float32)
        return {'x': x, 'Ws1': Ws1, 'bs1': bs1, 'Ws2': Ws2, 'bs2': bs2, 'We1': We1, 'be1': be1, 'We2': We2, 'be2': be2, 'Wr': Wr, 'br': br}
    _L0_ffn_all = _L0_ffn_setup()
    _L0_ffn_in = {k: v for k, v in _L0_ffn_all.items() if k in ('Ws1', 'bs1', 'Ws2', 'bs2', 'We1', 'be1', 'We2', 'be2', 'Wr', 'br')}
    del _L0_ffn_all
    return {'x': x, 'cond_8': cond_8, 'L0_cond_skill_gate': _L0_cond_in['skill_gate'], 'L0_cond_skill_up': _L0_cond_in['skill_up'], 'L0_cond_skill_down': _L0_cond_in['skill_down'], 'L0_cond_shared_gate': _L0_cond_in['shared_gate'], 'L0_cond_shared_up': _L0_cond_in['shared_up'], 'L0_cond_shared_down': _L0_cond_in['shared_down'], 'L0_attn_in_proj_weight': _L0_attn_in['in_proj_weight'], 'L0_attn_in_proj_bias': _L0_attn_in['in_proj_bias'], 'L0_attn_out_w': _L0_attn_in['out_w'], 'L0_attn_out_b': _L0_attn_in['out_b'], 'L0_cond2_W_base': _L0_cond2_in['W_base'], 'L0_cond2_b_base': _L0_cond2_in['b_base'], 'L0_cond2_As': _L0_cond2_in['As'], 'L0_cond2_Bs': _L0_cond2_in['Bs'], 'L0_ffn_Ws1': _L0_ffn_in['Ws1'], 'L0_ffn_bs1': _L0_ffn_in['bs1'], 'L0_ffn_Ws2': _L0_ffn_in['Ws2'], 'L0_ffn_bs2': _L0_ffn_in['bs2'], 'L0_ffn_We1': _L0_ffn_in['We1'], 'L0_ffn_be1': _L0_ffn_in['be1'], 'L0_ffn_We2': _L0_ffn_in['We2'], 'L0_ffn_be2': _L0_ffn_in['be2'], 'L0_ffn_Wr': _L0_ffn_in['Wr'], 'L0_ffn_br': _L0_ffn_in['br']}

def reference(x, cond_8, L0_cond_skill_gate, L0_cond_skill_up, L0_cond_skill_down, L0_cond_shared_gate, L0_cond_shared_up, L0_cond_shared_down, L0_attn_in_proj_weight, L0_attn_in_proj_bias, L0_attn_out_w, L0_attn_out_b, L0_cond2_W_base, L0_cond2_b_base, L0_cond2_As, L0_cond2_Bs, L0_ffn_Ws1, L0_ffn_bs1, L0_ffn_Ws2, L0_ffn_bs2, L0_ffn_We1, L0_ffn_be1, L0_ffn_We2, L0_ffn_be2, L0_ffn_Wr, L0_ffn_br):
    import jax
    import jax.numpy as jnp

    def _L0_cond_ref(x, router_logits, skill_gate, skill_up, skill_down, shared_gate, shared_up, shared_down):
        import jax, jax.numpy as jnp
        import numpy as np
        TOP_K = 2
        NUM_MOE_LAYERS = 12

        def _gemma_mlp(x, gate_w, up_w, down_w):
            g = jnp.einsum('bsh,hi->bsi', x, gate_w)
            u = jnp.einsum('bsh,hi->bsi', x, up_w)
            return jnp.einsum('bsi,ih->bsh', jax.nn.gelu(g, approximate=True) * u, down_w)
        B = x.shape[0]
        E = skill_gate.shape[0]
        rw = jax.nn.softmax(router_logits.astype(jnp.float32), axis=-1)
        w, sel = jax.lax.top_k(rw, TOP_K)
        w = w / w.sum(axis=-1, keepdims=True)
        w = w.astype(x.dtype)
        scale = 1.0 / NUM_MOE_LAYERS
        w = scale * w + (1.0 - scale) * jax.lax.stop_gradient(w)
        dense_w = jnp.zeros((B, E), x.dtype).at[jnp.arange(B)[:, None], sel].add(w)

        def step(acc, params):
            g, u, d, we = params
            return (acc + we[:, None, None] * _gemma_mlp(x, g, u, d), None)
        out, _ = jax.lax.scan(step, jnp.zeros_like(x), (skill_gate, skill_up, skill_down, dense_w.T))
        out = out + _gemma_mlp(x, shared_gate, shared_up, shared_down)
        return out

    def _L0_attn_ref(query, in_proj_weight, in_proj_bias, out_w, out_b):
        import jax, jax.numpy as jnp
        import numpy as np
        L, B, E, H = (512, 8, 256, 16)
        D = E // H
        EPS = 0.001
        tgt_len, bsz, embed_dim = query.shape
        qkv = query @ in_proj_weight.T + in_proj_bias
        q, k, v = jnp.split(qkv, 3, axis=-1)

        def to_heads(x):
            return x.reshape(tgt_len, bsz, H, D).transpose(1, 0, 2, 3)
        q = jax.nn.relu(to_heads(q))
        k = jax.nn.relu(to_heads(k))
        v = to_heads(v)
        idx = jnp.pi / 2 * jnp.arange(1, tgt_len + 1, dtype=jnp.float32)
        theta = (idx / tgt_len)[None, :, None, None]
        sin_t, cos_t = (jnp.sin(theta), jnp.cos(theta))
        q_ = jnp.concatenate([q * sin_t, q * cos_t], axis=-1)
        k_ = jnp.concatenate([k * sin_t, k * cos_t], axis=-1)
        kv = jnp.einsum('bshd,bshm->bhmd', k_, v)
        z = 1.0 / jnp.maximum(jnp.einsum('blhd,bhd->blh', q_, k_.sum(axis=1)), EPS)
        attn = jnp.einsum('blhd,bhmd,blh->blhm', q_, kv, z)
        attn = attn.transpose(1, 0, 2, 3).reshape(tgt_len, bsz, embed_dim)
        return attn @ out_w.T + out_b

    def _L0_cond2_ref(x, w, W_base, b_base, As, Bs):
        import jax, jax.numpy as jnp
        import numpy as np
        R = 16
        ALPHA = 32.0
        SCALING = ALPHA / R
        out = jnp.einsum('btc,oc->bto', x, W_base) + b_base
        h = jnp.einsum('btc,erc->bter', x, As)
        lora = jnp.einsum('bter,eor,be->bto', h, Bs, w)
        return out + lora * SCALING

    def _L0_ffn_ref(x, Ws1, bs1, Ws2, bs2, We1, be1, We2, be2, Wr, br):
        import jax, jax.numpy as jnp
        import numpy as np
        D = 256
        E = 12
        HS = 2 * D
        HR = 3 * D
        TAU = 1.5

        def _geglu(h):
            a, g = jnp.split(h, 2, axis=-1)
            return a * jax.nn.gelu(g, approximate=False)
        B, T, Dm = x.shape
        xf = x.reshape(-1, Dm)
        ys = _geglu(xf @ Ws1 + bs1) @ Ws2 + bs2
        logits = (xf @ Wr + br) / TAU
        top_val, top_idx = jax.lax.top_k(logits, 2)
        top_w = jax.nn.softmax(top_val, axis=-1)
        onehot = jax.nn.one_hot(top_idx, E, dtype=x.dtype)
        w = jnp.einsum('nke,nk->ne', onehot, top_w)
        h = jnp.einsum('nd,edh->enh', xf, We1) + be1[:, None, :]
        act = _geglu(h)
        yE = jnp.einsum('enh,ehd->end', act, We2) + be2[:, None, :]
        yr = jnp.einsum('end,ne->nd', yE, w)
        return (ys + yr).reshape(B, T, Dm)
    x = x + _L0_attn_ref(_L0_cond_ref(x, cond_8, L0_cond_skill_gate, L0_cond_skill_up, L0_cond_skill_down, L0_cond_shared_gate, L0_cond_shared_up, L0_cond_shared_down), L0_attn_in_proj_weight, L0_attn_in_proj_bias, L0_attn_out_w, L0_attn_out_b)
    x = x + _L0_ffn_ref(_L0_cond2_ref(x, cond_8, L0_cond2_W_base, L0_cond2_b_base, L0_cond2_As, L0_cond2_Bs), L0_ffn_Ws1, L0_ffn_bs1, L0_ffn_Ws2, L0_ffn_bs2, L0_ffn_We1, L0_ffn_be1, L0_ffn_We2, L0_ffn_be2, L0_ffn_Wr, L0_ffn_br)
    return x

_drawn_inputs = setup_inputs


def setup_inputs(seed=0):
    import zlib

    import numpy as np

    out = dict(_drawn_inputs(seed))
    spreads = {'L0_attn_in_proj_bias': (0.0, 0.1),
     'L0_attn_out_b': (0.0, 0.1),
     'L0_ffn_bs1': (0.0, 2.0),
     'L0_ffn_bs2': (0.0, 0.8),
     'L0_ffn_be1': (0.0, 0.621),
     'L0_ffn_be2': (0.0, 0.8),
     'L0_ffn_br': (0.0, 0.1)}
    factors = {'L0_cond_skill_gate': 6.569,
     'L0_cond_skill_up': 6.697,
     'L0_cond_skill_down': 6.424,
     'L0_cond_shared_gate': 5.09,
     'L0_cond_shared_up': 4.809,
     'L0_cond_shared_down': 4.796,
     'L0_attn_in_proj_weight': 4.098,
     'L0_cond2_b_base': 3.408,
     'L0_ffn_We1': 2.801,
     'L0_ffn_We2': 2.722}
    for name, (base, spread) in spreads.items():
        noise = np.random.default_rng([zlib.crc32(name.encode()), seed]).standard_normal(out[name].shape)
        drawn = base * np.exp(spread * noise) if base else spread * noise
        out[name] = jnp.asarray(drawn.astype(out[name].dtype))
    for name, factor in factors.items():
        out[name] = (out[name] * factor).astype(out[name].dtype)
    return out
```

```python
from contextlib import ExitStack

import numpy as np

import concourse.bass as bass
from concourse import mybir

F32 = mybir.dt.float32
F32R = mybir.dt.float32r
I32 = mybir.dt.int32
U32 = mybir.dt.uint32
ALU = mybir.AluOpType
ACT = mybir.ActivationFunctionType
AX_X = mybir.AxisListType.X
ds = bass.ds

P = 128
B, S, D = 8, 256, 256
T = B * S
C = D // P
TT = T // P
COND_E, COND_I, COND_K = 8, 1024, 2
PAIR = 2 * P
PIECE = C * PAIR
CHUNK = 3 * PIECE
COND_PAIRS = COND_I // PAIR
MLPS = 1 + COND_K
H, HD = 16, 16
EPS = 1e-3
SG = 4
SGP = S // SG
GRP = 16
NG = SGP // GRP
SGT = SGP * B
LR = 16
LORA_SCALE = 2.0
E, HS, HR = 12, 512, 768
TAU = 1.5
ES = 256
NT = (2 * T + E * (ES - 1)) // ES
SLOTS = NT * ES
FFN_PAIRS = HR // PAIR
BLK = 512
NB = T // BLK

C_ID, C_MASK, C_TRI, C_ONE = 0, P, 2 * P, 3 * P
C_SEG = 4 * P
C_IOTA = C_SEG + TT * E
C_EVEN = C_IOTA + E
C_ODD = C_EVEN + 1
C_J256 = C_ODD + 1
C_TILE = C_J256 + E * 8
C_W = C_TILE + NT * E

V_BQ, V_BK, V_OB, V_BB, V_BA, V_BG, V_W = 0, 2, 4, 6, 8, 12, 16
R_BV, R_BS2, R_BR, R_W = 0, D, 2 * D, 2 * D + E
W_QKV, W_O, W_B, W_A, W_L, W_W = 0, 1536, 2048, 2560, 2816, 3072


class Chip:

    def __init__(self, ins, out):
        self.xT = ins["xT"]
        self.cond_8 = ins["cond_8"]
        self.cond_w = ins["cond_w"]
        self.ffn_w = ins["ffn_w"]
        self.shared_w = ins["shared_w"]
        self.attn_w = ins["attn_w"]
        self.vec = ins["vec"]
        self.rows = ins["rows"]
        self.router = ins["router"]
        self.lora_w = ins["lora_w"]
        self.be1 = ins["be1"]
        self.be2 = ins["be2"]
        self.consts = ins["consts"]
        self.out = out


def stage_cond(nc, k):
    with ExitStack() as ctx:
        def sb(name, shape, dt=F32):
            return ctx.enter_context(nc.sbuf_tensor("a_" + name, shape, dt))

        def ps(name, shape, dt=F32):
            return ctx.enter_context(nc.psum_tensor("a_" + name, shape, dt))

        def sem(name):
            return ctx.enter_context(nc.semaphore("a_" + name))

        RING = 4
        NQ = 2 * MLPS * COND_PAIRS
        BQ = NQ // 2
        XP = COND_PAIRS * COND_K
        STEPS = B // 2

        cond = sb("cond", [B, COND_E])
        neg_top = sb("neg_top", [B, 1])
        ex = sb("ex", [B, COND_E])
        ex_sum = sb("ex_sum", [B, 1])
        ex_rec = sb("ex_rec", [B, 1])
        prob = sb("prob", [B, COND_E])
        top = sb("top", [B, 8])
        top_i = sb("top_i", [B, 8], U32)
        pair_sum = sb("pair_sum", [B, 1])
        pair_rec = sb("pair_rec", [B, 1])
        wk = sb("wk", [B, COND_K])
        wk1 = sb("wk1", [B, COND_K])
        wk3 = sb("wk3", [B, MLPS])
        w_row = sb("w_row", [1, B * MLPS])
        i_row = sb("i_row", [1, B * COND_K], U32)
        w_col = sb("w_col", [P, B * MLPS])

        w_raw = [sb(f"w_raw{i}", [P, CHUNK]) for i in range(RING)]
        w_hi = sb("w_hi", [P, RING + COND_PAIRS, CHUNK], F32R)
        w_lo = sb("w_lo", [P, RING + COND_PAIRS, CHUNK], F32R)
        x_raw = [sb(f"x_raw{i}", [P, C, S]) for i in range(2)]
        x_hi = [sb(f"x_hi{i}", [P, C, S], F32R) for i in range(2)]
        x_lo = [sb(f"x_lo{i}", [P, C, S], F32R) for i in range(2)]
        g_act = [sb(f"g_act{i}", [P, 2 * S]) for i in range(2)]
        hid = [sb(f"hid{i}", [P, 2 * S]) for i in range(2)]
        h_hi = [sb(f"h_hi{i}", [P, 2 * S], F32R) for i in range(2)]
        h_lo = [sb(f"h_lo{i}", [P, 2 * S], F32R) for i in range(2)]
        c_sb = sb("c_sb", [P, B, C, S])

        ps_g = [ps(f"ps_g{i}", [P, 2 * S]) for i in range(2)]
        ps_u = [ps(f"ps_u{i}", [P, 2 * S]) for i in range(2)]
        ps_d = [ps(f"ps_d{i}", [P, C, S]) for i in range(2)]
        ps_w = ps("ps_w", [P, 512])

        cond_in = sem("cond_in")
        ones_in = sem("ones_in")
        route = sem("route")
        exped = sem("exped")
        rows_in = sem("rows_in")
        w_bc = sem("w_bc")
        w_col_ok = sem("w_col_ok")
        raw_in = [sem(f"raw_in{i}") for i in range(RING)]
        x_in = [sem(f"x_in{i}") for i in range(2)]
        w_hi_ok = sem("w_hi_ok")
        w_lo_ok = sem("w_lo_ok")
        x_hi_ok = sem("x_hi_ok")
        x_lo_ok = sem("x_lo_ok")
        gu_ok = sem("gu_ok")
        gelu_ok = sem("gelu_ok")
        hid_ok = sem("hid_ok")
        h_hi_ok = sem("h_hi_ok")
        h_lo_ok = sem("h_lo_ok")
        down_ok = sem("down_ok")
        c_ok = sem("c_ok")
        c_out = sem("c_out")
        zeroed = sem("zeroed")
        x_out = sem("x_out")

        ident1 = sb("ident1", [1, P])
        ZN = 9
        zeros = sb("zeros", [P, SLOTS // P // ZN * D])

        block = ctx.enter_context(nc.Block())

        @block.sync
        def _(sp):
            sp.dma_start(cond[:, :], k.cond_8).then_inc(cond_in, 16)
            sp.dma_start(ident1[:, :], k.consts[0:1, C_ONE:C_ONE + P]).then_inc(ones_in, 16)
            for m in range(COND_PAIRS):
                if m == 1:
                    for b in range(2):
                        sp.dma_start(x_raw[b][:, :, :], k.xT[:, :, b * S:(b + 1) * S]).then_inc(x_in[b], 16)
                sp.dma_start(w_raw[m][:, :], k.cond_w[COND_E, m]).then_inc(raw_in[m], 16)
            sp.wait_ge(rows_in, 32)

            def batch(it, half):
                for n in range(XP):
                    e = expert[n // COND_PAIRS]
                    at = half * XP + n
                    sp.wait_ge(w_lo_ok, it * (6 * XP) + 3 * (at + 1))
                    sp.dma_start(w_raw[n % RING][:, :], k.cond_w[ds(e, 1), n % COND_PAIRS].rearrange("e p n -> (e p) n")
                                 ).then_inc(raw_in[n % RING], 16)

            def next_x(b, half):
                sp.wait_ge(x_lo_ok, b - 1)
                sp.dma_start(x_raw[half][:, :, :], k.xT[:, :, ds(b * S, S)]).then_inc(x_in[half], 16)

            with sp.Fori(0, STEPS - 1) as it:
                for half in range(2):
                    expert = [sp.value_load(i_row[0:1, ds(it * 4 + half * 2 + j, 1)], min_val=0, max_val=COND_E - 1)
                              for j in range(COND_K)]
                    batch(it, half)
                    next_x(it * 2 + half + 2, half)
            for half in range(2):
                b = 2 * (STEPS - 1) + half
                expert = [sp.value_load(i_row[0:1, 2 * b + j:2 * b + j + 1], min_val=0, max_val=COND_E - 1)
                          for j in range(COND_K)]
                batch(STEPS - 1, half)

        @block.gpsimd
        def _(pool):
            pool.wait_ge(route, 12)
            pool.dma_start(w_row[0:1, :].rearrange("o (b m) -> o b m", b=B), wk3[:, :]).then_inc(rows_in, 16)
            pool.dma_start(i_row[0:1, :].rearrange("o (b m) -> o b m", b=B), top_i[:, 0:COND_K]).then_inc(rows_in, 16)
            pool.memset(zeros[:, :], 0.0).then_inc(zeroed, 1)
            pool.wait_ge(zeroed, 1)
            x_v = k.x_slots.rearrange("(p a n) d -> p a (n d)", p=P, a=ZN)
            for i in range(ZN):
                pool.dma_start(x_v[:, i, :], zeros[:, :]).then_inc(x_out, 16)
            with pool.Fori(0, B) as b:
                pool.wait_ge(c_ok, b + 3)
                pool.dma_start(k.c_T[:, :, ds(b * S, S)],
                               c_sb[:, ds(b, 1), :, :].rearrange("p o c s -> p (o c) s")).then_inc(c_out, 16)
            pool.wait_ge(c_out, 16 * B)
            pool.wait_ge(x_out, 16 * ZN)

        @block.scalar
        def _(act):
            act.wait_ge(route, 1)
            act.wait_ge(cond_in, 16)
            act.activation(ex[:, :], cond[:, :], ACT.Exp, bias=neg_top[:, 0:1], accum_out=ex_sum[:, 0:1]).then_inc(exped, 1)

            def weight_heads(slot, raw, landed):
                act.wait_ge(raw_in[raw], landed)
                for i in range(3):
                    act.activation(w_hi[:, slot, i * PIECE:(i + 1) * PIECE],
                                   w_raw[raw][:, i * PIECE:(i + 1) * PIECE], ACT.Copy).then_inc(w_hi_ok, 1)

            def x_heads(half, landed):
                act.wait_ge(x_in[half], landed)
                act.activation(x_hi[half][:, :, :], x_raw[half][:, :, :], ACT.Copy).then_inc(x_hi_ok, 1)

            weight_heads(RING, 0, 16)
            x_heads(0, 16)
            for m in range(1, COND_PAIRS):
                weight_heads(RING + m, m, 16)

            def step(it, last):
                for q in range(NQ):
                    half, ql = divmod(q, BQ)
                    act.wait_ge(gu_ok, it * NQ + q + 1)
                    act.activation(g_act[q % 2][:, :], ps_g[q % 2][:, :], ACT.Gelu_apprx_tanh).then_inc(gelu_ok, 1)
                    act.wait_ge(hid_ok, it * NQ + q + 3)
                    act.wait_ge(down_ok, it * NQ + q + 1)
                    act.activation(h_hi[q % 2][:, :], hid[q % 2][:, :], ACT.Copy).then_inc(h_hi_ok, 1)
                    n = ql - 1
                    if 0 <= n < XP:
                        if n >= RING:
                            act.wait_ge(down_ok, it * NQ + half * BQ + n + 3)
                        weight_heads(n % RING, n % RING, it * (2 * XP // RING * 16) + 16 * (half * XP // RING + n // RING + 2))
                    if ql == BQ - 2 and not (last and half == 1):
                        x_heads(1 - half, it * 16 + 16 * (1 + half))

            with act.Fori(0, STEPS - 1) as it:
                step(it, False)
            step(STEPS - 1, True)

        @block.vector
        def _(dve):
            done = [0]

            def then(ins):
                done[0] += 1
                ins.then_inc(route, 1)
                dve.wait_ge(route, done[0])

            dve.sem_inc(hid_ok, 2)
            dve.sem_inc(c_ok, 2)
            dve.wait_ge(cond_in, 16)
            then(dve.tensor_reduce(neg_top[:, :], cond[:, :], AX_X, ALU.max, negate=True))
            dve.wait_ge(exped, 1)
            then(dve.reciprocal(ex_rec[:, :], ex_sum[:, :]))
            then(dve.tensor_scalar(prob[:, :], ex[:, :], ex_rec[:, 0:1], None, ALU.mult))
            then(dve.max(top[:, :], prob[:, :]))
            then(dve.max_index(top_i[:, :], top[:, :], prob[:, :]))
            then(dve.tensor_tensor(pair_sum[:, :], top[:, 0:1], top[:, 1:2], ALU.add))
            then(dve.reciprocal(pair_rec[:, :], pair_sum[:, :]))
            then(dve.tensor_scalar(wk[:, :], top[:, 0:COND_K], pair_rec[:, 0:1], None, ALU.mult))
            then(dve.tensor_scalar(wk1[:, :], wk[:, :], 1.0 / 12, None, ALU.mult))
            then(dve.tensor_scalar(wk[:, :], wk[:, :], 1.0 - 1.0 / 12, None, ALU.mult))
            then(dve.memset(wk3[:, 0:1], 1.0))
            then(dve.tensor_tensor(wk3[:, 1:MLPS], wk1[:, :], wk[:, :], ALU.add))
            dve.wait_ge(w_bc, 1)
            dve.tensor_copy(w_col[:, :], ps_w[:, 0:B * MLPS]).then_inc(w_col_ok, 1)

            def weight_tails(slot, raw, heads):
                for i in range(3):
                    dve.wait_ge(w_hi_ok, heads + i + 1)
                    cols = slice(i * PIECE, (i + 1) * PIECE)
                    dve.tensor_tensor(w_lo[:, slot, cols], w_raw[raw][:, cols], w_hi[:, slot, cols].bitcast(F32),
                                      ALU.subtract).then_inc(w_lo_ok, 1)

            def x_tails(half, b):
                dve.wait_ge(x_hi_ok, b + 1)
                dve.tensor_tensor(x_lo[half][:, :, :], x_raw[half][:, :, :], x_hi[half][:, :, :].bitcast(F32),
                                  ALU.subtract).then_inc(x_lo_ok, 1)

            weight_tails(RING, 0, 0)
            x_tails(0, 0)
            for m in range(1, COND_PAIRS):
                weight_tails(RING + m, m, 3 * m)
            dve.wait_ge(w_col_ok, 1)

            def step(it, last):
                for q in range(NQ):
                    half, ql = divmod(q, BQ)
                    m = ql // COND_PAIRS
                    dve.wait_ge(gelu_ok, it * NQ + q + 1)
                    col = it * (2 * MLPS) + half * MLPS + m
                    w = w_col[:, col:col + 1] if last else w_col[:, ds(col, 1)]
                    dve.scalar_tensor_tensor(hid[q % 2][:, :], ps_u[q % 2][:, :], w, g_act[q % 2][:, :],
                                             ALU.mult, ALU.mult).then_inc(hid_ok, 1)
                    dve.wait_ge(h_hi_ok, it * NQ + q + 1)
                    dve.tensor_tensor(h_lo[q % 2][:, :], hid[q % 2][:, :], h_hi[q % 2][:, :].bitcast(F32),
                                      ALU.subtract).then_inc(h_lo_ok, 1)
                    n = ql - 1
                    if 0 <= n < XP:
                        weight_tails(n % RING, n % RING, it * (6 * XP) + 3 * (COND_PAIRS + half * XP + n))
                    if ql == BQ - 2 and not (last and half == 1):
                        x_tails(1 - half, it * 2 + half + 1)
                    if ql == BQ - 1:
                        b = it * 2 + half
                        dve.wait_ge(down_ok, it * NQ + q + 3)
                        out = c_sb[:, b, :, :] if last else c_sb[:, ds(b, 1), :, :].rearrange("p o c s -> p (o c) s")
                        dve.tensor_copy(out, ps_d[half][:, :, :]).then_inc(c_ok, 1)

            with dve.Fori(0, STEPS - 1) as it:
                step(it, False)
            step(STEPS - 1, True)

        @block.tensor
        def _(pe):
            pe.sem_inc(down_ok, 2)
            pe.wait_ge(ones_in, 16)
            pe.wait_ge(rows_in, 32)
            pe.matmul(ps_w[:, 0:B * MLPS], ident1[0:1, :], w_row[0:1, :], start=True, stop=True).then_inc(w_bc, 1)

            def gate_up(it, q):
                half, ql = divmod(q % NQ, BQ)
                if ql == 0:
                    pe.wait_ge(x_lo_ok, it * 2 + q // BQ + 1)
                if ql >= COND_PAIRS:
                    n = ql - COND_PAIRS
                    slot = n % RING
                    pe.wait_ge(w_lo_ok, it * (6 * XP) + 3 * (COND_PAIRS + half * XP + n + 1))
                else:
                    slot = RING + ql
                    if isinstance(it, int) and it == -1:
                        pe.wait_ge(w_lo_ok, 3)
                pe.wait_ge(hid_ok, it * NQ + q + 1)
                for dst, off in ((ps_g[q % 2], 0), (ps_u[q % 2], PIECE)):
                    for i in range(2):
                        for c in range(C):
                            cols = slice(off + c * PAIR + i * P, off + c * PAIR + (i + 1) * P)
                            wh, wl = w_hi[:, slot, cols], w_lo[:, slot, cols]
                            o = dst[:, i * S:(i + 1) * S]
                            pe.matmul(o, wh, x_hi[half][:, c, :], start=(c == 0), stop=False)
                            pe.matmul(o, wh, x_lo[half][:, c, :], start=False, stop=False)
                            mm = pe.matmul(o, wl, x_hi[half][:, c, :], start=False, stop=(c == C - 1))
                mm.then_inc(gu_ok, 1)

            def down(it, q):
                half, ql = divmod(q, BQ)
                slot = (ql - COND_PAIRS) % RING if ql >= COND_PAIRS else RING + ql
                if ql == 0:
                    pe.wait_ge(c_ok, it * 2 + half + 1)
                pe.wait_ge(h_lo_ok, it * NQ + q + 1)
                for d in range(C):
                    for i in range(2):
                        cols = slice(2 * PIECE + i * D + d * P, 2 * PIECE + i * D + (d + 1) * P)
                        wh, wl = w_hi[:, slot, cols], w_lo[:, slot, cols]
                        hh, hl = h_hi[q % 2][:, i * S:(i + 1) * S], h_lo[q % 2][:, i * S:(i + 1) * S]
                        o = ps_d[half][:, d, :]
                        pe.matmul(o, wh, hh, start=(ql == 0 and d == 0 and i == 0), stop=False, skip_group_check=True)
                        pe.matmul(o, wh, hl, start=False, stop=False, skip_group_check=True)
                        mm = pe.matmul(o, wl, hh, start=False, stop=(ql == BQ - 1 and i == 1), skip_group_check=True)
                mm.then_inc(down_ok, 1)

            pe.wait_ge(w_lo_ok, 3 * COND_PAIRS)
            gate_up(0, 0)

            def step(it, last):
                for q in range(NQ):
                    if not (last and q == NQ - 1):
                        gate_up(it, q + 1)
                    down(it, q)

            with pe.Fori(0, STEPS - 1) as it:
                step(it, False)
            step(STEPS - 1, True)


def stage_attention(nc, k):
    with ExitStack() as ctx:
        def sb(name, shape, dt=F32):
            return ctx.enter_context(nc.sbuf_tensor("b_" + name, shape, dt))

        def ps(name, shape, dt=F32):
            return ctx.enter_context(nc.psum_tensor("b_" + name, shape, dt))

        def sem(name):
            return ctx.enter_context(nc.semaphore("b_" + name))

        ROWS = 32
        NJ = P // ROWS
        NS = NG * NJ
        WN = W_B
        w_raw = sb("w_raw", [P, WN])
        w_hi = sb("w_hi", [P, WN], F32R)
        w_lo = sb("w_lo", [P, WN], F32R)
        vec = sb("vec", [P, V_W])
        rows = sb("rows", [P, R_W])
        cst = sb("cst", [P, C_W])
        q_bias = sb("q_bias", [P, 2, C])
        c_raw = sb("c_raw", [P, C, B, SGP])
        c_hi = sb("c_hi", [P, C, SGT], F32R)
        c_lo = sb("c_lo", [P, C, SGT], F32R)
        x_raw = sb("x_raw", [P, C, B, SGP])
        qeo = sb("qeo", [P, C, 2, SGT])
        kk = sb("kk", [P, C, SGT])
        v_aug = sb("v_aug", [P, NG, H, HD + 1])
        sm = [sb(f"sm{i}", [P, 4, P]) for i in range(2)]
        den = sb("den", [P, H])
        rec = sb("rec", [P, H])
        an = [sb(f"an{i}", [P, H, HD]) for i in range(2)]
        at_hi = sb("at_hi", [P, C, SGT], F32R)
        at_lo = sb("at_lo", [P, C, SGT], F32R)
        o_tmp = [sb(f"o_tmp{i}", [P, SGT]) for i in range(C)]
        x2 = sb("x2", [P, SG, C, B, SGP])

        ps_a = [ps(f"ps_a{i}", [P, SGT]) for i in range(2)]
        ps_s = [ps(f"ps_s{i}", [P, 4 * P]) for i in range(2)]
        ps_o = [ps(f"ps_o{i}", [P, H, HD + 1]) for i in range(2)]
        ps_t = ps("ps_t", [P, C, P])

        par_in = sem("par_in")
        w_in = sem("w_in")
        c_in = sem("c_in")
        x_in = sem("x_in")
        w_hi_ok = sem("w_hi_ok")
        w_lo_ok = sem("w_lo_ok")
        qb_ok = sem("qb_ok")
        c_hi_ok = sem("c_hi_ok")
        c_lo_ok = sem("c_lo_ok")
        pj_ok = sem("pj_ok")
        qk_ok = sem("qk_ok")
        v_ok = sem("v_ok")
        s_ok = sem("s_ok")
        m_ok = sem("m_ok")
        pv_ok = sem("pv_ok")
        den_ok = sem("den_ok")
        n_ok = sem("n_ok")
        t_ok = sem("t_ok")
        ahi_ok = sem("ahi_ok")
        alo_ok = sem("alo_ok")
        op_ok = sem("op_ok")
        o_ok = sem("o_ok")
        x2_ok = sem("x2_ok")
        x2_out = sem("x2_out")

        block = ctx.enter_context(nc.Block())

        @block.sync
        def _(sp):
            sp.dma_start(w_raw[:, :], k.attn_w[:, 0:WN]).then_inc(w_in, 16)
            sp.dma_start(vec[:, :], k.vec).then_inc(par_in, 16)
            sp.dma_start(rows[:, :], k.rows).then_inc(par_in, 16)
            sp.dma_start(cst[:, :], k.consts).then_inc(par_in, 16)
            c_v = k.c_T.rearrange("p c (b s) -> p c b s", b=B)
            x_v = k.xT.rearrange("p c (b s) -> p c b s", b=B)
            with sp.Fori(0, SG) as it:
                sp.wait_ge(c_lo_ok, it * 2 + 2)
                for c in range(C):
                    sp.dma_start(c_raw[:, c, :, :], c_v[:, c, :, ds(it * SGP, SGP)]).then_inc(c_in, 16)
                sp.wait_ge(x2_ok, it * 2 + 2)
                for c in range(C):
                    sp.dma_start(x_raw[:, c, :, :], x_v[:, c, :, ds(it * SGP, SGP)]).then_inc(x_in, 16)

        @block.gpsimd
        def _(pool):
            x2_v = k.x2_T.rearrange("p c (b s) -> p c b s", b=B)
            with pool.Fori(0, SG) as it:
                pool.wait_ge(x2_ok, it * 2 + 4)
                for c in range(C):
                    pool.dma_start(x2_v[:, c, :, ds(it * SGP, SGP)],
                                   x2[:, ds(it, 1), c, :, :].rearrange("p o b s -> p (o b) s")).then_inc(x2_out, 16)
            pool.wait_ge(x2_out, 16 * C * SG)

        def grouped(ap, c):
            return ap[:, c, :, :].rearrange("p b (g s) -> p g b s", g=NG)

        def by_group(ap):
            return ap.rearrange("p (g b s) -> p g b s", g=NG, b=B)

        @block.scalar
        def _(act):
            act.wait_ge(w_in, 16)
            for i in range(WN // 512):
                cols = slice(i * 512, (i + 1) * 512)
                act.activation(w_hi[:, cols], w_raw[:, cols], ACT.Copy).then_inc(w_hi_ok, 1)
            act.wait_ge(par_in, 48)
            act.wait_ge(qb_ok, 2)
            with act.Fori(0, SG) as it:
                act.wait_ge(c_in, it * 32 + 32)
                for c in range(C):
                    act.activation(by_group(c_hi[:, c, :]), grouped(c_raw, c), ACT.Copy).then_inc(c_hi_ok, 1)
                for e in range(C):
                    act.wait_ge(pj_ok, it * 8 + e + 1)
                    act.wait_ge(s_ok, it * NS + 1)
                    for o in range(2):
                        ins = act.activation(qeo[:, e, o, :], ps_a[e][:, :], ACT.Relu, bias=q_bias[:, o, e:e + 1],
                                             scale=cst[:, C_EVEN + o:C_EVEN + o + 1])
                    ins.then_inc(qk_ok, 1)
                for e in range(C):
                    act.wait_ge(pj_ok, it * 8 + e + 3)
                    act.activation(kk[:, e, :], ps_a[e][:, :], ACT.Relu, bias=vec[:, V_BK + e:V_BK + e + 1]
                                   ).then_inc(qk_ok, 1)
                for g in range(NG):
                    act.wait_ge(t_ok, it * NG + g + 1)
                    act.activation(at_hi[:, :, g * P:(g + 1) * P], ps_t[:, :, :], ACT.Copy).then_inc(ahi_ok, 1)
                for e in range(C):
                    act.wait_ge(op_ok, it * 2 + e + 1)
                    act.activation(o_tmp[e][:, :], ps_a[e][:, :], ACT.Identity, bias=vec[:, V_OB + e:V_OB + e + 1]
                                   ).then_inc(o_ok, 1)

        @block.vector
        def _(dve):
            dve.sem_inc(c_lo_ok, 2)
            dve.sem_inc(m_ok, 2)
            dve.sem_inc(n_ok, 2)
            dve.sem_inc(alo_ok, 1)
            dve.sem_inc(x2_ok, 2)
            dve.memset(v_aug[:, :, :, HD:HD + 1], 1.0)
            dve.wait_ge(par_in, 48)
            for o in range(2):
                dve.tensor_scalar(q_bias[:, o, :], vec[:, V_BQ:V_BQ + C], cst[:, C_EVEN + o:C_EVEN + o + 1], None,
                                  ALU.mult).then_inc(qb_ok, 1)
            for i in range(WN // 512):
                cols = slice(i * 512, (i + 1) * 512)
                dve.wait_ge(w_hi_ok, i + 1)
                dve.tensor_tensor(w_lo[:, cols], w_raw[:, cols], w_hi[:, cols].bitcast(F32), ALU.subtract
                                  ).then_inc(w_lo_ok, 1)
            mask = cst[:, C_MASK:C_MASK + P].unsqueeze(1).broadcast_to([P, 4, P])

            def norm(it, g):
                dve.wait_ge(pv_ok, it * NG + g + 1)
                o = ps_o[g % 2]
                dve.tensor_scalar(den[:, :], o[:, :, HD], EPS, None, ALU.max).then_inc(den_ok, 1)
                dve.wait_ge(den_ok, it * (2 * NG) + 2 * g + 1)
                dve.reciprocal(rec[:, :], den[:, :]).then_inc(den_ok, 1)
                dve.wait_ge(den_ok, it * (2 * NG) + 2 * g + 2)
                dve.tensor_tensor(an[g % 2][:, :, :], o[:, :, 0:HD],
                                  rec[:, :].unsqueeze(2).broadcast_to([P, H, HD]), ALU.mult).then_inc(n_ok, 1)

            def tails(it, g):
                dve.wait_ge(ahi_ok, it * NG + g + 1)
                cols = slice(g * P, (g + 1) * P)
                dve.tensor_tensor(at_lo[:, :, cols], ps_t[:, :, :], at_hi[:, :, cols].bitcast(F32), ALU.subtract
                                  ).then_inc(alo_ok, 1)

            with dve.Fori(0, SG) as it:
                for c in range(C):
                    dve.wait_ge(c_hi_ok, it * 2 + c + 1)
                    dve.tensor_tensor(by_group(c_lo[:, c, :]), grouped(c_raw, c),
                                      by_group(c_hi[:, c, :]).bitcast(F32), ALU.subtract).then_inc(c_lo_ok, 1)
                for g in range(NG):
                    dve.wait_ge(pj_ok, it * 8 + g + 5)
                    dve.tensor_tensor(v_aug[:, g, :, 0:HD], ps_a[g % 2][:, 0:D].rearrange("p (h d) -> p h d", h=H),
                                      rows[:, R_BV:R_BV + D].rearrange("p (h d) -> p h d", h=H), ALU.add
                                      ).then_inc(v_ok, 1)
                for n in range(NS):
                    dve.wait_ge(s_ok, it * NS + n + 2)
                    dve.tensor_tensor(sm[n % 2][:, :, :], ps_s[n % 2][:, :].rearrange("p (h t) -> p h t", h=4), mask,
                                      ALU.mult).then_inc(m_ok, 1)
                    if n >= NJ and n % NJ == 0:
                        norm(it, n // NJ - 1)
                    if n >= NJ and n % NJ == 3:
                        tails(it, n // NJ - 1)
                norm(it, NG - 1)
                tails(it, NG - 1)
                dve.wait_ge(x_in, it * 32 + 32)
                for e in range(C):
                    dve.wait_ge(o_ok, it * 2 + e + 3)
                    dve.tensor_tensor(x2[:, ds(it, 1), e, :, :].rearrange("p o b (g s) -> p g (o b) s", g=NG),
                                      by_group(o_tmp[e][:, :]), grouped(x_raw, e), ALU.add).then_inc(x2_ok, 1)

        @block.tensor
        def _(pe):
            pe.sem_inc(s_ok, 1)
            pe.sem_inc(o_ok, 2)
            pe.wait_ge(w_lo_ok, WN // 512)
            ident = cst[:, C_ID:C_ID + P]

            def three(o, sh, sl, mh, ml, first, last):
                pe.matmul(o, sh, mh, start=first, stop=False)
                pe.matmul(o, sh, ml, start=False, stop=False)
                return pe.matmul(o, sl, mh, start=False, stop=last)

            def pv(it, n):
                g, j = divmod(n, NJ)
                if j == 0:
                    pe.wait_ge(n_ok, it * NG + g + 1)
                if n == 0:
                    pe.wait_ge(v_ok, it * NG + NG)
                pe.wait_ge(m_ok, it * NS + n + 3)
                for e in range(C):
                    for o in range(2):
                        head = e * (H // 2) + 2 * j + o
                        mm = pe.matmul(ps_o[g % 2][:, head, :], sm[n % 2][:, 2 * e + o, :], v_aug[:, g, head, :],
                                       start=True, stop=True)
                if j == NJ - 1:
                    mm.then_inc(pv_ok, 1)

            def turn(it, g):
                pe.wait_ge(n_ok, it * NG + g + 3)
                pe.wait_ge(alo_ok, it * NG + g + 1)
                for c in range(C):
                    mm = pe.transpose(ps_t[:, c, :], an[g % 2][:, c * (H // 2):(c + 1) * (H // 2), :].rearrange("p h d -> p (h d)"), ident)
                mm.then_inc(t_ok, 1)

            with pe.Fori(0, SG) as it:
                pe.wait_ge(c_lo_ok, it * 2 + 4)
                for n in range(4):
                    e, base = n % 2, (n // 2) * D
                    if n < 2:
                        pe.wait_ge(o_ok, it * 2 + n + 1)
                    else:
                        pe.wait_ge(qk_ok, it * 4 + n - 1)
                    for c in range(C):
                        cols = slice(c * 3 * D + base + e * P, c * 3 * D + base + (e + 1) * P)
                        mm = three(ps_a[n % 2][:, :], w_hi[:, cols], w_lo[:, cols], c_hi[:, c, :], c_lo[:, c, :],
                                   c == 0, c == C - 1)
                    mm.then_inc(pj_ok, 1)
                for g in range(NG):
                    if g < 2:
                        pe.wait_ge(qk_ok, it * 4 + g + 3)
                    else:
                        pe.wait_ge(v_ok, it * NG + g - 1)
                    tok = slice(g * P, (g + 1) * P)
                    for c in range(C):
                        cols = slice(c * 3 * D + 2 * D, (c + 1) * 3 * D)
                        mm = three(ps_a[g % 2][:, 0:D], c_hi[:, c, tok], c_lo[:, c, tok], w_hi[:, cols], w_lo[:, cols],
                                   c == 0, c == C - 1)
                    mm.then_inc(pj_ok, 1)
                for n in range(NS):
                    g, j = divmod(n, NJ)
                    r, tok = slice(j * ROWS, (j + 1) * ROWS), slice(g * P, (g + 1) * P)
                    pe.wait_ge(m_ok, it * NS + n + 1)
                    for e in range(C):
                        mm = pe.matmul(ps_s[n % 2][:, e * 2 * P:(e + 1) * 2 * P], kk[r, e, tok], qeo[r, e, :, tok],
                                       start=True, stop=True)
                    mm.then_inc(s_ok, 1)
                    if n > 0:
                        pv(it, n - 1)
                    if n >= NJ and n % NJ == 2:
                        turn(it, n // NJ - 1)
                pv(it, NS - 1)
                turn(it, NG - 1)
                pe.wait_ge(alo_ok, it * NG + NG + 1)
                pe.wait_ge(v_ok, it * NG + NG)
                for e in range(C):
                    for c in range(C):
                        cols = slice(W_O + c * D + e * P, W_O + c * D + (e + 1) * P)
                        mm = three(ps_a[e][:, :], w_hi[:, cols], w_lo[:, cols], at_hi[:, c, :], at_lo[:, c, :],
                                   c == 0, c == C - 1)
                    mm.then_inc(op_ok, 1)


def stage_lora(nc, k):
    with ExitStack() as ctx:
        def sb(name, shape, dt=F32):
            return ctx.enter_context(nc.sbuf_tensor("c_" + name, shape, dt))

        def ps(name, shape, dt=F32):
            return ctx.enter_context(nc.psum_tensor("c_" + name, shape, dt))

        def sem(name):
            return ctx.enter_context(nc.semaphore("c_" + name))

        WN = W_W - W_B
        A0, L0 = W_A - W_B, W_L - W_B
        U = BLK // P
        w_raw = sb("w_raw", [P, WN])
        w_hi = sb("w_hi", [P, WN], F32R)
        w_lo = sb("w_lo", [P, WN], F32R)
        vec = sb("vec", [P, V_W])
        rows = sb("rows", [P, R_W])
        ident = sb("ident", [P, P])
        router = sb("router", [P, C, E])
        lora_raw = sb("lora_raw", [P, B])
        lora_w = sb("lora_w", [P, B])
        x_raw = sb("x_raw", [P, C, BLK])
        x_hi = sb("x_hi", [P, C, BLK], F32R)
        x_lo = sb("x_lo", [P, C, BLK], F32R)
        ha = sb("ha", [P, BLK])
        ha_hi = sb("ha_hi", [P, BLK], F32R)
        ha_lo = sb("ha_lo", [P, BLK], F32R)
        y = sb("y", [P, C, BLK])
        ps_h = ps("ps_h", [P, BLK])
        ps_y = [ps(f"ps_y{i}", [P, BLK]) for i in range(C)]
        ps_l = ps("ps_l", [P, U, E])
        ps_t = [ps(f"ps_t{i}", [P, 2, D]) for i in range(2)]

        par_in = sem("par_in")
        w_in = sem("w_in")
        x_in = sem("x_in")
        w_hi_ok = sem("w_hi_ok")
        w_lo_ok = sem("w_lo_ok")
        lw_ok = sem("lw_ok")
        x_hi_ok = sem("x_hi_ok")
        x_lo_ok = sem("x_lo_ok")
        h_ok = sem("h_ok")
        ha_ok = sem("ha_ok")
        ha_hi_ok = sem("ha_hi_ok")
        ha_lo_ok = sem("ha_lo_ok")
        ym_ok = sem("ym_ok")
        y_ok = sem("y_ok")
        y_free = sem("y_free")
        lm_ok = sem("lm_ok")
        lg_ok = sem("lg_ok")
        t_ok = sem("t_ok")
        yn_ok = sem("yn_ok")
        y_out = sem("y_out")
        block = ctx.enter_context(nc.Block())

        @block.sync
        def _(sp):
            sp.dma_start(w_raw[:, :], k.attn_w[:, W_B:W_W]).then_inc(w_in, 16)
            sp.dma_start(vec[:, :], k.vec).then_inc(par_in, 16)
            sp.dma_start(rows[:, :], k.rows).then_inc(par_in, 16)
            sp.dma_start(ident[:, :], k.consts[:, C_ID:C_ID + P]).then_inc(par_in, 16)
            sp.dma_start(router[:, :, :], k.router).then_inc(par_in, 16)
            sp.dma_start(lora_raw[:, :], k.lora_w).then_inc(par_in, 16)
            with sp.Fori(0, NB) as it:
                sp.wait_ge(x_lo_ok, it + 1)
                sp.dma_start(x_raw[:, :, :], k.x2_T[:, :, ds(it * BLK, BLK)]).then_inc(x_in, 16)

        @block.gpsimd
        def _(pool):
            pool.sem_inc(y_free, 1)
            with pool.Fori(0, NB) as it:
                pool.wait_ge(y_ok, it * 2 + 4)
                pool.dma_start(k.y_T[:, :, ds(it * BLK, BLK)], y[:, :, :]).then_inc(y_out, 16)
                pool.wait_ge(y_out, it * 16 + 16)
                pool.wait_ge(t_ok, it * 2 + 2)
                pool.sem_inc(y_free, 1)

        @block.scalar
        def _(act):
            act.wait_ge(w_in, 16)
            for i in range(WN // 512):
                cols = slice(i * 512, (i + 1) * 512)
                act.activation(w_hi[:, cols], w_raw[:, cols], ACT.Copy).then_inc(w_hi_ok, 1)
            act.wait_ge(par_in, 80)
            with act.Fori(0, NB) as it:
                act.wait_ge(x_in, it * 16 + 16)
                act.activation(x_hi[:, :, :], x_raw[:, :, :], ACT.Copy).then_inc(x_hi_ok, 1)
                act.wait_ge(ha_ok, it * 2 + 4)
                act.activation(ha_hi[:, :], ha[:, :], ACT.Copy).then_inc(ha_hi_ok, 1)
                act.wait_ge(y_free, it + 1)
                for o in range(C):
                    act.wait_ge(ym_ok, it * 2 + o + 1)
                    act.activation(y[:, o, :], ps_y[o][:, :], ACT.Identity, bias=vec[:, V_BB + o:V_BB + o + 1]
                                   ).then_inc(y_ok, 1)

        @block.vector
        def _(dve):
            dve.sem_inc(x_lo_ok, 1)
            dve.sem_inc(ha_ok, 2)
            dve.sem_inc(lg_ok, 1)
            dve.sem_inc(yn_ok, 2)
            dve.wait_ge(par_in, 80)
            dve.tensor_scalar(lora_w[:, :], lora_raw[:, :], LORA_SCALE, None, ALU.mult).then_inc(lw_ok, 1)
            for i in range(WN // 512):
                cols = slice(i * 512, (i + 1) * 512)
                dve.wait_ge(w_hi_ok, i + 1)
                dve.tensor_tensor(w_lo[:, cols], w_raw[:, cols], w_hi[:, cols].bitcast(F32), ALU.subtract
                                  ).then_inc(w_lo_ok, 1)
            dve.wait_ge(lw_ok, 1)
            with dve.Fori(0, NB) as it:
                dve.wait_ge(x_hi_ok, it + 1)
                dve.tensor_tensor(x_lo[:, :, :], x_raw[:, :, :], x_hi[:, :, :].bitcast(F32), ALU.subtract
                                  ).then_inc(x_lo_ok, 1)
                dve.wait_ge(h_ok, it + 1)
                for b in range(2):
                    cols = slice(b * S, (b + 1) * S)
                    dve.tensor_scalar(ha[:, cols], ps_h[:, cols], lora_w[:, ds(it * 2 + b, 1)], None, ALU.mult
                                      ).then_inc(ha_ok, 1)
                dve.wait_ge(ha_hi_ok, it + 1)
                dve.tensor_tensor(ha_lo[:, :], ha[:, :], ha_hi[:, :].bitcast(F32), ALU.subtract).then_inc(ha_lo_ok, 1)
                dve.wait_ge(lm_ok, it + 1)
                dve.tensor_tensor(k.logit[:, ds(it * U, U), :], ps_l[:, :, :],
                                  rows[:, R_BR:R_BR + E].unsqueeze(1).broadcast_to([P, U, E]), ALU.add
                                  ).then_inc(lg_ok, 1)
                for i in range(2):
                    dve.wait_ge(t_ok, it * 2 + i + 1)
                    dve.tensor_copy(k.y_nat[:, ds(it * U + 2 * i, 2), :], ps_t[i][:, :, :]).then_inc(yn_ok, 1)

        @block.tensor
        def _(pe):
            pe.sem_inc(y_ok, 2)

            def three(o, sh, sl, mh, ml, first, last):
                pe.matmul(o, sh, mh, start=first, stop=False)
                pe.matmul(o, sh, ml, start=False, stop=False)
                return pe.matmul(o, sl, mh, start=False, stop=last)

            pe.wait_ge(w_lo_ok, WN // 512)
            pe.wait_ge(par_in, 80)
            with pe.Fori(0, NB) as it:
                pe.wait_ge(x_lo_ok, it + 2)
                pe.wait_ge(ha_ok, it * 2 + 2)
                for c in range(C):
                    cols = slice(A0 + c * P, A0 + (c + 1) * P)
                    mm = three(ps_h[:, :], w_hi[:, cols], w_lo[:, cols], x_hi[:, c, :], x_lo[:, c, :], c == 0, c == C - 1)
                mm.then_inc(h_ok, 1)
                for o in range(C):
                    pe.wait_ge(y_ok, it * 2 + o + 1)
                    for c in range(C):
                        cols = slice(c * D + o * P, c * D + (o + 1) * P)
                        three(ps_y[o][:, :], w_hi[:, cols], w_lo[:, cols], x_hi[:, c, :], x_lo[:, c, :], c == 0, False)
                pe.wait_ge(ha_lo_ok, it + 1)
                for o in range(C):
                    cols = slice(L0 + o * P, L0 + (o + 1) * P)
                    three(ps_y[o][:, :], w_hi[:, cols], w_lo[:, cols], ha_hi[:, :], ha_lo[:, :], False, True
                          ).then_inc(ym_ok, 1)
                pe.wait_ge(y_ok, it * 2 + 4)
                pe.wait_ge(lg_ok, it + 1)
                for u in range(U):
                    for c in range(C):
                        mm = pe.matmul(ps_l[:, u, :], y[:, c, u * P:(u + 1) * P], router[:, c, :],
                                       start=(c == 0), stop=(c == C - 1))
                mm.then_inc(lm_ok, 1)
                for i in range(2):
                    pe.wait_ge(yn_ok, it * 2 + i + 1)
                    for u in range(2):
                        for c in range(C):
                            mm = pe.transpose(ps_t[i][:, u, c * P:(c + 1) * P],
                                              y[:, c, (2 * i + u) * P:(2 * i + u + 1) * P], ident[:, :])
                    mm.then_inc(t_ok, 1)


def stage_route(nc, k):
    with ExitStack() as ctx:
        def sb(name, shape, dt=F32):
            return ctx.enter_context(nc.sbuf_tensor("d_" + name, shape, dt))

        def ps(name, shape, dt=F32):
            return ctx.enter_context(nc.psum_tensor("d_" + name, shape, dt))

        def sem(name):
            return ctx.enter_context(nc.semaphore("d_" + name))

        NI = HS // P
        U = BLK // P
        ITP = 2
        cst = sb("cst", [P, C_W])
        vec = sb("vec", [P, V_W])
        rows = sb("rows", [P, R_W])
        lt = sb("lt", [P, TT, E])
        top = sb("top", [P, TT, 8])
        top_i = sb("top_i", [P, TT, 8], U32)
        idx = sb("idx", [P, TT, 2])
        dif = sb("dif", [P, TT])
        ex = sb("ex", [P, TT])
        ex1 = sb("ex1", [P, TT])
        one_hot = [sb(f"one_hot{i}", [P, TT, E]) for i in range(2)]
        both = sb("both", [P, TT, E])
        tot = sb("tot", [P, E, TT])
        inc = sb("inc", [P, E, TT])
        exc = sb("exc", [P, E, TT])
        more = sb("more", [P, E, 8])
        tiles = sb("tiles", [P, E])
        tend = sb("tend", [P, E])
        tbeg = sb("tbeg", [P, E])
        sbase = sb("sbase", [P, E])
        slot = sb("slot", [P, TT, E])
        slot2 = sb("slot2", [P, TT, E])
        mine = [sb(f"mine{i}", [P, TT, E]) for i in range(2)]
        posf = [sb(f"posf{i}", [P, TT]) for i in range(2)]
        past = sb("past", [P, NT, E])
        npast = sb("npast", [P, NT])
        w_raw = sb("w_raw", [P, 2, CHUNK])
        w_hi = sb("w_hi", [P, 2, CHUNK], F32R)
        w_lo = sb("w_lo", [P, 2, CHUNK], F32R)
        y_raw = sb("y_raw", [P, C, BLK])
        x_raw = sb("x_raw", [P, C, BLK])
        y_hi = sb("y_hi", [P, C, BLK], F32R)
        y_lo = sb("y_lo", [P, C, BLK], F32R)
        g_act = [sb(f"g_act{i}", [P, BLK]) for i in range(2)]
        hid = [sb(f"hid{i}", [P, BLK]) for i in range(2)]
        h_hi = [sb(f"h_hi{i}", [P, BLK], F32R) for i in range(2)]
        h_lo = [sb(f"h_lo{i}", [P, BLK], F32R) for i in range(2)]
        ps_a = [ps(f"ps_a{i}", [P, BLK]) for i in range(2)]
        ps_g = [ps(f"ps_g{i}", [P, BLK]) for i in range(2)]
        ps_o = [ps(f"ps_o{i}", [P, 2, D]) for i in range(2)]
        ps_r = [ps(f"ps_r{i}", [P, TT, E]) for i in range(2)]

        cst_in = sem("cst_in")
        par_in = sem("par_in")
        w_in = sem("w_in")
        y_in = sem("y_in")
        x_in = sem("x_in")
        route = sem("route")
        exped = sem("exped")
        ranks = sem("ranks")
        both_ok = sem("both_ok")
        pos_ok = sem("pos_ok")
        moved = sem("moved")
        w_hi_ok = sem("w_hi_ok")
        w_lo_ok = sem("w_lo_ok")
        y_hi_ok = sem("y_hi_ok")
        y_lo_ok = sem("y_lo_ok")
        ag_ok = sem("ag_ok")
        gelu_ok = sem("gelu_ok")
        hid_ok = sem("hid_ok")
        h_hi_ok = sem("h_hi_ok")
        h_lo_ok = sem("h_lo_ok")
        down_ok = sem("down_ok")
        res_ok = sem("res_ok")
        base_ok = sem("base_ok")
        block = ctx.enter_context(nc.Block())

        @block.sync
        def _(sp):
            sp.dma_start(cst[:, :], k.consts).then_inc(cst_in, 16)
            sp.dma_start(w_raw[:, :, :], k.shared_w.rearrange("j p n -> p j n")).then_inc(w_in, 16)
            sp.dma_start(vec[:, :], k.vec).then_inc(par_in, 16)
            sp.dma_start(rows[:, :], k.rows).then_inc(par_in, 16)
            with sp.Fori(0, NB) as it:
                sp.wait_ge(y_lo_ok, it + 1)
                sp.dma_start(y_raw[:, :, :], k.y_T[:, :, ds(it * BLK, BLK)]).then_inc(y_in, 16)
                sp.wait_ge(res_ok, it + 1)
                sp.dma_start(x_raw[:, :, :], k.x2_T[:, :, ds(it * BLK, BLK)]).then_inc(x_in, 16)

        @block.gpsimd
        def _(pool):
            pool.wait_ge(pos_ok, 2)
            for n in range(TT):
                for j in range(2):
                    pool.indirect_dma_start(out=k.x_slots, out_offset=bass.IndirectOffsetOnAxis(ap=k.pos[j][:, n:n + 1], axis=0),
                                            in_=k.y_nat[:, n, :], in_offset=None).then_inc(moved, 16)
            pool.wait_ge(moved, 16 * 2 * TT)

        @block.scalar
        def _(act):
            act.wait_ge(w_in, 16)
            for j in range(2):
                for i in range(3):
                    cols = slice(i * PIECE, (i + 1) * PIECE)
                    act.activation(w_hi[:, j, cols], w_raw[:, j, cols], ACT.Copy).then_inc(w_hi_ok, 1)
            act.wait_ge(exped, 1)
            act.activation(ex[:, :], dif[:, :], ACT.Exp).then_inc(exped, 1)
            act.wait_ge(par_in, 32)
            with act.Fori(0, NB) as it:
                act.wait_ge(y_in, it * 16 + 16)
                act.activation(y_hi[:, :, :], y_raw[:, :, :], ACT.Copy).then_inc(y_hi_ok, 1)
                for i in range(NI):
                    act.wait_ge(ag_ok, it * NI + i + 1)
                    act.activation(g_act[i % 2][:, :], ps_g[i % 2][:, :], ACT.Gelu, bias=vec[:, V_BG + i:V_BG + i + 1]
                                   ).then_inc(gelu_ok, 1)
                    act.wait_ge(hid_ok, it * NI + i + 3)
                    act.wait_ge(down_ok, it * NI + i + 1)
                    act.activation(h_hi[i % 2][:, :], hid[i % 2][:, :], ACT.Copy).then_inc(h_hi_ok, 1)

        @block.vector
        def _(dve):
            done = [0]

            def then(ins):
                done[0] += 1
                ins.then_inc(route, 1)
                dve.wait_ge(route, done[0])

            dve.sem_inc(y_lo_ok, 1)
            dve.sem_inc(hid_ok, 2)
            dve.sem_inc(base_ok, 2)
            then(dve.tensor_scalar(lt[:, :, :], k.logit[:, :, :], 1.0 / TAU, None, ALU.mult))
            for n in range(TT):
                ins = dve.max(top[:, n, :], lt[:, n, :])
            then(ins)
            for n in range(TT):
                ins = dve.max_index(top_i[:, n, :], top[:, n, :], lt[:, n, :])
            then(ins)
            dve.tensor_tensor(dif[:, :], top[:, :, 1], top[:, :, 0], ALU.subtract).then_inc(exped, 1)
            then(dve.tensor_copy(idx[:, :, :], top_i[:, :, 0:2]))
            dve.wait_ge(cst_in, 16)
            iota = cst[:, C_IOTA:C_IOTA + E].unsqueeze(1).broadcast_to([P, TT, E])
            for j in range(2):
                ins = dve.tensor_tensor(one_hot[j][:, :, :], iota, idx[:, :, j:j + 1].broadcast_to([P, TT, E]), ALU.is_equal)
            then(ins)
            dve.tensor_tensor(both[:, :, :], one_hot[0][:, :, :], one_hot[1][:, :, :], ALU.add).then_inc(both_ok, 1)
            dve.wait_ge(exped, 2)
            then(dve.tensor_scalar(ex1[:, :], ex[:, :], 1.0, None, ALU.add))
            then(dve.reciprocal(k.gate[0][:, :], ex1[:, :]))
            then(dve.tensor_tensor(k.gate[1][:, :], ex[:, :], k.gate[0][:, :], ALU.mult))
            dve.wait_ge(ranks, 1)
            then(dve.tensor_copy(tot[:, :, :], ps_r[1][:, :, :].rearrange("p t e -> p e t")))
            then(dve.tensor_tensor_scan(inc[:, :, :].rearrange("p e t -> p (e t)"), cst[:, C_SEG:C_SEG + TT * E],
                                        tot[:, :, :].rearrange("p e t -> p (e t)"), 0.0, ALU.mult, ALU.add))
            then(dve.tensor_tensor(exc[:, :, :], inc[:, :, :], tot[:, :, :], ALU.subtract))
            then(dve.tensor_tensor(more[:, :, :], inc[:, :, TT - 1:TT].broadcast_to([P, E, 8]),
                                   cst[:, C_J256:C_J256 + E * 8].rearrange("p (e j) -> p e j", e=E), ALU.is_gt))
            then(dve.tensor_reduce(tiles[:, :], more[:, :, :], AX_X, ALU.add))
            then(dve.tensor_tensor_scan(tend[:, :], cst[:, C_ONE:C_ONE + E], tiles[:, :], 0.0, ALU.mult, ALU.add))
            then(dve.tensor_tensor(tbeg[:, :], tend[:, :], tiles[:, :], ALU.subtract))
            then(dve.tensor_scalar(sbase[:, :], tbeg[:, :], float(ES), None, ALU.mult))
            then(dve.tensor_tensor(slot[:, :, :], ps_r[0][:, :, :], exc[:, :, :].rearrange("p e t -> p t e"), ALU.add))
            then(dve.tensor_tensor(slot2[:, :, :], slot[:, :, :], sbase[:, :].unsqueeze(1).broadcast_to([P, TT, E]), ALU.add))
            for j in range(2):
                ins = dve.tensor_tensor(mine[j][:, :, :], one_hot[j][:, :, :], slot2[:, :, :], ALU.mult)
            then(ins)
            for j in range(2):
                ins = dve.tensor_reduce(posf[j][:, :], mine[j][:, :, :], AX_X, ALU.add)
            then(ins)
            for j in range(2):
                dve.tensor_copy(k.pos[j][:, :], posf[j][:, :]).then_inc(pos_ok, 1)
            then(dve.tensor_tensor(past[:, :, :], tend[:, :].unsqueeze(1).broadcast_to([P, NT, E]),
                                   cst[:, C_TILE:C_TILE + NT * E].rearrange("p (t e) -> p t e", t=NT), ALU.is_le))
            then(dve.tensor_reduce(npast[:, :], past[:, :, :], AX_X, ALU.add))
            then(dve.tensor_scalar(k.tile_e[:, :], npast[:, :], float(E - 1), None, ALU.min))
            for j in range(2):
                for i in range(3):
                    cols = slice(i * PIECE, (i + 1) * PIECE)
                    dve.wait_ge(w_hi_ok, 3 * j + i + 1)
                    dve.tensor_tensor(w_lo[:, j, cols], w_raw[:, j, cols], w_hi[:, j, cols].bitcast(F32), ALU.subtract
                                      ).then_inc(w_lo_ok, 1)
            dve.wait_ge(par_in, 32)
            with dve.Fori(0, NB) as it:
                dve.wait_ge(y_hi_ok, it + 1)
                dve.tensor_tensor(y_lo[:, :, :], y_raw[:, :, :], y_hi[:, :, :].bitcast(F32), ALU.subtract
                                  ).then_inc(y_lo_ok, 1)
                for i in range(NI):
                    dve.wait_ge(gelu_ok, it * NI + i + 1)
                    dve.scalar_tensor_tensor(hid[i % 2][:, :], ps_a[i % 2][:, :], vec[:, V_BA + i:V_BA + i + 1],
                                             g_act[i % 2][:, :], ALU.add, ALU.mult).then_inc(hid_ok, 1)
                    dve.wait_ge(h_hi_ok, it * NI + i + 1)
                    dve.tensor_tensor(h_lo[i % 2][:, :], hid[i % 2][:, :], h_hi[i % 2][:, :].bitcast(F32), ALU.subtract
                                      ).then_inc(h_lo_ok, 1)
                dve.wait_ge(down_ok, it * NI + NI + 2)
                for i in range(2):
                    dve.tensor_tensor(k.base[:, ds(it * U + 2 * i, 2), :], ps_o[i][:, :, :],
                                      rows[:, R_BS2:R_BS2 + D].unsqueeze(1).broadcast_to([P, 2, D]), ALU.add
                                      ).then_inc(base_ok, 1)

        @block.tensor
        def _(pe):
            pe.sem_inc(down_ok, 2)
            pe.sem_inc(res_ok, 1)
            pe.wait_ge(cst_in, 16)
            pe.wait_ge(both_ok, 1)
            flat = both[:, :, :].rearrange("p t e -> p (t e)")
            pe.matmul(ps_r[0][:, :, :].rearrange("p t e -> p (t e)"), cst[:, C_TRI:C_TRI + P], flat, start=True, stop=True)
            pe.matmul(ps_r[1][:, :, :].rearrange("p t e -> p (t e)"), cst[:, C_ONE:C_ONE + P], flat, start=True, stop=True
                      ).then_inc(ranks, 1)
            pe.wait_ge(w_lo_ok, 6)

            def act_gate(it, i):
                j, t = divmod(i, ITP)
                pe.wait_ge(hid_ok, it * NI + i + 1)
                for dst, off in ((ps_a[i % 2], 0), (ps_g[i % 2], PIECE)):
                    for c in range(C):
                        cols = slice(off + c * PAIR + t * P, off + c * PAIR + (t + 1) * P)
                        wh, wl = w_hi[:, j, cols], w_lo[:, j, cols]
                        pe.matmul(dst[:, :], wh, y_hi[:, c, :], start=(c == 0), stop=False)
                        pe.matmul(dst[:, :], wh, y_lo[:, c, :], start=False, stop=False)
                        mm = pe.matmul(dst[:, :], wl, y_hi[:, c, :], start=False, stop=(c == C - 1))
                mm.then_inc(ag_ok, 1)

            def down(it, i):
                j, t = divmod(i, ITP)
                pe.wait_ge(h_lo_ok, it * NI + i + 1)
                cols = slice(2 * PIECE + t * D, 2 * PIECE + (t + 1) * D)
                wh, wl = w_hi[:, j, cols], w_lo[:, j, cols]
                for u in range(U):
                    tok = slice(u * P, (u + 1) * P)
                    hh, hl = h_hi[i % 2][:, tok], h_lo[i % 2][:, tok]
                    o = ps_o[u // 2][:, u % 2, :]
                    last = i == NI - 1
                    pe.matmul(o, hh, wh, start=False, stop=False, skip_group_check=True)
                    pe.matmul(o, hh, wl, start=False, stop=False, skip_group_check=True)
                    mm = pe.matmul(o, hl, wh, start=False, stop=last, skip_group_check=True)
                mm.then_inc(down_ok, 1)

            def residual(it):
                pe.wait_ge(x_in, it * 16 + 16)
                pe.wait_ge(base_ok, it * 2 + 2)
                for u in range(U):
                    for c in range(C):
                        mm = pe.matmul(ps_o[u // 2][:, u % 2, c * P:(c + 1) * P], x_raw[:, c, u * P:(u + 1) * P],
                                       cst[:, C_ID:C_ID + P], start=(u % 2 == 0 and c == 0), stop=False,
                                       skip_group_check=True)
                mm.then_inc(res_ok, 1)

            with pe.Fori(0, NB) as it:
                pe.wait_ge(y_lo_ok, it + 2)
                act_gate(it, 0)
                residual(it)
                for i in range(NI):
                    if i < NI - 1:
                        act_gate(it, i + 1)
                    down(it, i)


def stage_experts(nc, k):
    with ExitStack() as ctx:
        def sb(name, shape, dt=F32):
            return ctx.enter_context(nc.sbuf_tensor("e_" + name, shape, dt))

        def ps(name, shape, dt=F32):
            return ctx.enter_context(nc.psum_tensor("e_" + name, shape, dt))

        def sem(name):
            return ctx.enter_context(nc.semaphore("e_" + name))

        NP = FFN_PAIRS
        RING = 2 * NP
        NQ = 2 * NP
        STEPS = NT // 2
        U = ES // P
        NI = HR // P
        assert NT == 2 * STEPS + 1
        w_raw = [sb(f"w_raw{i}", [P, CHUNK]) for i in range(RING)]
        w_hi = sb("w_hi", [P, RING, CHUNK], F32R)
        w_lo = sb("w_lo", [P, RING, CHUNK], F32R)
        ident = sb("ident", [P, P])
        b1 = [sb(f"b1_{i}", [P, 2 * NI]) for i in range(2)]
        b2 = [sb(f"b2_{i}", [P, D]) for i in range(2)]
        x_raw = [sb(f"x_raw{i}", [P, U, D]) for i in range(2)]
        x_hi = [sb(f"x_hi{i}", [P, C, ES], F32R) for i in range(2)]
        x_lo = [sb(f"x_lo{i}", [P, C, ES], F32R) for i in range(2)]
        g_act = [sb(f"g_act{i}", [P, 2, ES]) for i in range(2)]
        hid = [sb(f"hid{i}", [P, 2, ES]) for i in range(2)]
        h_hi = [sb(f"h_hi{i}", [P, 2, ES], F32R) for i in range(2)]
        h_lo = [sb(f"h_lo{i}", [P, 2, ES], F32R) for i in range(2)]
        yo = [sb(f"yo{i}", [P, U, D]) for i in range(2)]
        ps_a = [ps(f"ps_a{i}", [P, 2, ES]) for i in range(2)]
        ps_g = [ps(f"ps_g{i}", [P, 2, ES]) for i in range(2)]
        ps_o = [ps(f"ps_o{i}", [P, U, D]) for i in range(2)]
        ps_t = ps("ps_t", [P, C, ES])

        id_in = sem("id_in")
        raw_in = [sem(f"raw_in{i}") for i in range(RING)]
        b_in = [sem(f"b_in{i}") for i in range(2)]
        x_in = [sem(f"x_in{i}") for i in range(2)]
        w_hi_ok = sem("w_hi_ok")
        w_lo_ok = sem("w_lo_ok")
        t_ok = sem("t_ok")
        x_hi_ok = sem("x_hi_ok")
        x_lo_ok = sem("x_lo_ok")
        ag_ok = sem("ag_ok")
        gelu_ok = sem("gelu_ok")
        hid_ok = sem("hid_ok")
        h_hi_ok = sem("h_hi_ok")
        h_lo_ok = sem("h_lo_ok")
        down_ok = sem("down_ok")
        yo_ok = sem("yo_ok")
        yo_free = sem("yo_free")
        y_out = sem("y_out")
        block = ctx.enter_context(nc.Block())
        x_v = k.x_slots.rearrange("(t u p) d -> p t u d", u=U, p=P)
        y_v = k.y_slots.rearrange("(t u p) d -> p t u d", u=U, p=P)

        @block.sync
        def _(sp):
            sp.dma_start(ident[:, :], k.consts[:, C_ID:C_ID + P]).then_inc(id_in, 16)

            def tile(it, half):
                t = it * 2 + half
                static = isinstance(it, int)
                tt = slice(t, t + 1) if static else ds(t, 1)
                e = sp.value_load(k.tile_e[0:1, tt], min_val=0, max_val=E - 1)
                sp.wait_ge(t_ok, t + 1)
                sp.dma_start(x_raw[half][:, :, :], x_v[:, tt, :, :].rearrange("p o u d -> p (o u) d")
                             ).then_inc(x_in[half], 16)
                for j in range(NP):
                    n = half * NP + j
                    sp.wait_ge(w_lo_ok, it * (3 * RING) + 3 * (n + 1))
                    sp.dma_start(w_raw[n][:, :], k.ffn_w[ds(e, 1), j].rearrange("e p n -> (e p) n")
                                 ).then_inc(raw_in[n], 16)

            with sp.Fori(0, STEPS) as it:
                for half in range(2):
                    tile(it, half)
            tile(STEPS, 0)

        @block.gpsimd
        def _(pool):
            pool.sem_inc(yo_free, 2)

            def biases(t, half):
                tt = slice(t, t + 1) if isinstance(t, int) else ds(t, 1)
                e = pool.value_load(k.tile_e[0:1, tt], min_val=0, max_val=E - 1)
                pool.dma_start(b1[half][:, :], k.be1[ds(e, 1)].rearrange("e p n -> (e p) n")).then_inc(b_in[half], 16)
                pool.dma_start(b2[half][:, :], k.be2[ds(e, 1), :].broadcast_to([P, D])).then_inc(b_in[half], 16)

            def store(t, half):
                tt = slice(t, t + 1) if isinstance(t, int) else ds(t, 1)
                pool.dma_start(y_v[:, tt, :, :].rearrange("p o u d -> p (o u) d"), yo[half][:, :, :]).then_inc(y_out, 16)

            def tile(it, half):
                pool.wait_ge(yo_ok, it * 2 + half + 3)
                store(it * 2 + half, half)
                biases(it * 2 + half + 2, half)
                pool.wait_ge(y_out, it * 32 + 16 * half + 16)
                pool.sem_inc(yo_free, 1)

            biases(0, 0)
            biases(1, 1)
            with pool.Fori(0, STEPS - 1) as it:
                for half in range(2):
                    tile(it, half)
            tile(STEPS - 1, 0)
            for t in (NT - 2, NT - 1):
                pool.wait_ge(yo_ok, t + 3)
                store(t, t % 2)
            pool.wait_ge(y_out, 16 * NT)

        @block.scalar
        def _(act):
            def weight_heads(slot, landed):
                act.wait_ge(raw_in[slot], landed)
                for i in range(3):
                    cols = slice(i * PIECE, (i + 1) * PIECE)
                    act.activation(w_hi[:, slot, cols], w_raw[slot][:, cols], ACT.Copy).then_inc(w_hi_ok, 1)

            def x_heads(it, half):
                act.wait_ge(t_ok, it * 2 + half + 3)
                act.activation(x_hi[half % 2][:, :, :], ps_t[:, :, :], ACT.Copy).then_inc(x_hi_ok, 1)

            x_heads(0, 0)
            for n in range(NP):
                weight_heads(n, 16)

            def step(it, last):
                for q in range(NP if last else NQ):
                    half, j = divmod(q, NP)
                    act.wait_ge(ag_ok, it * NQ + q + 1)
                    if j == 0:
                        act.wait_ge(b_in[half], it * 32 + 32)
                    for i in range(2):
                        b = NI + 2 * j + i
                        ins = act.activation(g_act[q % 2][:, i, :], ps_g[q % 2][:, i, :], ACT.Gelu, bias=b1[half][:, b:b + 1])
                    ins.then_inc(gelu_ok, 1)
                    act.wait_ge(hid_ok, it * NQ + q + 3)
                    act.wait_ge(down_ok, it * NQ + q + 1)
                    act.activation(h_hi[q % 2][:, :, :], hid[q % 2][:, :, :], ACT.Copy).then_inc(h_hi_ok, 1)
                    if not last:
                        n = q + NP
                        weight_heads(n % RING, it * 16 + 16 * (1 + n // RING))
                        if j == 1:
                            x_heads(it, half + 1)

            with act.Fori(0, STEPS) as it:
                step(it, False)
            step(STEPS, True)

        @block.vector
        def _(dve):
            dve.sem_inc(w_lo_ok, 3 * RING)
            dve.sem_inc(x_lo_ok, 1)
            dve.sem_inc(hid_ok, 2)
            dve.sem_inc(yo_ok, 2)

            def weight_tails(slot, heads):
                for i in range(3):
                    cols = slice(i * PIECE, (i + 1) * PIECE)
                    dve.wait_ge(w_hi_ok, heads + i + 1)
                    dve.tensor_tensor(w_lo[:, slot, cols], w_raw[slot][:, cols], w_hi[:, slot, cols].bitcast(F32),
                                      ALU.subtract).then_inc(w_lo_ok, 1)

            def x_tails(it, half):
                dve.wait_ge(x_hi_ok, it * 2 + half + 1)
                dve.tensor_tensor(x_lo[half % 2][:, :, :], ps_t[:, :, :], x_hi[half % 2][:, :, :].bitcast(F32),
                                  ALU.subtract).then_inc(x_lo_ok, 1)

            x_tails(0, 0)
            for n in range(NP):
                weight_tails(n, 3 * n)

            def step(it, last):
                for q in range(NP if last else NQ):
                    half, j = divmod(q, NP)
                    dve.wait_ge(gelu_ok, it * NQ + q + 1)
                    if j == 0:
                        dve.wait_ge(b_in[half], it * 32 + 32)
                    for i in range(2):
                        b = 2 * j + i
                        ins = dve.scalar_tensor_tensor(hid[q % 2][:, i, :], ps_a[q % 2][:, i, :], b1[half][:, b:b + 1],
                                                       g_act[q % 2][:, i, :], ALU.add, ALU.mult)
                    ins.then_inc(hid_ok, 1)
                    dve.wait_ge(h_hi_ok, it * NQ + q + 1)
                    dve.tensor_tensor(h_lo[q % 2][:, :, :], hid[q % 2][:, :, :], h_hi[q % 2][:, :, :].bitcast(F32),
                                      ALU.subtract).then_inc(h_lo_ok, 1)
                    if not last:
                        weight_tails((q + NP) % RING, it * (3 * NQ) + 3 * (q + NP))
                        if j == 1:
                            x_tails(it, half + 1)
                    if j == NP - 1:
                        dve.wait_ge(down_ok, it * NQ + q + 3)
                        dve.wait_ge(yo_free, it * 2 + half + 1)
                        dve.tensor_tensor(yo[half][:, :, :], ps_o[half][:, :, :],
                                          b2[half][:, :].unsqueeze(1).broadcast_to([P, U, D]), ALU.add).then_inc(yo_ok, 1)

            with dve.Fori(0, STEPS) as it:
                step(it, False)
            step(STEPS, True)

        @block.tensor
        def _(pe):
            pe.sem_inc(t_ok, 2)
            pe.sem_inc(down_ok, 2)
            pe.wait_ge(id_in, 16)

            def turn(it, half):
                pe.wait_ge(x_in[half % 2], it * 16 + 16 * (1 + half // 2))
                pe.wait_ge(x_lo_ok, it * 2 + half + 1)
                for u in range(U):
                    for c in range(C):
                        mm = pe.transpose(ps_t[:, c, u * P:(u + 1) * P], x_raw[half % 2][:, u, c * P:(c + 1) * P], ident[:, :])
                mm.then_inc(t_ok, 1)

            def gate_up(it, q):
                half, j = divmod(q, NP)
                slot, x = q % NQ, half % 2
                if j == 0:
                    pe.wait_ge(x_lo_ok, it * 2 + half + 2)
                pe.wait_ge(w_lo_ok, it * (3 * NQ) + 3 * (q + 1) + 3 * RING)
                pe.wait_ge(hid_ok, it * NQ + q + 1)
                for dst, off in ((ps_a[q % 2], 0), (ps_g[q % 2], PIECE)):
                    for i in range(2):
                        for c in range(C):
                            cols = slice(off + c * PAIR + i * P, off + c * PAIR + (i + 1) * P)
                            wh, wl = w_hi[:, slot, cols], w_lo[:, slot, cols]
                            pe.matmul(dst[:, i, :], wh, x_hi[x][:, c, :], start=(c == 0), stop=False)
                            pe.matmul(dst[:, i, :], wh, x_lo[x][:, c, :], start=False, stop=False)
                            mm = pe.matmul(dst[:, i, :], wl, x_hi[x][:, c, :], start=False, stop=(c == C - 1))
                mm.then_inc(ag_ok, 1)

            def down(it, q):
                half, j = divmod(q, NP)
                if j == 0:
                    pe.wait_ge(yo_ok, it * 2 + half + 1)
                pe.wait_ge(h_lo_ok, it * NQ + q + 1)
                for u in range(U):
                    tok = slice(u * P, (u + 1) * P)
                    for i in range(2):
                        cols = slice(2 * PIECE + i * D, 2 * PIECE + (i + 1) * D)
                        wh, wl = w_hi[:, q, cols], w_lo[:, q, cols]
                        hh, hl = h_hi[q % 2][:, i, tok], h_lo[q % 2][:, i, tok]
                        o = ps_o[half][:, u, :]
                        pe.matmul(o, hh, wh, start=(j == 0 and u == 0 and i == 0), stop=False, skip_group_check=True)
                        pe.matmul(o, hh, wl, start=False, stop=False, skip_group_check=True)
                        mm = pe.matmul(o, hl, wh, start=False, stop=(j == NP - 1 and i == 1), skip_group_check=True)
                mm.then_inc(down_ok, 1)

            turn(0, 0)
            gate_up(0, 0)

            def step(it, last):
                n = NP if last else NQ
                for q in range(n):
                    if not (last and q == n - 1):
                        gate_up(it, q + 1)
                    down(it, q)
                    if not last and q % NP == 0:
                        turn(it, q // NP + 1)

            with pe.Fori(0, STEPS) as it:
                step(it, False)
            step(STEPS, True)


def stage_combine(nc, k):
    with ExitStack() as ctx:
        def sb(name, shape, dt=F32):
            return ctx.enter_context(nc.sbuf_tensor("f_" + name, shape, dt))

        def sem(name):
            return ctx.enter_context(nc.semaphore("f_" + name))

        got = [sb(f"got{j}", [P, TT, D]) for j in range(2)]
        part = sb("part", [P, TT, D])
        res = sb("res", [P, TT, D])
        landed = [sem(f"landed{n}") for n in range(TT)]
        part_ok = sem("part_ok")
        res_ok = sem("res_ok")
        stored = sem("stored")
        block = ctx.enter_context(nc.Block())

        @block.gpsimd
        def _(pool):
            for n in range(TT):
                for j in range(2):
                    pool.indirect_dma_start(out=got[j][:, n, :], out_offset=None, in_=k.y_slots,
                                            in_offset=bass.IndirectOffsetOnAxis(ap=k.pos[j][:, n:n + 1], axis=0)
                                            ).then_inc(landed[n], 16)

        @block.vector
        def _(dve):
            for n in range(TT):
                dve.wait_ge(landed[n], 32)
                dve.scalar_tensor_tensor(part[:, n, :], got[0][:, n, :], k.gate[0][:, n:n + 1], k.base[:, n, :],
                                         ALU.mult, ALU.add).then_inc(part_ok, 1)
                dve.wait_ge(part_ok, n + 1)
                dve.scalar_tensor_tensor(res[:, n, :], got[1][:, n, :], k.gate[1][:, n:n + 1], part[:, n, :],
                                         ALU.mult, ALU.add).then_inc(res_ok, 1)

        @block.sync
        def _(sp):
            o_v = k.out.rearrange("(t p) d -> p t d", p=P)
            with sp.Fori(0, TT // 2) as n:
                sp.wait_ge(res_ok, n * 2 + 2)
                sp.dma_start(o_v[:, ds(n * 2, 2), :], res[:, ds(n * 2, 2), :]).then_inc(stored, 16)
            sp.wait_ge(stored, 16 * (TT // 2))


def program(nc, ins, out):
    k = Chip(ins, out)

    def dram(name, shape):
        return nc.dram_tensor(name, shape, F32, kind="Internal").ap()

    k.c_T = dram("c_T", (P, C, T))
    k.x2_T = dram("x2_T", (P, C, T))
    k.y_T = dram("y_T", (P, C, T))
    k.x_slots = dram("x_slots", (SLOTS, D))
    k.y_slots = dram("y_slots", (SLOTS, D))
    with ExitStack() as ctx:
        def sb(name, shape, dt=F32):
            return ctx.enter_context(nc.sbuf_tensor(name, shape, dt))

        k.pos = [sb(f"pos{j}", [P, TT], U32) for j in range(2)]
        k.gate = [sb(f"gate{j}", [P, TT]) for j in range(2)]
        k.tile_e = sb("tile_e", [P, NT], I32)
        stage_cond(nc, k)
        stage_attention(nc, k)
        k.base = sb("base", [P, TT, D])
        with ExitStack() as inner:
            k.logit = inner.enter_context(nc.sbuf_tensor("logit", [P, TT, E], F32))
            k.y_nat = inner.enter_context(nc.sbuf_tensor("y_nat", [P, TT, D], F32))
            stage_lora(nc, k)
            stage_route(nc, k)
        stage_experts(nc, k)
        stage_combine(nc, k)


def constants():
    a = np.zeros((P, C_W), np.float32)
    a[:, C_ID:C_ID + P] = np.eye(P)
    theta = np.pi / 2 * np.arange(1, B + 1) / B
    ang = np.sin(theta)[:, None] * np.sin(theta)[None] + np.cos(theta)[:, None] * np.cos(theta)[None]
    a[:, C_MASK:C_MASK + P] = np.kron(ang, np.eye(GRP))
    a[:, C_TRI:C_TRI + P] = np.triu(np.ones((P, P)), 1)
    a[:, C_ONE:C_ONE + P] = 1
    a[:, C_SEG:C_SEG + TT * E] = np.tile(np.arange(TT) != 0, E)
    a[:, C_IOTA:C_IOTA + E] = np.arange(E)
    a[:, C_EVEN] = (np.arange(P) // HD) % 2 == 0
    a[:, C_ODD] = (np.arange(P) // HD) % 2 == 1
    a[:, C_J256:C_J256 + E * 8] = np.tile(np.arange(8) * ES, E)
    a[:, C_TILE:C_TILE + NT * E] = np.repeat(np.arange(NT), E)
    return a


def halves(w):
    return w.reshape(C, P, -1).transpose(1, 0, 2)


def packed(**i):
    f = {n: np.asarray(v) for n, v in i.items()}
    cat = lambda *a: np.concatenate([x.reshape(P, -1) for x in a], axis=1)

    def mlp(gate, up, down, pairs):
        out = []
        for j in range(pairs):
            cols = slice(j * PAIR, (j + 1) * PAIR)
            out.append(cat(halves(gate[:, cols]), halves(up[:, cols]), halves(down[cols])))
        return np.stack(out)

    g, u, d = (f["L0_cond_skill_" + n] for n in ("gate", "up", "down"))
    cond = [mlp(g[e], u[e], d[e], COND_PAIRS) for e in range(COND_E)]
    cond.append(mlp(f["L0_cond_shared_gate"], f["L0_cond_shared_up"], f["L0_cond_shared_down"], COND_PAIRS))
    w1, w2 = f["L0_ffn_We1"], f["L0_ffn_We2"]
    col = lambda v: v.reshape(-1, P).T
    qkv_b, bs1, be1 = f["L0_attn_in_proj_bias"], f["L0_ffn_bs1"], f["L0_ffn_be1"]
    bs = f["L0_cond2_Bs"].transpose(0, 2, 1).reshape(P, D)
    rows = np.concatenate([qkv_b[2 * D:], f["L0_ffn_bs2"], f["L0_ffn_br"]])
    arrays = {
        "xT": halves(f["x"].reshape(T, D).T),
        "cond_8": f["cond_8"],
        "cond_w": np.stack(cond),
        "ffn_w": np.stack([mlp(w1[e][:, :HR], w1[e][:, HR:], w2[e], FFN_PAIRS) for e in range(E)]),
        "shared_w": mlp(f["L0_ffn_Ws1"][:, :HS], f["L0_ffn_Ws1"][:, HS:], f["L0_ffn_Ws2"], HS // PAIR),
        "attn_w": cat(halves(f["L0_attn_in_proj_weight"].T), halves(f["L0_attn_out_w"].T),
                      halves(f["L0_cond2_W_base"].T), halves(f["L0_cond2_As"].reshape(P, D).T), bs),
        "vec": cat(col(qkv_b[:D]), col(qkv_b[D:2 * D]), col(f["L0_attn_out_b"]), col(f["L0_cond2_b_base"]),
                   col(bs1[:HS]), col(bs1[HS:])),
        "rows": np.broadcast_to(rows, (P, R_W)),
        "router": halves(f["L0_ffn_Wr"]),
        "lora_w": np.repeat(f["cond_8"].T, LR, axis=0),
        "be1": be1.reshape(E, 2 * HR // P, P).transpose(0, 2, 1),
        "be2": f["L0_ffn_be2"],
        "consts": constants(),
    }
    return {n: np.ascontiguousarray(a) for n, a in arrays.items()}


def kernel(**inputs):
    import concourse.bacc as _bacc
    from concourse.bass_utils import run_bass_kernel_spmd as _run

    nc = _bacc.Bacc("TRN2", target_bir_lowering=False, num_devices=1)
    arrays = packed(**inputs)
    ins = {n: nc.dram_tensor("in_" + n, a.shape, F32, kind="ExternalInput").ap() for n, a in arrays.items()}
    out = nc.dram_tensor("out", (T, D), F32, kind="ExternalOutput").ap()
    program(nc, ins, out)
    r = _run(nc, [{"in_" + n: a for n, a in arrays.items()}], core_ids=[0])
    return r.results[0]["out"].reshape(B, S, D)
```

```python
from contextlib import ExitStack

import numpy as np

import concourse.bass as bass
from concourse import mybir

F32 = mybir.dt.float32
F32R = mybir.dt.float32r
I32 = mybir.dt.int32
U32 = mybir.dt.uint32
ALU = mybir.AluOpType
ACT = mybir.ActivationFunctionType
AX_X = mybir.AxisListType.X
ds = bass.ds

P = 128
B, S, D = 8, 256, 256
T = B * S
C = D // P
TT = T // P
COND_E, COND_I, COND_K = 8, 1024, 2
PAIR = 2 * P
PIECE = C * PAIR
CHUNK = 3 * PIECE
COND_PAIRS = COND_I // PAIR
MLPS = 1 + COND_K
H, HD = 16, 16
EPS = 1e-3
SG = 4
SGP = S // SG
GRP = 16
NG = SGP // GRP
SGT = SGP * B
LR = 16
LORA_SCALE = 2.0
E, HS, HR = 12, 512, 768
TAU = 1.5
ES = 256
NT = (2 * T + E * (ES - 1)) // ES
SLOTS = NT * ES
FFN_PAIRS = HR // PAIR
BLK = 512
NB = T // BLK

C_ID, C_MASK, C_HEADS = 0, P, 2 * P
C_HEAD = C_HEADS + P // HD
C_TRI = C_HEAD
C_ONE = C_TRI + P
C_SEG = C_ONE + P
C_IOTA = C_SEG + TT * E
C_J256 = C_IOTA + E
C_TILE = C_J256 + E * 8
C_W = C_TILE + NT * E

V_BQ, V_BK, V_OB, V_BB, V_BA, V_BG, V_W = 0, 2, 4, 6, 8, 12, 16
R_BV, R_BS2, R_BR, R_W = 0, D, 2 * D, 2 * D + E
W_QKV, W_O, W_B, W_A, W_L, W_W = 0, 1536, 2048, 2560, 2816, 3072


class Chip:

    def __init__(self, ins, out):
        self.xT = ins["xT"]
        self.cond_8 = ins["cond_8"]
        self.cond_w = ins["cond_w"]
        self.ffn_w = ins["ffn_w"]
        self.shared_w = ins["shared_w"]
        self.attn_w = ins["attn_w"]
        self.vec = ins["vec"]
        self.rows = ins["rows"]
        self.router = ins["router"]
        self.lora_w = ins["lora_w"]
        self.be1 = ins["be1"]
        self.be2 = ins["be2"]
        self.consts = ins["consts"]
        self.out = out


def stage_cond(nc, k):
    with ExitStack() as ctx:
        def sb(name, shape, dt=F32):
            return ctx.enter_context(nc.sbuf_tensor("a_" + name, shape, dt))

        def ps(name, shape, dt=F32):
            return ctx.enter_context(nc.psum_tensor("a_" + name, shape, dt))

        def sem(name):
            return ctx.enter_context(nc.semaphore("a_" + name))

        RING = 4
        NQ = 2 * MLPS * COND_PAIRS
        BQ = NQ // 2
        XP = COND_PAIRS * COND_K
        STEPS = B // 2

        cond = sb("cond", [B, COND_E])
        neg_top = sb("neg_top", [B, 1])
        ex = sb("ex", [B, COND_E])
        ex_sum = sb("ex_sum", [B, 1])
        ex_rec = sb("ex_rec", [B, 1])
        prob = sb("prob", [B, COND_E])
        top = sb("top", [B, 8])
        top_i = sb("top_i", [B, 8], U32)
        pair_sum = sb("pair_sum", [B, 1])
        pair_rec = sb("pair_rec", [B, 1])
        wk = sb("wk", [B, COND_K])
        wk1 = sb("wk1", [B, COND_K])
        wk3 = sb("wk3", [B, MLPS])
        w_row = sb("w_row", [1, B * MLPS])
        i_row = sb("i_row", [1, B * COND_K], U32)
        w_col = sb("w_col", [P, B * MLPS])

        w_raw = [sb(f"w_raw{i}", [P, CHUNK]) for i in range(RING)]
        w_hi = sb("w_hi", [P, RING + COND_PAIRS, CHUNK], F32R)
        w_lo = sb("w_lo", [P, RING + COND_PAIRS, CHUNK], F32R)
        x_raw = [sb(f"x_raw{i}", [P, C, S]) for i in range(2)]
        x_hi = [sb(f"x_hi{i}", [P, C, S], F32R) for i in range(2)]
        x_lo = [sb(f"x_lo{i}", [P, C, S], F32R) for i in range(2)]
        g_act = [sb(f"g_act{i}", [P, 2 * S]) for i in range(2)]
        hid = [sb(f"hid{i}", [P, 2 * S]) for i in range(2)]
        h_hi = [sb(f"h_hi{i}", [P, 2 * S], F32R) for i in range(2)]
        h_lo = [sb(f"h_lo{i}", [P, 2 * S], F32R) for i in range(2)]

        ps_g = [ps(f"ps_g{i}", [P, 2 * S]) for i in range(2)]
        ps_u = [ps(f"ps_u{i}", [P, 2 * S]) for i in range(2)]
        ps_d = [ps(f"ps_d{i}", [P, C, S]) for i in range(2)]
        ps_w = ps("ps_w", [P, 512])

        cond_in = sem("cond_in")
        ones_in = sem("ones_in")
        route = sem("route")
        exped = sem("exped")
        rows_in = sem("rows_in")
        w_bc = sem("w_bc")
        w_col_ok = sem("w_col_ok")
        raw_in = [sem(f"raw_in{i}") for i in range(RING)]
        x_in = [sem(f"x_in{i}") for i in range(2)]
        w_hi_ok = sem("w_hi_ok")
        w_lo_ok = sem("w_lo_ok")
        x_hi_ok = sem("x_hi_ok")
        x_lo_ok = sem("x_lo_ok")
        gu_ok = sem("gu_ok")
        gelu_ok = sem("gelu_ok")
        hid_ok = sem("hid_ok")
        h_hi_ok = sem("h_hi_ok")
        h_lo_ok = sem("h_lo_ok")
        down_ok = sem("down_ok")
        c_ok = sem("c_ok")
        par_in = sem("par_in")
        zeroed = sem("zeroed")
        x_out = sem("x_out")

        ident1 = sb("ident1", [1, P])
        ZN = SLOTS // P // 2
        zeros = sb("zeros", [P, SLOTS // P // ZN * D])

        block = ctx.enter_context(nc.Block())

        @block.sync
        def _(sp):
            sp.dma_start(cond[:, :], k.cond_8).then_inc(cond_in, 16)
            sp.dma_start(ident1[:, :], k.consts[0:1, C_ONE:C_ONE + P]).then_inc(ones_in, 16)
            for m in range(COND_PAIRS):
                if m == 1:
                    for b in range(2):
                        sp.dma_start(x_raw[b][:, :, :], k.xT[:, :, b * S:(b + 1) * S]).then_inc(x_in[b], 16)
                sp.dma_start(w_raw[m][:, :], k.cond_w[COND_E, m]).then_inc(raw_in[m], 16)
            sp.dma_start(k.attn_raw[:, :], k.attn_w).then_inc(par_in, 16)
            sp.dma_start(k.vec_sb[:, :], k.vec).then_inc(par_in, 16)
            sp.dma_start(k.rows_sb[:, :], k.rows).then_inc(par_in, 16)
            sp.dma_start(k.head_sb[:, :], k.consts[:, 0:C_HEAD]).then_inc(par_in, 16)
            sp.wait_ge(rows_in, 32)

            def batch(it, half):
                for n in range(XP):
                    e = expert[n // COND_PAIRS]
                    at = half * XP + n
                    sp.wait_ge(w_lo_ok, it * (6 * XP) + 3 * (at + 1))
                    sp.dma_start(w_raw[n % RING][:, :], k.cond_w[ds(e, 1), n % COND_PAIRS].rearrange("e p n -> (e p) n")
                                 ).then_inc(raw_in[n % RING], 16)

            def next_x(b, half):
                sp.wait_ge(x_lo_ok, b - 1)
                sp.dma_start(x_raw[half][:, :, :], k.xT[:, :, ds(b * S, S)]).then_inc(x_in[half], 16)

            with sp.Fori(0, STEPS - 1) as it:
                for half in range(2):
                    expert = [sp.value_load(i_row[0:1, ds(it * 4 + half * 2 + j, 1)], min_val=0, max_val=COND_E - 1)
                              for j in range(COND_K)]
                    batch(it, half)
                    next_x(it * 2 + half + 2, half)
            for half in range(2):
                b = 2 * (STEPS - 1) + half
                expert = [sp.value_load(i_row[0:1, 2 * b + j:2 * b + j + 1], min_val=0, max_val=COND_E - 1)
                          for j in range(COND_K)]
                batch(STEPS - 1, half)
            sp.wait_ge(par_in, 64)

        @block.gpsimd
        def _(pool):
            pool.wait_ge(route, 12)
            pool.dma_start(w_row[0:1, :].rearrange("o (b m) -> o b m", b=B), wk3[:, :]).then_inc(rows_in, 16)
            pool.dma_start(i_row[0:1, :].rearrange("o (b m) -> o b m", b=B), top_i[:, 0:COND_K]).then_inc(rows_in, 16)
            pool.memset(zeros[:, :], 0.0).then_inc(zeroed, 1)
            pool.wait_ge(zeroed, 1)
            x_v = k.x_slots.rearrange("(p a n) d -> p a (n d)", p=P, a=ZN)
            for i in range(ZN):
                pool.dma_start(x_v[:, i, :], zeros[:, :]).then_inc(x_out, 16)
            pool.wait_ge(x_out, 16 * ZN)

        @block.scalar
        def _(act):
            act.wait_ge(route, 1)
            act.wait_ge(cond_in, 16)
            act.activation(ex[:, :], cond[:, :], ACT.Exp, bias=neg_top[:, 0:1], accum_out=ex_sum[:, 0:1]).then_inc(exped, 1)

            def weight_heads(slot, raw, landed):
                act.wait_ge(raw_in[raw], landed)
                for i in range(3):
                    act.activation(w_hi[:, slot, i * PIECE:(i + 1) * PIECE],
                                   w_raw[raw][:, i * PIECE:(i + 1) * PIECE], ACT.Copy).then_inc(w_hi_ok, 1)

            def x_heads(half, landed):
                act.wait_ge(x_in[half], landed)
                act.activation(x_hi[half][:, :, :], x_raw[half][:, :, :], ACT.Copy).then_inc(x_hi_ok, 1)

            weight_heads(RING, 0, 16)
            x_heads(0, 16)
            for m in range(1, COND_PAIRS):
                weight_heads(RING + m, m, 16)

            def step(it, last):
                for q in range(NQ):
                    half, ql = divmod(q, BQ)
                    act.wait_ge(gu_ok, it * NQ + q + 1)
                    act.activation(g_act[q % 2][:, :], ps_g[q % 2][:, :], ACT.Gelu_apprx_tanh).then_inc(gelu_ok, 1)
                    act.wait_ge(hid_ok, it * NQ + q + 3)
                    act.wait_ge(down_ok, it * NQ + q + 1)
                    act.activation(h_hi[q % 2][:, :], hid[q % 2][:, :], ACT.Copy).then_inc(h_hi_ok, 1)
                    n = ql - 1
                    if 0 <= n < XP:
                        if n >= RING:
                            act.wait_ge(down_ok, it * NQ + half * BQ + n + 3)
                        weight_heads(n % RING, n % RING, it * (2 * XP // RING * 16) + 16 * (half * XP // RING + n // RING + 2))
                    if ql == BQ - 2 and not (last and half == 1):
                        x_heads(1 - half, it * 16 + 16 * (1 + half))

            with act.Fori(0, STEPS - 1) as it:
                step(it, False)
            step(STEPS - 1, True)

        @block.vector
        def _(dve):
            done = [0]

            def then(ins):
                done[0] += 1
                ins.then_inc(route, 1)
                dve.wait_ge(route, done[0])

            dve.sem_inc(hid_ok, 2)
            dve.sem_inc(c_ok, 2)
            dve.wait_ge(cond_in, 16)
            then(dve.tensor_reduce(neg_top[:, :], cond[:, :], AX_X, ALU.max, negate=True))
            dve.wait_ge(exped, 1)
            then(dve.reciprocal(ex_rec[:, :], ex_sum[:, :]))
            then(dve.tensor_scalar(prob[:, :], ex[:, :], ex_rec[:, 0:1], None, ALU.mult))
            then(dve.max(top[:, :], prob[:, :]))
            then(dve.max_index(top_i[:, :], top[:, :], prob[:, :]))
            then(dve.tensor_tensor(pair_sum[:, :], top[:, 0:1], top[:, 1:2], ALU.add))
            then(dve.reciprocal(pair_rec[:, :], pair_sum[:, :]))
            then(dve.tensor_scalar(wk[:, :], top[:, 0:COND_K], pair_rec[:, 0:1], None, ALU.mult))
            then(dve.tensor_scalar(wk1[:, :], wk[:, :], 1.0 / 12, None, ALU.mult))
            then(dve.tensor_scalar(wk[:, :], wk[:, :], 1.0 - 1.0 / 12, None, ALU.mult))
            then(dve.memset(wk3[:, 0:1], 1.0))
            then(dve.tensor_tensor(wk3[:, 1:MLPS], wk1[:, :], wk[:, :], ALU.add))
            dve.wait_ge(w_bc, 1)
            dve.tensor_copy(w_col[:, :], ps_w[:, 0:B * MLPS]).then_inc(w_col_ok, 1)

            def weight_tails(slot, raw, heads):
                for i in range(3):
                    dve.wait_ge(w_hi_ok, heads + i + 1)
                    cols = slice(i * PIECE, (i + 1) * PIECE)
                    dve.tensor_tensor(w_lo[:, slot, cols], w_raw[raw][:, cols], w_hi[:, slot, cols].bitcast(F32),
                                      ALU.subtract).then_inc(w_lo_ok, 1)

            def x_tails(half, b):
                dve.wait_ge(x_hi_ok, b + 1)
                dve.tensor_tensor(x_lo[half][:, :, :], x_raw[half][:, :, :], x_hi[half][:, :, :].bitcast(F32),
                                  ALU.subtract).then_inc(x_lo_ok, 1)

            weight_tails(RING, 0, 0)
            x_tails(0, 0)
            for m in range(1, COND_PAIRS):
                weight_tails(RING + m, m, 3 * m)
            dve.wait_ge(w_col_ok, 1)

            def step(it, last):
                for q in range(NQ):
                    half, ql = divmod(q, BQ)
                    m = ql // COND_PAIRS
                    dve.wait_ge(gelu_ok, it * NQ + q + 1)
                    col = it * (2 * MLPS) + half * MLPS + m
                    w = w_col[:, col:col + 1] if last else w_col[:, ds(col, 1)]
                    dve.scalar_tensor_tensor(hid[q % 2][:, :], ps_u[q % 2][:, :], w, g_act[q % 2][:, :],
                                             ALU.mult, ALU.mult).then_inc(hid_ok, 1)
                    dve.wait_ge(h_hi_ok, it * NQ + q + 1)
                    dve.tensor_tensor(h_lo[q % 2][:, :], hid[q % 2][:, :], h_hi[q % 2][:, :].bitcast(F32),
                                      ALU.subtract).then_inc(h_lo_ok, 1)
                    n = ql - 1
                    if 0 <= n < XP:
                        weight_tails(n % RING, n % RING, it * (6 * XP) + 3 * (COND_PAIRS + half * XP + n))
                    if ql == BQ - 2 and not (last and half == 1):
                        x_tails(1 - half, it * 2 + half + 1)
                    if ql == BQ - 1:
                        b = it * 2 + half
                        dve.wait_ge(down_ok, it * NQ + q + 3)
                        out = k.c_sb[:, b, :, :] if last else k.c_sb[:, ds(b, 1), :, :].rearrange("p o c s -> p (o c) s")
                        dve.tensor_copy(out, ps_d[half][:, :, :]).then_inc(c_ok, 1)

            with dve.Fori(0, STEPS - 1) as it:
                step(it, False)
            step(STEPS - 1, True)

        @block.tensor
        def _(pe):
            pe.sem_inc(down_ok, 2)
            pe.wait_ge(ones_in, 16)
            pe.wait_ge(rows_in, 32)
            pe.matmul(ps_w[:, 0:B * MLPS], ident1[0:1, :], w_row[0:1, :], start=True, stop=True).then_inc(w_bc, 1)

            def gate_up(it, q):
                half, ql = divmod(q % NQ, BQ)
                if ql == 0:
                    pe.wait_ge(x_lo_ok, it * 2 + q // BQ + 1)
                if ql >= COND_PAIRS:
                    n = ql - COND_PAIRS
                    slot = n % RING
                    pe.wait_ge(w_lo_ok, it * (6 * XP) + 3 * (COND_PAIRS + half * XP + n + 1))
                else:
                    slot = RING + ql
                    if isinstance(it, int) and it == -1:
                        pe.wait_ge(w_lo_ok, 3)
                pe.wait_ge(hid_ok, it * NQ + q + 1)
                for dst, off in ((ps_g[q % 2], 0), (ps_u[q % 2], PIECE)):
                    for i in range(2):
                        for c in range(C):
                            cols = slice(off + c * PAIR + i * P, off + c * PAIR + (i + 1) * P)
                            wh, wl = w_hi[:, slot, cols], w_lo[:, slot, cols]
                            o = dst[:, i * S:(i + 1) * S]
                            pe.matmul(o, wh, x_hi[half][:, c, :], start=(c == 0), stop=False)
                            pe.matmul(o, wh, x_lo[half][:, c, :], start=False, stop=False)
                            mm = pe.matmul(o, wl, x_hi[half][:, c, :], start=False, stop=(c == C - 1))
                mm.then_inc(gu_ok, 1)

            def down(it, q):
                half, ql = divmod(q, BQ)
                slot = (ql - COND_PAIRS) % RING if ql >= COND_PAIRS else RING + ql
                if ql == 0:
                    pe.wait_ge(c_ok, it * 2 + half + 1)
                pe.wait_ge(h_lo_ok, it * NQ + q + 1)
                for d in range(C):
                    for i in range(2):
                        cols = slice(2 * PIECE + i * D + d * P, 2 * PIECE + i * D + (d + 1) * P)
                        wh, wl = w_hi[:, slot, cols], w_lo[:, slot, cols]
                        hh, hl = h_hi[q % 2][:, i * S:(i + 1) * S], h_lo[q % 2][:, i * S:(i + 1) * S]
                        o = ps_d[half][:, d, :]
                        pe.matmul(o, wh, hh, start=(ql == 0 and d == 0 and i == 0), stop=False, skip_group_check=True)
                        pe.matmul(o, wh, hl, start=False, stop=False, skip_group_check=True)
                        mm = pe.matmul(o, wl, hh, start=False, stop=(ql == BQ - 1 and i == 1), skip_group_check=True)
                mm.then_inc(down_ok, 1)

            pe.wait_ge(w_lo_ok, 3 * COND_PAIRS)
            gate_up(0, 0)

            def step(it, last):
                for q in range(NQ):
                    if not (last and q == NQ - 1):
                        gate_up(it, q + 1)
                    down(it, q)

            with pe.Fori(0, STEPS - 1) as it:
                step(it, False)
            step(STEPS - 1, True)


def span(start, n):
    return slice(start, start + n) if isinstance(start, int) else ds(start, n)


def three(pe, o, sh, sl, mh, ml, first, last):
    pe.matmul(o, sh, mh, start=first, stop=False)
    pe.matmul(o, sh, ml, start=False, stop=False)
    return pe.matmul(o, sl, mh, start=False, stop=last)


def stage_attention(nc, k):
    with ExitStack() as ctx:
        def sb(name, shape, dt=F32):
            return ctx.enter_context(nc.sbuf_tensor("b_" + name, shape, dt))

        def ps(name, shape, dt=F32):
            return ctx.enter_context(nc.psum_tensor("b_" + name, shape, dt))

        def sem(name):
            return ctx.enter_context(nc.semaphore("b_" + name))

        ROWS = 32
        NJ = P // ROWS
        NS = NG * NJ
        LAG = 3
        WN = W_B
        VW = 2 * ROWS
        PW = (W_W - W_B) // BLK
        SW = CHUNK // BLK
        w_hi = sb("w_hi", [P, WN], F32R)
        w_lo = sb("w_lo", [P, WN], F32R)
        sh_raw = sb("sh_raw", [P, CHUNK])
        c_hi = sb("c_hi", [P, C, SGT], F32R)
        c_lo = sb("c_lo", [P, C, SGT], F32R)
        x_raw = sb("x_raw", [P, C, B, SGP])
        qq = sb("qq", [P, C, SGT])
        qm = [sb(f"qm{i}", [P, C, 2, P]) for i in range(2)]
        kk = sb("kk", [P, C, SGT])
        v_raw = sb("v_raw", [P, NG, H // 2, 2, HD])
        v_hi = sb("v_hi", [P, NG, H // 2, 2, VW], F32R)
        v_lo = sb("v_lo", [P, NG, H // 2, 2, VW], F32R)
        sm = [sb(f"sm{i}", [P, 4, P]) for i in range(2)]
        sm_hi = [sb(f"sm_hi{i}", [P, 4, P], F32R) for i in range(4)]
        sm_lo = [sb(f"sm_lo{i}", [P, 4, P], F32R) for i in range(4)]
        frame = sb("frame", [P, 2, VW])
        num = sb("num", [P, C, P])
        den = sb("den", [P, C, P])
        rec = sb("rec", [P, C, P])
        an = [sb(f"an{i}", [P, C, P]) for i in range(2)]
        at_hi = sb("at_hi", [P, C, SGT], F32R)
        at_lo = sb("at_lo", [P, C, SGT], F32R)
        o_tmp = [sb(f"o_tmp{i}", [P, SGT]) for i in range(C)]

        ps_a = [ps(f"ps_a{i}", [P, SGT]) for i in range(2)]
        ps_s = [ps(f"ps_s{i}", [P, 4 * P]) for i in range(2)]
        ps_o = [ps(f"ps_o{i}", [VW, NJ, C, P]) for i in range(2)]

        cst_in = sem("cst_in")
        sh_in = sem("sh_in")
        x_in = sem("x_in")
        w_hi_ok = sem("w_hi_ok")
        w_lo_ok = sem("w_lo_ok")
        late_hi_ok = sem("late_hi_ok")
        late_lo_ok = sem("late_lo_ok")
        qm_ok = [sem(f"qm{o}_ok") for o in range(2)]
        zero_ok = sem("zero_ok")
        lo_zero_ok = sem("lo_zero_ok")
        ones_ok = sem("ones_ok")
        c_hi_ok = sem("c_hi_ok")
        c_lo_ok = sem("c_lo_ok")
        pj_ok = sem("pj_ok")
        qk_ok = sem("qk_ok")
        v_ok = sem("v_ok")
        v_hi_ok = sem("v_hi_ok")
        v_lo_ok = sem("v_lo_ok")
        s_ok = sem("s_ok")
        m_ok = sem("m_ok")
        sm_hi_ok = sem("sm_hi_ok")
        sm_lo_ok = sem("sm_lo_ok")
        pv_ok = sem("pv_ok")
        den_ok = sem("den_ok")
        num_ok = sem("num_ok")
        rec_ok = sem("rec_ok")
        n_ok = sem("n_ok")
        ahi_ok = sem("ahi_ok")
        alo_ok = sem("alo_ok")
        op_ok = sem("op_ok")
        o_ok = sem("o_ok")
        x2_ok = sem("x2_ok")

        block = ctx.enter_context(nc.Block())

        @block.sync
        def _(sp):
            sp.dma_start(sh_raw[:, :], k.shared_w[0]).then_inc(sh_in, 16)
            sp.dma_start(k.cst[:, :], k.consts).then_inc(cst_in, 16)
            x_v = k.xT.rearrange("p c (b s) -> p c b s", b=B)
            with sp.Fori(0, SG) as it:
                sp.wait_ge(x2_ok, it * 2 + 2)
                for c in range(C):
                    sp.dma_start(x_raw[:, c, :, :], x_v[:, c, :, ds(it * SGP, SGP)]).then_inc(x_in, 16)
            sp.wait_ge(cst_in, 16)
            sp.wait_ge(late_lo_ok, PW + SW)
            sp.dma_start(sh_raw[:, :], k.shared_w[1]).then_inc(sh_in, 16)

        def grouped(ap):
            return ap.rearrange("p b (g s) -> p g b s", g=NG)

        def block_of(it, c):
            return grouped(k.c_sb[:, :, c, span(it * SGP, SGP)])

        def by_group(ap):
            return ap.rearrange("p (g b s) -> p g b s", g=NG, b=B)

        def late_piece(i):
            if i < PW:
                cols = slice(i * BLK, (i + 1) * BLK)
                return k.lora_hi[:, cols], k.lora_lo[:, cols], k.attn_raw[:, W_B + i * BLK:W_B + (i + 1) * BLK]
            j, t = divmod(i - PW, SW)
            cols = slice(t * BLK, (t + 1) * BLK)
            return k.sh_hi[:, j, cols], k.sh_lo[:, j, cols], sh_raw[:, cols]

        LATE = PW + 2 * SW

        @block.gpsimd
        def _(pool):
            pool.sem_inc(sm_lo_ok, 2)
            pool.sem_inc(alo_ok, 2)
            pool.wait_ge(zero_ok, 3)
            pool.tensor_scalar(v_lo[:, :, :, :, :].rearrange("p g h o d -> p (g h) (o d)"),
                               frame[:, :, :].rearrange("p o d -> p (o d)").unsqueeze(1).broadcast_to(
                                   [P, NG * H // 2, 2 * VW]), 0.0, None, ALU.mult).then_inc(lo_zero_ok, 1)
            pool.wait_ge(lo_zero_ok, 1)

            def value_tails(it):
                for g in range(NG):
                    pool.wait_ge(v_hi_ok, it * NG + g + 1)
                    for o in range(2):
                        cols = slice(o * HD, (o + 1) * HD)
                        ins = pool.tensor_tensor(v_lo[:, g, :, o, cols], v_raw[:, g, :, o, :],
                                                 v_hi[:, g, :, o, cols].bitcast(F32), ALU.subtract)
                    ins.then_inc(v_lo_ok, 1)

            def attended_tails(it, g):
                pool.wait_ge(ahi_ok, it * NG + g + 1)
                cols = slice(g * P, (g + 1) * P)
                pool.tensor_tensor(at_lo[:, :, cols], an[g % 2][:, :, :], at_hi[:, :, cols].bitcast(F32), ALU.subtract
                                   ).then_inc(alo_ok, 1)

            def step(it, last):
                for n in range(NS):
                    pool.wait_ge(sm_hi_ok, it * NS + n + 1)
                    pool.tensor_tensor(sm_lo[n % 4][:, :, :], sm[n % 2][:, :, :], sm_hi[n % 4][:, :, :].bitcast(F32),
                                       ALU.subtract).then_inc(sm_lo_ok, 1)
                    if n >= 2 * NJ + LAG and (n - LAG) % NJ == 0:
                        attended_tails(it, (n - LAG) // NJ - 2)
                attended_tails(it, NG - 2)
                attended_tails(it, NG - 1)
                if not last:
                    value_tails(it + 1)

            value_tails(0)
            with pool.Fori(0, SG - 1) as it:
                step(it, False)
            step(SG - 1, True)

        @block.scalar
        def _(act):
            def c_heads(it):
                for c in range(C):
                    act.activation(by_group(c_hi[:, c, :]), block_of(it, c), ACT.Copy).then_inc(c_hi_ok, 1)

            def masked(it, n):
                g, j = divmod(n, NJ)
                head = C_HEADS + 2 * j
                act.activation(qm[n % 2][:, :, 0, :], qq[:, :, g * P:(g + 1) * P], ACT.Copy,
                               scale=k.head_sb[:, head:head + 1]).then_inc(qm_ok[0], 1)

            def queries_keys(it):
                for e in range(C):
                    act.wait_ge(pj_ok, it * 8 + e + 1)
                    act.wait_ge(s_ok, it * NS + 1)
                    act.wait_ge(qm_ok[1], it * NS + 1)
                    act.activation(qq[:, e, :], ps_a[e][:, :], ACT.Relu, bias=k.vec_sb[:, V_BQ + e:V_BQ + e + 1]
                                   ).then_inc(qk_ok, 1)
                act.wait_ge(qk_ok, it * 4 + 2)
                masked(it, 0)
                masked(it, 1)
                for e in range(C):
                    act.wait_ge(pj_ok, it * 8 + e + 3)
                    act.activation(kk[:, e, :], ps_a[e][:, :], ACT.Relu, bias=k.vec_sb[:, V_BK + e:V_BK + e + 1]
                                   ).then_inc(qk_ok, 1)

            def value_heads(it):
                for g in range(NG):
                    act.wait_ge(v_ok, it * NG + g + 1)
                    for o in range(2):
                        ins = act.activation(v_hi[:, g, :, o, o * HD:(o + 1) * HD], v_raw[:, g, :, o, :], ACT.Copy)
                    ins.then_inc(v_hi_ok, 1)

            def numerators(it, g):
                act.wait_ge(pv_ok, it * NS + (g + 1) * NJ + 4)
                act.wait_ge(n_ok, it * NG + g + 1)
                for j in range(NJ):
                    ins = act.activation(num[j * ROWS:(j + 1) * ROWS, :, :],
                                         ps_o[g % 2][0:ROWS, j, :, :], ACT.Copy)
                ins.then_inc(num_ok, 1)

            def attended_heads(it, g):
                act.wait_ge(n_ok, it * NG + g + 2)
                act.activation(at_hi[:, :, g * P:(g + 1) * P], an[g % 2][:, :, :], ACT.Copy).then_inc(ahi_ok, 1)

            def step(it, last):
                for n in range(NS):
                    act.wait_ge(m_ok, it * NS + n + 3)
                    act.wait_ge(pv_ok, it * NS + n + 1)
                    act.activation(sm_hi[n % 4][:, :, :], sm[n % 2][:, :, :], ACT.Copy).then_inc(sm_hi_ok, 1)
                    if n + 2 < NS:
                        act.wait_ge(s_ok, it * NS + n + 2)
                        masked(it, n + 2)
                    if n >= NJ + LAG and (n - LAG) % NJ == 0:
                        if n >= 2 * NJ + LAG:
                            attended_heads(it, (n - LAG) // NJ - 2)
                        numerators(it, (n - LAG) // NJ - 1)
                    if not last and n == 1:
                        act.wait_ge(pj_ok, it * 8 + 8)
                        c_heads(it + 1)
                    if last and n < LATE:
                        if n in (PW, PW + SW):
                            act.wait_ge(sh_in, 16 * ((n - PW) // SW + 1))
                        hi, _, raw = late_piece(n)
                        act.activation(hi, raw, ACT.Copy).then_inc(late_hi_ok, 1)
                if not last:
                    queries_keys(it + 1)
                attended_heads(it, NG - 2)
                numerators(it, NG - 1)
                attended_heads(it, NG - 1)
                if not last:
                    value_heads(it + 1)
                for e in range(C):
                    act.wait_ge(op_ok, it * 2 + e + 1)
                    act.wait_ge(x2_ok, it * 2 + e + 1)
                    act.activation(o_tmp[e][:, :], ps_a[e][:, :], ACT.Identity, bias=k.vec_sb[:, V_OB + e:V_OB + e + 1]
                                   ).then_inc(o_ok, 1)

            c_heads(0)
            for i in range(WN // BLK):
                cols = slice(i * BLK, (i + 1) * BLK)
                act.activation(w_hi[:, cols], k.attn_raw[:, cols], ACT.Copy).then_inc(w_hi_ok, 1)
            queries_keys(0)
            act.wait_ge(ones_ok, 1)
            value_heads(0)
            with act.Fori(0, SG - 1) as it:
                step(it, False)
            step(SG - 1, True)

        @block.vector
        def _(dve):
            dve.sem_inc(m_ok, 2)
            dve.sem_inc(n_ok, 1)
            dve.sem_inc(den_ok, 2)
            dve.sem_inc(x2_ok, 2)
            dve.sem_inc(qm_ok[1], 1)
            mask = k.head_sb[:, C_MASK:C_MASK + P].unsqueeze(1).broadcast_to([P, 4, P])

            def c_tails(it):
                for c in range(C):
                    dve.wait_ge(c_hi_ok, it * 2 + c + 1)
                    dve.tensor_tensor(by_group(c_lo[:, c, :]), block_of(it, c), by_group(c_hi[:, c, :]).bitcast(F32),
                                      ALU.subtract).then_inc(c_lo_ok, 1)

            def masked(it, n):
                g, j = divmod(n, NJ)
                head = C_HEADS + 2 * j + 1
                dve.tensor_scalar(qm[n % 2][:, :, 1, :], qq[:, :, g * P:(g + 1) * P], k.head_sb[:, head:head + 1],
                                  None, ALU.mult).then_inc(qm_ok[1], 1)

            def first_masked(it):
                dve.wait_ge(qk_ok, it * 4 + 2)
                dve.wait_ge(s_ok, it * NS + 1)
                masked(it, 0)
                masked(it, 1)

            def values(it):
                for g in range(NG):
                    dve.wait_ge(pj_ok, it * 8 + g + 5)
                    dve.tensor_tensor(v_raw[:, g, :, :, :].rearrange("p h o d -> p (h o d)"), ps_a[g % 2][:, 0:D],
                                      k.rows_sb[:, R_BV:R_BV + D], ALU.add).then_inc(v_ok, 1)

            def norm(it, g, part):
                if part == 0:
                    dve.wait_ge(pv_ok, it * NS + (g + 1) * NJ + 4)
                if part < 2:
                    for j in (2 * part, 2 * part + 1):
                        ins = dve.tensor_scalar(den[j * ROWS:(j + 1) * ROWS, :, :], ps_o[g % 2][ROWS:VW, j, :, :],
                                                EPS, None, ALU.max)
                    if part == 1:
                        ins.then_inc(den_ok, 1)
                    return
                if part == 2:
                    dve.wait_ge(den_ok, it * NG + g + 3)
                dve.reciprocal(rec[:, part - 2, :], den[:, part - 2, :]).then_inc(rec_ok, 1)
                if part == 3:
                    dve.wait_ge(rec_ok, it * (2 * NG) + 2 * g + 2)
                    dve.wait_ge(num_ok, it * NG + g + 3)
                    dve.wait_ge(alo_ok, it * NG + g + 1)
                    dve.tensor_tensor(an[g % 2][:, :, :], num[:, :, :], rec[:, :, :], ALU.mult).then_inc(n_ok, 1)

            def step(it, last):
                for n in range(NS):
                    dve.wait_ge(s_ok, it * NS + n + 2)
                    dve.wait_ge(sm_lo_ok, it * NS + n + 1)
                    dve.tensor_tensor(sm[n % 2][:, :, :], ps_s[n % 2][:, :].rearrange("p (h t) -> p h t", h=4), mask,
                                      ALU.mult).then_inc(m_ok, 1)
                    if n + 2 < NS:
                        masked(it, n + 2)
                    if n >= NJ + LAG:
                        norm(it, *divmod(n - NJ - LAG, 4))
                    if not last and n == 3:
                        c_tails(it + 1)
                    if last and n < LATE:
                        dve.wait_ge(late_hi_ok, n + 1)
                        hi, lo, raw = late_piece(n)
                        dve.tensor_tensor(lo, raw, hi.bitcast(F32), ALU.subtract).then_inc(late_lo_ok, 1)
                for m in range(NS - NJ - LAG, NS - 4):
                    norm(it, *divmod(m, 4))
                if not last:
                    first_masked(it + 1)
                for part in range(4):
                    norm(it, NG - 1, part)
                if not last:
                    values(it + 1)
                dve.wait_ge(x_in, it * 32 + 32)
                for e in range(C):
                    dve.wait_ge(o_ok, it * 2 + e + 3)
                    dve.tensor_tensor(grouped(k.x2[:, e, :, span(it * SGP, SGP)]), by_group(o_tmp[e][:, :]),
                                      grouped(x_raw[:, e, :, :]), ALU.add).then_inc(x2_ok, 1)

            dve.memset(frame[:, :, :], 0.0).then_inc(zero_ok, 1)
            dve.wait_ge(zero_ok, 1)
            for o in range(2):
                dve.memset(frame[:, o, ROWS + o * HD:ROWS + (o + 1) * HD], 1.0).then_inc(zero_ok, 1)
            c_tails(0)
            for i in range(WN // BLK):
                cols = slice(i * BLK, (i + 1) * BLK)
                dve.wait_ge(w_hi_ok, i + 1)
                dve.tensor_tensor(w_lo[:, cols], k.attn_raw[:, cols], w_hi[:, cols].bitcast(F32), ALU.subtract
                                  ).then_inc(w_lo_ok, 1)
            first_masked(0)
            dve.wait_ge(zero_ok, 3)
            dve.tensor_copy(v_hi[:, :, :, :, :].rearrange("p g h o d -> p (g h) (o d)"),
                            frame[:, :, :].rearrange("p o d -> p (o d)").unsqueeze(1).broadcast_to(
                                [P, NG * H // 2, 2 * VW])).then_inc(ones_ok, 1)
            values(0)
            with dve.Fori(0, SG - 1) as it:
                step(it, False)
            step(SG - 1, True)

        @block.tensor
        def _(pe):
            pe.sem_inc(s_ok, 1)
            pe.sem_inc(pv_ok, 4)
            pe.sem_inc(o_ok, 2)
            pe.sem_inc(num_ok, 2)
            def query_key(it, n):
                e, base = n % 2, (n // 2) * D
                if n < 2:
                    if not (isinstance(it, int) and it == 0):
                        pe.wait_ge(o_ok, it * 2 + n - 1)
                else:
                    pe.wait_ge(qk_ok, it * 4 + n - 1)
                for c in range(C):
                    cols = slice(c * 3 * D + base + e * P, c * 3 * D + base + (e + 1) * P)
                    mm = three(pe, ps_a[n % 2][:, :], w_hi[:, cols], w_lo[:, cols], c_hi[:, c, :], c_lo[:, c, :],
                               c == 0, c == C - 1)
                mm.then_inc(pj_ok, 1)

            def value(it, g):
                if g < 2:
                    pe.wait_ge(qk_ok, it * 4 + g + 3)
                else:
                    pe.wait_ge(v_ok, it * NG + g - 1)
                tok = slice(g * P, (g + 1) * P)
                for c in range(C):
                    cols = slice(c * 3 * D + 2 * D, (c + 1) * 3 * D)
                    mm = three(pe, ps_a[g % 2][:, 0:D], c_hi[:, c, tok], c_lo[:, c, tok], w_hi[:, cols], w_lo[:, cols],
                               c == 0, c == C - 1)
                mm.then_inc(pj_ok, 1)

            def scores(it, n):
                g, j = divmod(n, NJ)
                tok = slice(g * P, (g + 1) * P)
                if n == 0:
                    pe.wait_ge(qk_ok, it * 4 + 4)
                pe.wait_ge(qm_ok[0], it * NS + n + 1)
                pe.wait_ge(qm_ok[1], it * NS + n + 2)
                pe.wait_ge(m_ok, it * NS + n + 1)
                for e in range(C):
                    mm = pe.matmul(ps_s[n % 2][:, e * 2 * P:(e + 1) * 2 * P], kk[:, e, tok], qm[n % 2][:, e, :, :],
                                   start=True, stop=True)
                mm.then_inc(s_ok, 1)

            def pv(it, n):
                g, j = divmod(n, NJ)
                if j == 0:
                    pe.wait_ge(num_ok, it * NG + g + 1)
                    pe.wait_ge(den_ok, it * NG + g + 1)
                    pe.wait_ge(v_lo_ok, it * NG + g + 1)
                pe.wait_ge(sm_lo_ok, it * NS + n + 3)
                for e in range(C):
                    for o in range(2):
                        s, pair = 2 * e + o, e * (H // 4) + j
                        out = ps_o[g % 2][:, j, e, :]
                        vh, vl = v_hi[:, g, pair, o, :], v_lo[:, g, pair, o, :]
                        pe.matmul(out, vh, sm_hi[n % 4][:, s, :], start=(j % 2 == 0 and s == 0), stop=False,
                                  skip_group_check=True)
                        pe.matmul(out, vh, sm_lo[n % 4][:, s, :], start=False, stop=False, skip_group_check=True)
                        mm = pe.matmul(out, vl, sm_hi[n % 4][:, s, :], start=False, stop=(o == 1),
                                       skip_group_check=True)
                mm.then_inc(pv_ok, 1)

            def output(it, last):
                pe.wait_ge(alo_ok, it * NG + NG + 2)
                for e in range(C):
                    if not last:
                        pe.wait_ge(v_ok, it * NG + NG + NG - 1 + e)
                    for c in range(C):
                        cols = slice(W_O + c * D + e * P, W_O + c * D + (e + 1) * P)
                        mm = three(pe, ps_a[e][:, :], w_hi[:, cols], w_lo[:, cols], at_hi[:, c, :], at_lo[:, c, :],
                                   c == 0, c == C - 1)
                    mm.then_inc(op_ok, 1)

            def step(it, last):
                for n in range(NS):
                    scores(it, n)
                    if n >= LAG:
                        pv(it, n - LAG)
                if not last:
                    pe.wait_ge(c_lo_ok, it * 2 + 4)
                    query_key(it + 1, 0)
                pv(it, NS - 3)
                if not last:
                    query_key(it + 1, 1)
                pv(it, NS - 2)
                pv(it, NS - 1)
                if not last:
                    query_key(it + 1, 2)
                    query_key(it + 1, 3)
                if not last:
                    for g in range(NG):
                        value(it + 1, g)
                output(it, last)

            pe.wait_ge(c_lo_ok, 2)
            for n in range(4):
                pe.wait_ge(w_lo_ok, 2 + n // 2)
                query_key(0, n)
            for g in range(NG):
                value(0, g)
            pe.wait_ge(ones_ok, 1)
            pe.wait_ge(w_lo_ok, WN // BLK)
            with pe.Fori(0, SG - 1) as it:
                step(it, False)
            step(SG - 1, True)


def stage_lora(nc, k):
    with ExitStack() as ctx:
        def sb(name, shape, dt=F32):
            return ctx.enter_context(nc.sbuf_tensor("c_" + name, shape, dt))

        def ps(name, shape, dt=F32):
            return ctx.enter_context(nc.psum_tensor("c_" + name, shape, dt))

        def sem(name):
            return ctx.enter_context(nc.semaphore("c_" + name))

        A0, L0 = W_A - W_B, W_L - W_B
        U = BLK // P
        router = sb("router", [P, C, E])
        lora_raw = sb("lora_raw", [P, B])
        lora_w = sb("lora_w", [P, B])
        x_hi = sb("x_hi", [P, C, BLK], F32R)
        x_lo = sb("x_lo", [P, C, BLK], F32R)
        ha = sb("ha", [P, BLK])
        ha_hi = sb("ha_hi", [P, BLK], F32R)
        ha_lo = sb("ha_lo", [P, BLK], F32R)
        y = sb("y", [P, C, BLK])
        logit = sb("logit", [P, U, E])
        lt = sb("lt", [P, U, E])
        top = sb("top", [P, U, 8])
        top_i = sb("top_i", [P, U, 8], U32)
        idx = sb("idx", [P, U, 2])
        ps_h = ps("ps_h", [P, BLK])
        ps_y = [ps(f"ps_y{i}", [P, BLK]) for i in range(C)]
        ps_l = ps("ps_l", [P, U, E])
        ps_t = [ps(f"ps_t{i}", [P, 2, D]) for i in range(2)]

        par_in = sem("par_in")
        lw_ok = sem("lw_ok")
        x_hi_ok = sem("x_hi_ok")
        x_lo_ok = sem("x_lo_ok")
        h_ok = sem("h_ok")
        ha_ok = sem("ha_ok")
        ha_hi_ok = sem("ha_hi_ok")
        ha_lo_ok = sem("ha_lo_ok")
        ym_ok = sem("ym_ok")
        y_ok = sem("y_ok")
        y_hi_ok = sem("y_hi_ok")
        y_lo_ok = sem("y_lo_ok")
        yb_ok = sem("yb_ok")
        lm_ok = sem("lm_ok")
        lg_ok = sem("lg_ok")
        t_ok = sem("t_ok")
        yn_ok = sem("yn_ok")
        route = sem("route")
        block = ctx.enter_context(nc.Block())

        @block.sync
        def _(sp):
            sp.dma_start(lora_raw[:, :], k.lora_w).then_inc(par_in, 16)
            sp.dma_start(router[:, :, :], k.router).then_inc(par_in, 16)

        def x2_of(it):
            return k.x2[:, :, span(it * 2, 2), :].rearrange("p c b s -> p c (b s)")

        @block.gpsimd
        def _(pool):
            pool.sem_inc(y_lo_ok, 2)
            with pool.Fori(0, NB) as it:
                for o in range(C):
                    pool.wait_ge(y_hi_ok, it * 2 + o + 1)
                    cols = ds(it * BLK, BLK)
                    pool.tensor_tensor(k.y_lo[:, o, cols], y[:, o, :], k.y_hi[:, o, cols].bitcast(F32), ALU.subtract
                                       ).then_inc(y_lo_ok, 1)

        @block.scalar
        def _(act):
            def x_heads(it):
                act.activation(x_hi[:, :, :], x2_of(it), ACT.Copy).then_inc(x_hi_ok, 1)

            def hidden_heads(it):
                act.wait_ge(ha_ok, it * 2 + 2)
                act.activation(ha_hi[:, :], ha[:, :], ACT.Copy).then_inc(ha_hi_ok, 1)

            def outputs(it):
                for o in range(C):
                    act.wait_ge(ym_ok, it * 2 + o + 1)
                    act.wait_ge(y_lo_ok, it * 2 + o + 1)
                    act.activation(y[:, o, :], ps_y[o][:, :], ACT.Identity, bias=k.vec_sb[:, V_BB + o:V_BB + o + 1]
                                   ).then_inc(y_ok, 1)
                for o in range(C):
                    act.wait_ge(y_ok, it * 2 + o + 1)
                    act.activation(k.y_hi[:, o, span(it * BLK, BLK)], y[:, o, :], ACT.Copy).then_inc(y_hi_ok, 1)

            x_heads(0)
            hidden_heads(0)
            with act.Fori(0, NB - 1) as it:
                act.wait_ge(yb_ok, it + 1)
                x_heads(it + 1)
                outputs(it)
                hidden_heads(it + 1)
            outputs(NB - 1)

        @block.vector
        def _(dve):
            R = 4
            dve.sem_inc(lg_ok, 1)
            dve.sem_inc(yn_ok, 2)

            def x_tails(it):
                dve.wait_ge(x_hi_ok, it + 1)
                dve.tensor_tensor(x_lo[:, :, :], x2_of(it), x_hi[:, :, :].bitcast(F32), ALU.subtract
                                  ).then_inc(x_lo_ok, 1)

            def hidden(it):
                dve.wait_ge(h_ok, it + 1)
                for b in range(2):
                    cols = slice(b * S, (b + 1) * S)
                    dve.tensor_scalar(ha[:, cols], ps_h[:, cols], lora_w[:, span(it * 2 + b, 1)], None, ALU.mult
                                      ).then_inc(ha_ok, 1)
                dve.wait_ge(ha_hi_ok, it + 1)
                dve.tensor_tensor(ha_lo[:, :], ha[:, :], ha_hi[:, :].bitcast(F32), ALU.subtract).then_inc(ha_lo_ok, 1)

            def turned(it):
                for i in range(2):
                    dve.wait_ge(t_ok, it * 2 + i + 1)
                    dve.tensor_copy(k.y_nat[:, span(it * U + 2 * i, 2), :], ps_t[i][:, :, :]).then_inc(yn_ok, 1)

            def choices(it):
                tiles = span(it * U, U)
                dve.wait_ge(lm_ok, it + 1)
                dve.tensor_tensor(logit[:, :, :], ps_l[:, :, :],
                                  k.rows_sb[:, R_BR:R_BR + E].unsqueeze(1).broadcast_to([P, U, E]), ALU.add
                                  ).then_inc(route, 1)
                dve.wait_ge(route, it * R + 1)
                dve.tensor_scalar(lt[:, :, :], logit[:, :, :], 1.0 / TAU, None, ALU.mult).then_inc(lg_ok, 1)
                dve.wait_ge(lg_ok, it + 2)
                turned(it)
                for u in range(U):
                    ins = dve.max(top[:, u, :], lt[:, u, :])
                ins.then_inc(route, 1)
                dve.wait_ge(route, it * R + 2)
                dve.tensor_tensor(k.dif[:, tiles], top[:, :, 1], top[:, :, 0], ALU.subtract)
                for u in range(U):
                    ins = dve.max_index(top_i[:, u, :], top[:, u, :], lt[:, u, :])
                ins.then_inc(route, 1)
                dve.wait_ge(route, it * R + 3)
                dve.tensor_copy(idx[:, :, :], top_i[:, :, 0:2]).then_inc(route, 1)
                dve.wait_ge(route, it * R + 4)
                iota = k.cst[:, C_IOTA:C_IOTA + E].unsqueeze(1).broadcast_to([P, U, E])
                for j in range(2):
                    dve.tensor_tensor(k.one_hot[j][:, tiles, :], iota, idx[:, :, j:j + 1].broadcast_to([P, U, E]),
                                      ALU.is_equal)

            x_tails(0)
            dve.wait_ge(par_in, 32)
            dve.tensor_scalar(lora_w[:, :], lora_raw[:, :], LORA_SCALE, None, ALU.mult).then_inc(lw_ok, 1)
            dve.wait_ge(lw_ok, 1)
            hidden(0)
            with dve.Fori(0, NB - 1) as it:
                x_tails(it + 1)
                hidden(it + 1)
                choices(it)
            choices(NB - 1)

        @block.tensor
        def _(pe):
            def base(it):
                pe.wait_ge(x_lo_ok, it + 1)
                for c in range(C):
                    cols = slice(A0 + c * P, A0 + (c + 1) * P)
                    mm = three(pe, ps_h[:, :], k.lora_hi[:, cols], k.lora_lo[:, cols], x_hi[:, c, :], x_lo[:, c, :],
                               c == 0, c == C - 1)
                mm.then_inc(h_ok, 1)
                for o in range(C):
                    if not (isinstance(it, int) and it == 0):
                        pe.wait_ge(y_ok, it * 2 + o - 1)
                    for c in range(C):
                        cols = slice(c * D + o * P, c * D + (o + 1) * P)
                        mm = three(pe, ps_y[o][:, :], k.lora_hi[:, cols], k.lora_lo[:, cols], x_hi[:, c, :],
                                   x_lo[:, c, :], c == 0, False)
                mm.then_inc(yb_ok, 1)

            def lora(it):
                pe.wait_ge(ha_lo_ok, it + 1)
                for o in range(C):
                    cols = slice(L0 + o * P, L0 + (o + 1) * P)
                    three(pe, ps_y[o][:, :], k.lora_hi[:, cols], k.lora_lo[:, cols], ha_hi[:, :], ha_lo[:, :], False,
                          True).then_inc(ym_ok, 1)

            def finish(it):
                pe.wait_ge(y_ok, it * 2 + 2)
                pe.wait_ge(lg_ok, it + 1)
                for u in range(U):
                    for c in range(C):
                        mm = pe.matmul(ps_l[:, u, :], y[:, c, u * P:(u + 1) * P], router[:, c, :],
                                       start=(c == 0), stop=(c == C - 1))
                mm.then_inc(lm_ok, 1)
                for i in range(2):
                    pe.wait_ge(yn_ok, it * 2 + i + 1)
                    for u in range(2):
                        for c in range(C):
                            tok = slice((2 * i + u) * P, (2 * i + u + 1) * P)
                            mm = pe.transpose(ps_t[i][:, u, c * P:(c + 1) * P], y[:, c, tok],
                                              k.head_sb[:, C_ID:C_ID + P])
                    mm.then_inc(t_ok, 1)

            base(0)
            lora(0)
            pe.wait_ge(par_in, 32)
            with pe.Fori(0, NB - 1) as it:
                base(it + 1)
                finish(it)
                lora(it + 1)
            finish(NB - 1)


def stage_route(nc, k):
    with ExitStack() as ctx:
        def sb(name, shape, dt=F32):
            return ctx.enter_context(nc.sbuf_tensor("d_" + name, shape, dt))

        def ps(name, shape, dt=F32):
            return ctx.enter_context(nc.psum_tensor("d_" + name, shape, dt))

        def sem(name):
            return ctx.enter_context(nc.semaphore("d_" + name))

        NI = HS // P
        U = BLK // P
        ITP = 2
        cst, vec, rows, one_hot = k.cst, k.vec_sb, k.rows_sb, k.one_hot
        ex = sb("ex", [P, TT])
        ex1 = sb("ex1", [P, TT])
        both = sb("both", [P, TT, E])
        tot = sb("tot", [P, E, TT])
        inc = sb("inc", [P, E, TT])
        exc = sb("exc", [P, E, TT])
        more = sb("more", [P, E, 8])
        tiles = sb("tiles", [P, E])
        tend = sb("tend", [P, E])
        tbeg = sb("tbeg", [P, E])
        sbase = sb("sbase", [P, E])
        slot = sb("slot", [P, TT, E])
        slot2 = sb("slot2", [P, TT, E])
        mine = [sb(f"mine{i}", [P, TT, E]) for i in range(2)]
        posf = [sb(f"posf{i}", [P, TT]) for i in range(2)]
        past = sb("past", [P, NT, E])
        npast = sb("npast", [P, NT])
        w_hi, w_lo = k.sh_hi, k.sh_lo
        x_raw = sb("x_raw", [P, C, BLK])
        base = [sb(f"base{i}", [P, 2, D]) for i in range(2)]
        g_act = [sb(f"g_act{i}", [P, BLK]) for i in range(2)]
        hid = [sb(f"hid{i}", [P, BLK]) for i in range(2)]
        h_hi = [sb(f"h_hi{i}", [P, BLK], F32R) for i in range(2)]
        h_lo = [sb(f"h_lo{i}", [P, BLK], F32R) for i in range(2)]
        ps_a = [ps(f"ps_a{i}", [P, BLK]) for i in range(2)]
        ps_g = [ps(f"ps_g{i}", [P, BLK]) for i in range(2)]
        ps_o = [ps(f"ps_o{i}", [P, 2, D]) for i in range(2)]
        ps_r = [ps(f"ps_r{i}", [P, TT, E]) for i in range(2)]

        x_in = sem("x_in")
        route = sem("route")
        exped = sem("exped")
        ranks = sem("ranks")
        both_ok = sem("both_ok")
        pos_ok = sem("pos_ok")
        moved = sem("moved")
        ag_ok = sem("ag_ok")
        gelu_ok = sem("gelu_ok")
        hid_ok = sem("hid_ok")
        h_hi_ok = sem("h_hi_ok")
        h_lo_ok = sem("h_lo_ok")
        down_ok = sem("down_ok")
        res_ok = sem("res_ok")
        base_ok = sem("base_ok")
        base_out = [sem(f"base_out{i}") for i in range(2)]
        block = ctx.enter_context(nc.Block())

        @block.sync
        def _(sp):
            out_v = k.base.rearrange("(t p) d -> p t d", p=P)

            def load(it):
                for c in range(C):
                    sp.dma_start(x_raw[:, c, :], k.x2[:, c, span(it * 2, 2), :].rearrange("p b s -> p (b s)")
                                 ).then_inc(x_in, 16)

            def store(it):
                for i in range(2):
                    sp.wait_ge(base_ok, it * 2 + i + 3)
                    sp.dma_start(out_v[:, span(it * U + 2 * i, 2), :], base[i][:, :, :]).then_inc(base_out[i], 16)

            for i in range(2):
                sp.sem_inc(base_out[i], 16)
            load(0)
            with sp.Fori(0, NB - 1) as it:
                sp.wait_ge(res_ok, it + 1)
                load(it + 1)
                store(it)
            store(NB - 1)
            for i in range(2):
                sp.wait_ge(base_out[i], 16 * NB + 16)

        @block.gpsimd
        def _(pool):
            pool.wait_ge(pos_ok, 2)
            for n in range(TT):
                for j in range(2):
                    pool.indirect_dma_start(out=k.x_slots, out_offset=bass.IndirectOffsetOnAxis(ap=k.pos[j][:, n:n + 1], axis=0),
                                            in_=k.y_nat[:, n, :], in_offset=None).then_inc(moved, 16)
            pool.wait_ge(moved, 16 * 2 * TT)

        @block.scalar
        def _(act):
            act.activation(ex[:, :], k.dif[:, :], ACT.Exp).then_inc(exped, 1)
            with act.Fori(0, NB) as it:
                for i in range(NI):
                    act.wait_ge(ag_ok, it * NI + i + 1)
                    act.activation(g_act[i % 2][:, :], ps_g[i % 2][:, :], ACT.Gelu, bias=vec[:, V_BG + i:V_BG + i + 1]
                                   ).then_inc(gelu_ok, 1)
                    act.wait_ge(hid_ok, it * NI + i + 3)
                    act.wait_ge(down_ok, it * NI + i + 1)
                    act.activation(h_hi[i % 2][:, :], hid[i % 2][:, :], ACT.Copy).then_inc(h_hi_ok, 1)

        @block.vector
        def _(dve):
            done = [0]

            def then(ins):
                done[0] += 1
                ins.then_inc(route, 1)
                dve.wait_ge(route, done[0])

            dve.sem_inc(hid_ok, 2)
            dve.sem_inc(base_ok, 2)
            dve.tensor_tensor(both[:, :, :], one_hot[0][:, :, :], one_hot[1][:, :, :], ALU.add).then_inc(both_ok, 1)
            dve.wait_ge(exped, 1)
            then(dve.tensor_scalar(ex1[:, :], ex[:, :], 1.0, None, ALU.add))
            then(dve.reciprocal(k.gate[0][:, :], ex1[:, :]))
            then(dve.tensor_tensor(k.gate[1][:, :], ex[:, :], k.gate[0][:, :], ALU.mult))
            dve.wait_ge(ranks, 1)
            then(dve.tensor_copy(tot[:, :, :], ps_r[1][:, :, :].rearrange("p t e -> p e t")))
            then(dve.tensor_tensor_scan(inc[:, :, :].rearrange("p e t -> p (e t)"), cst[:, C_SEG:C_SEG + TT * E],
                                        tot[:, :, :].rearrange("p e t -> p (e t)"), 0.0, ALU.mult, ALU.add))
            then(dve.tensor_tensor(exc[:, :, :], inc[:, :, :], tot[:, :, :], ALU.subtract))
            then(dve.tensor_tensor(more[:, :, :], inc[:, :, TT - 1:TT].broadcast_to([P, E, 8]),
                                   cst[:, C_J256:C_J256 + E * 8].rearrange("p (e j) -> p e j", e=E), ALU.is_gt))
            then(dve.tensor_reduce(tiles[:, :], more[:, :, :], AX_X, ALU.add))
            then(dve.tensor_tensor_scan(tend[:, :], cst[:, C_ONE:C_ONE + E], tiles[:, :], 0.0, ALU.mult, ALU.add))
            then(dve.tensor_tensor(tbeg[:, :], tend[:, :], tiles[:, :], ALU.subtract))
            then(dve.tensor_scalar(sbase[:, :], tbeg[:, :], float(ES), None, ALU.mult))
            then(dve.tensor_tensor(slot[:, :, :], ps_r[0][:, :, :], exc[:, :, :].rearrange("p e t -> p t e"), ALU.add))
            then(dve.tensor_tensor(slot2[:, :, :], slot[:, :, :], sbase[:, :].unsqueeze(1).broadcast_to([P, TT, E]), ALU.add))
            for j in range(2):
                ins = dve.tensor_tensor(mine[j][:, :, :], one_hot[j][:, :, :], slot2[:, :, :], ALU.mult)
            then(ins)
            for j in range(2):
                ins = dve.tensor_reduce(posf[j][:, :], mine[j][:, :, :], AX_X, ALU.add)
            then(ins)
            for j in range(2):
                dve.tensor_copy(k.pos[j][:, :], posf[j][:, :]).then_inc(pos_ok, 1)
            then(dve.tensor_tensor(past[:, :, :], tend[:, :].unsqueeze(1).broadcast_to([P, NT, E]),
                                   cst[:, C_TILE:C_TILE + NT * E].rearrange("p (t e) -> p t e", t=NT), ALU.is_le))
            then(dve.tensor_reduce(npast[:, :], past[:, :, :], AX_X, ALU.add))
            then(dve.tensor_scalar(k.tile_e[:, :], npast[:, :], float(E - 1), None, ALU.min))
            with dve.Fori(0, NB) as it:
                for i in range(NI):
                    dve.wait_ge(gelu_ok, it * NI + i + 1)
                    dve.scalar_tensor_tensor(hid[i % 2][:, :], ps_a[i % 2][:, :], vec[:, V_BA + i:V_BA + i + 1],
                                             g_act[i % 2][:, :], ALU.add, ALU.mult).then_inc(hid_ok, 1)
                    dve.wait_ge(h_hi_ok, it * NI + i + 1)
                    dve.tensor_tensor(h_lo[i % 2][:, :], hid[i % 2][:, :], h_hi[i % 2][:, :].bitcast(F32), ALU.subtract
                                      ).then_inc(h_lo_ok, 1)
                dve.wait_ge(down_ok, it * NI + NI + 2)
                for i in range(2):
                    dve.wait_ge(base_out[i], it * 16 + 16)
                    dve.tensor_tensor(base[i][:, :, :], ps_o[i][:, :, :],
                                      rows[:, R_BS2:R_BS2 + D].unsqueeze(1).broadcast_to([P, 2, D]), ALU.add
                                      ).then_inc(base_ok, 1)

        @block.tensor
        def _(pe):
            pe.sem_inc(down_ok, 2)
            def act_gate(it, i):
                j, t = divmod(i, ITP)
                pe.wait_ge(hid_ok, it * NI + i + 1)
                tok = span((it + i // NI) * BLK, BLK)
                i, j = i % NI, j % (NI // ITP)
                for dst, off in ((ps_a[i % 2], 0), (ps_g[i % 2], PIECE)):
                    for c in range(C):
                        cols = slice(off + c * PAIR + t * P, off + c * PAIR + (t + 1) * P)
                        wh, wl = w_hi[:, j, cols], w_lo[:, j, cols]
                        pe.matmul(dst[:, :], wh, k.y_hi[:, c, tok], start=(c == 0), stop=False)
                        pe.matmul(dst[:, :], wh, k.y_lo[:, c, tok], start=False, stop=False)
                        mm = pe.matmul(dst[:, :], wl, k.y_hi[:, c, tok], start=False, stop=(c == C - 1))
                mm.then_inc(ag_ok, 1)

            def down(it, i):
                j, t = divmod(i, ITP)
                pe.wait_ge(h_lo_ok, it * NI + i + 1)
                cols = slice(2 * PIECE + t * D, 2 * PIECE + (t + 1) * D)
                wh, wl = w_hi[:, j, cols], w_lo[:, j, cols]
                for u in range(U):
                    tok = slice(u * P, (u + 1) * P)
                    hh, hl = h_hi[i % 2][:, tok], h_lo[i % 2][:, tok]
                    o = ps_o[u // 2][:, u % 2, :]
                    last = i == NI - 1
                    pe.matmul(o, hh, wh, start=False, stop=False, skip_group_check=True)
                    pe.matmul(o, hh, wl, start=False, stop=False, skip_group_check=True)
                    mm = pe.matmul(o, hl, wh, start=False, stop=last, skip_group_check=True)
                mm.then_inc(down_ok, 1)

            def residual(it):
                pe.wait_ge(x_in, it * 32 + 32)
                pe.wait_ge(base_ok, it * 2 + 2)
                for u in range(U):
                    for c in range(C):
                        mm = pe.matmul(ps_o[u // 2][:, u % 2, c * P:(c + 1) * P], x_raw[:, c, u * P:(u + 1) * P],
                                       cst[:, C_ID:C_ID + P], start=(u % 2 == 0 and c == 0), stop=False,
                                       skip_group_check=True)
                mm.then_inc(res_ok, 1)

            act_gate(0, 0)
            pe.wait_ge(both_ok, 1)
            flat = both[:, :, :].rearrange("p t e -> p (t e)")
            pe.matmul(ps_r[0][:, :, :].rearrange("p t e -> p (t e)"), cst[:, C_TRI:C_TRI + P], flat, start=True, stop=True)
            pe.matmul(ps_r[1][:, :, :].rearrange("p t e -> p (t e)"), cst[:, C_ONE:C_ONE + P], flat, start=True, stop=True
                      ).then_inc(ranks, 1)

            def step(it, last):
                for i in range(NI):
                    if not (last and i == NI - 1):
                        act_gate(it, i + 1)
                    if i == 0:
                        residual(it)
                    down(it, i)

            with pe.Fori(0, NB - 1) as it:
                step(it, False)
            step(NB - 1, True)


def stage_experts(nc, k):
    with ExitStack() as ctx:
        def sb(name, shape, dt=F32):
            return ctx.enter_context(nc.sbuf_tensor("e_" + name, shape, dt))

        def ps(name, shape, dt=F32):
            return ctx.enter_context(nc.psum_tensor("e_" + name, shape, dt))

        def sem(name):
            return ctx.enter_context(nc.semaphore("e_" + name))

        NP = FFN_PAIRS
        RING = 2 * NP
        NQ = 2 * NP
        STEPS = NT // 2
        U = ES // P
        NI = HR // P
        assert NT == 2 * STEPS + 1
        w_raw = [sb(f"w_raw{i}", [P, CHUNK]) for i in range(RING)]
        w_hi = sb("w_hi", [P, RING, CHUNK], F32R)
        w_lo = sb("w_lo", [P, RING, CHUNK], F32R)
        ident = sb("ident", [P, P])
        b1 = [sb(f"b1_{i}", [P, 2 * NI]) for i in range(2)]
        b2 = [sb(f"b2_{i}", [P, D]) for i in range(2)]
        x_raw = [sb(f"x_raw{i}", [P, U, D]) for i in range(2)]
        x_hi = [sb(f"x_hi{i}", [P, C, ES], F32R) for i in range(2)]
        x_lo = [sb(f"x_lo{i}", [P, C, ES], F32R) for i in range(2)]
        g_act = [sb(f"g_act{i}", [P, 2, ES]) for i in range(2)]
        hid = [sb(f"hid{i}", [P, 2, ES]) for i in range(2)]
        h_hi = [sb(f"h_hi{i}", [P, 2, ES], F32R) for i in range(2)]
        h_lo = [sb(f"h_lo{i}", [P, 2, ES], F32R) for i in range(2)]
        yo = [sb(f"yo{i}", [P, U, D]) for i in range(2)]
        ps_a = [ps(f"ps_a{i}", [P, 2, ES]) for i in range(2)]
        ps_g = [ps(f"ps_g{i}", [P, 2, ES]) for i in range(2)]
        ps_o = [ps(f"ps_o{i}", [P, U, D]) for i in range(2)]
        ps_t = ps("ps_t", [P, C, ES])

        id_in = sem("id_in")
        raw_in = [sem(f"raw_in{i}") for i in range(RING)]
        b_in = [sem(f"b_in{i}") for i in range(2)]
        x_in = [sem(f"x_in{i}") for i in range(2)]
        w_hi_ok = sem("w_hi_ok")
        w_lo_ok = sem("w_lo_ok")
        t_ok = sem("t_ok")
        x_hi_ok = sem("x_hi_ok")
        x_lo_ok = sem("x_lo_ok")
        ag_ok = sem("ag_ok")
        gelu_ok = sem("gelu_ok")
        hid_ok = sem("hid_ok")
        h_hi_ok = sem("h_hi_ok")
        h_lo_ok = sem("h_lo_ok")
        down_ok = sem("down_ok")
        yo_ok = sem("yo_ok")
        yo_free = sem("yo_free")
        y_out = sem("y_out")
        block = ctx.enter_context(nc.Block())
        x_v = k.x_slots.rearrange("(t u p) d -> p t u d", u=U, p=P)
        y_v = k.y_slots.rearrange("(t u p) d -> p t u d", u=U, p=P)

        @block.sync
        def _(sp):
            sp.dma_start(ident[:, :], k.consts[:, C_ID:C_ID + P]).then_inc(id_in, 16)

            def tile(it, half):
                t = it * 2 + half
                static = isinstance(it, int)
                tt = slice(t, t + 1) if static else ds(t, 1)
                e = sp.value_load(k.tile_e[0:1, tt], min_val=0, max_val=E - 1)
                sp.wait_ge(t_ok, t + 1)
                sp.dma_start(x_raw[half][:, :, :], x_v[:, tt, :, :].rearrange("p o u d -> p (o u) d")
                             ).then_inc(x_in[half], 16)
                for j in range(NP):
                    n = half * NP + j
                    sp.wait_ge(w_lo_ok, it * (3 * RING) + 3 * (n + 1))
                    sp.dma_start(w_raw[n][:, :], k.ffn_w[ds(e, 1), j].rearrange("e p n -> (e p) n")
                                 ).then_inc(raw_in[n], 16)

            with sp.Fori(0, STEPS) as it:
                for half in range(2):
                    tile(it, half)
            tile(STEPS, 0)

        @block.gpsimd
        def _(pool):
            pool.sem_inc(yo_free, 2)

            def biases(t, half):
                tt = slice(t, t + 1) if isinstance(t, int) else ds(t, 1)
                e = pool.value_load(k.tile_e[0:1, tt], min_val=0, max_val=E - 1)
                pool.dma_start(b1[half][:, :], k.be1[ds(e, 1)].rearrange("e p n -> (e p) n")).then_inc(b_in[half], 16)
                pool.dma_start(b2[half][:, :], k.be2[ds(e, 1), :].broadcast_to([P, D])).then_inc(b_in[half], 16)

            def store(t, half):
                tt = slice(t, t + 1) if isinstance(t, int) else ds(t, 1)
                pool.dma_start(y_v[:, tt, :, :].rearrange("p o u d -> p (o u) d"), yo[half][:, :, :]).then_inc(y_out, 16)

            def tile(it, half):
                pool.wait_ge(yo_ok, it * 2 + half + 3)
                store(it * 2 + half, half)
                biases(it * 2 + half + 2, half)
                pool.wait_ge(y_out, it * 32 + 16 * half + 16)
                pool.sem_inc(yo_free, 1)

            biases(0, 0)
            biases(1, 1)
            with pool.Fori(0, STEPS - 1) as it:
                for half in range(2):
                    tile(it, half)
            tile(STEPS - 1, 0)
            for t in (NT - 2, NT - 1):
                pool.wait_ge(yo_ok, t + 3)
                store(t, t % 2)
            pool.wait_ge(y_out, 16 * NT)

        @block.scalar
        def _(act):
            def weight_heads(slot, landed):
                act.wait_ge(raw_in[slot], landed)
                for i in range(3):
                    cols = slice(i * PIECE, (i + 1) * PIECE)
                    act.activation(w_hi[:, slot, cols], w_raw[slot][:, cols], ACT.Copy).then_inc(w_hi_ok, 1)

            def x_heads(it, half):
                act.wait_ge(t_ok, it * 2 + half + 3)
                act.activation(x_hi[half % 2][:, :, :], ps_t[:, :, :], ACT.Copy).then_inc(x_hi_ok, 1)

            x_heads(0, 0)
            for n in range(NP):
                weight_heads(n, 16)

            def step(it, last):
                for q in range(NP if last else NQ):
                    half, j = divmod(q, NP)
                    act.wait_ge(ag_ok, it * NQ + q + 1)
                    if j == 0:
                        act.wait_ge(b_in[half], it * 32 + 32)
                    for i in range(2):
                        b = NI + 2 * j + i
                        ins = act.activation(g_act[q % 2][:, i, :], ps_g[q % 2][:, i, :], ACT.Gelu, bias=b1[half][:, b:b + 1])
                    ins.then_inc(gelu_ok, 1)
                    act.wait_ge(hid_ok, it * NQ + q + 3)
                    act.wait_ge(down_ok, it * NQ + q + 1)
                    act.activation(h_hi[q % 2][:, :, :], hid[q % 2][:, :, :], ACT.Copy).then_inc(h_hi_ok, 1)
                    if not last:
                        n = q + NP
                        weight_heads(n % RING, it * 16 + 16 * (1 + n // RING))
                        if j == 1:
                            x_heads(it, half + 1)

            with act.Fori(0, STEPS) as it:
                step(it, False)
            step(STEPS, True)

        @block.vector
        def _(dve):
            dve.sem_inc(w_lo_ok, 3 * RING)
            dve.sem_inc(x_lo_ok, 1)
            dve.sem_inc(hid_ok, 2)
            dve.sem_inc(yo_ok, 2)

            def weight_tails(slot, heads):
                for i in range(3):
                    cols = slice(i * PIECE, (i + 1) * PIECE)
                    dve.wait_ge(w_hi_ok, heads + i + 1)
                    dve.tensor_tensor(w_lo[:, slot, cols], w_raw[slot][:, cols], w_hi[:, slot, cols].bitcast(F32),
                                      ALU.subtract).then_inc(w_lo_ok, 1)

            def x_tails(it, half):
                dve.wait_ge(x_hi_ok, it * 2 + half + 1)
                dve.tensor_tensor(x_lo[half % 2][:, :, :], ps_t[:, :, :], x_hi[half % 2][:, :, :].bitcast(F32),
                                  ALU.subtract).then_inc(x_lo_ok, 1)

            x_tails(0, 0)
            for n in range(NP):
                weight_tails(n, 3 * n)

            def step(it, last):
                for q in range(NP if last else NQ):
                    half, j = divmod(q, NP)
                    dve.wait_ge(gelu_ok, it * NQ + q + 1)
                    if j == 0:
                        dve.wait_ge(b_in[half], it * 32 + 32)
                    for i in range(2):
                        b = 2 * j + i
                        ins = dve.scalar_tensor_tensor(hid[q % 2][:, i, :], ps_a[q % 2][:, i, :], b1[half][:, b:b + 1],
                                                       g_act[q % 2][:, i, :], ALU.add, ALU.mult)
                    ins.then_inc(hid_ok, 1)
                    dve.wait_ge(h_hi_ok, it * NQ + q + 1)
                    dve.tensor_tensor(h_lo[q % 2][:, :, :], hid[q % 2][:, :, :], h_hi[q % 2][:, :, :].bitcast(F32),
                                      ALU.subtract).then_inc(h_lo_ok, 1)
                    if not last:
                        weight_tails((q + NP) % RING, it * (3 * NQ) + 3 * (q + NP))
                        if j == 1:
                            x_tails(it, half + 1)
                    if j == NP - 1:
                        dve.wait_ge(down_ok, it * NQ + q + 3)
                        dve.wait_ge(yo_free, it * 2 + half + 1)
                        dve.tensor_tensor(yo[half][:, :, :], ps_o[half][:, :, :],
                                          b2[half][:, :].unsqueeze(1).broadcast_to([P, U, D]), ALU.add).then_inc(yo_ok, 1)

            with dve.Fori(0, STEPS) as it:
                step(it, False)
            step(STEPS, True)

        @block.tensor
        def _(pe):
            pe.sem_inc(t_ok, 2)
            pe.sem_inc(down_ok, 2)
            pe.wait_ge(id_in, 16)

            def turn(it, half):
                pe.wait_ge(x_in[half % 2], it * 16 + 16 * (1 + half // 2))
                pe.wait_ge(x_lo_ok, it * 2 + half + 1)
                for u in range(U):
                    for c in range(C):
                        mm = pe.transpose(ps_t[:, c, u * P:(u + 1) * P], x_raw[half % 2][:, u, c * P:(c + 1) * P], ident[:, :])
                mm.then_inc(t_ok, 1)

            def gate_up(it, q):
                half, j = divmod(q, NP)
                slot, x = q % NQ, half % 2
                if j == 0:
                    pe.wait_ge(x_lo_ok, it * 2 + half + 2)
                pe.wait_ge(w_lo_ok, it * (3 * NQ) + 3 * (q + 1) + 3 * RING)
                pe.wait_ge(hid_ok, it * NQ + q + 1)
                for dst, off in ((ps_a[q % 2], 0), (ps_g[q % 2], PIECE)):
                    for i in range(2):
                        for c in range(C):
                            cols = slice(off + c * PAIR + i * P, off + c * PAIR + (i + 1) * P)
                            wh, wl = w_hi[:, slot, cols], w_lo[:, slot, cols]
                            pe.matmul(dst[:, i, :], wh, x_hi[x][:, c, :], start=(c == 0), stop=False)
                            pe.matmul(dst[:, i, :], wh, x_lo[x][:, c, :], start=False, stop=False)
                            mm = pe.matmul(dst[:, i, :], wl, x_hi[x][:, c, :], start=False, stop=(c == C - 1))
                mm.then_inc(ag_ok, 1)

            def down(it, q):
                half, j = divmod(q, NP)
                if j == 0:
                    pe.wait_ge(yo_ok, it * 2 + half + 1)
                pe.wait_ge(h_lo_ok, it * NQ + q + 1)
                for u in range(U):
                    tok = slice(u * P, (u + 1) * P)
                    for i in range(2):
                        cols = slice(2 * PIECE + i * D, 2 * PIECE + (i + 1) * D)
                        wh, wl = w_hi[:, q, cols], w_lo[:, q, cols]
                        hh, hl = h_hi[q % 2][:, i, tok], h_lo[q % 2][:, i, tok]
                        o = ps_o[half][:, u, :]
                        pe.matmul(o, hh, wh, start=(j == 0 and u == 0 and i == 0), stop=False, skip_group_check=True)
                        pe.matmul(o, hh, wl, start=False, stop=False, skip_group_check=True)
                        mm = pe.matmul(o, hl, wh, start=False, stop=(j == NP - 1 and i == 1), skip_group_check=True)
                mm.then_inc(down_ok, 1)

            turn(0, 0)
            gate_up(0, 0)

            def step(it, last):
                n = NP if last else NQ
                for q in range(n):
                    if not (last and q == n - 1):
                        gate_up(it, q + 1)
                    down(it, q)
                    if not last and q % NP == 0:
                        turn(it, q // NP + 1)

            with pe.Fori(0, STEPS) as it:
                step(it, False)
            step(STEPS, True)


def stage_combine(nc, k):
    with ExitStack() as ctx:
        def sb(name, shape, dt=F32):
            return ctx.enter_context(nc.sbuf_tensor("f_" + name, shape, dt))

        def sem(name):
            return ctx.enter_context(nc.semaphore("f_" + name))

        got = [sb(f"got{j}", [P, TT, D]) for j in range(2)]
        part = sb("part", [P, TT, D])
        res = sb("res", [P, TT, D])
        base = sb("base", [P, TT, D])
        base_in = sem("base_in")
        landed = [sem(f"landed{n}") for n in range(TT)]
        part_ok = sem("part_ok")
        res_ok = sem("res_ok")
        stored = sem("stored")
        block = ctx.enter_context(nc.Block())

        @block.gpsimd
        def _(pool):
            for n in range(TT):
                for j in range(2):
                    pool.indirect_dma_start(out=got[j][:, n, :], out_offset=None, in_=k.y_slots,
                                            in_offset=bass.IndirectOffsetOnAxis(ap=k.pos[j][:, n:n + 1], axis=0)
                                            ).then_inc(landed[n], 16)

        @block.vector
        def _(dve):
            dve.wait_ge(base_in, 16)
            for n in range(TT):
                dve.wait_ge(landed[n], 32)
                dve.scalar_tensor_tensor(part[:, n, :], got[0][:, n, :], k.gate[0][:, n:n + 1], base[:, n, :],
                                         ALU.mult, ALU.add).then_inc(part_ok, 1)
                dve.wait_ge(part_ok, n + 1)
                dve.scalar_tensor_tensor(res[:, n, :], got[1][:, n, :], k.gate[1][:, n:n + 1], part[:, n, :],
                                         ALU.mult, ALU.add).then_inc(res_ok, 1)

        @block.sync
        def _(sp):
            o_v = k.out.rearrange("(t p) d -> p t d", p=P)
            sp.dma_start(base[:, :, :], k.base.rearrange("(t p) d -> p t d", p=P)).then_inc(base_in, 16)
            with sp.Fori(0, TT // 2) as n:
                sp.wait_ge(res_ok, n * 2 + 2)
                sp.dma_start(o_v[:, ds(n * 2, 2), :], res[:, ds(n * 2, 2), :]).then_inc(stored, 16)
            sp.wait_ge(stored, 16 * (TT // 2))


def program(nc, ins, out):
    k = Chip(ins, out)

    def dram(name, shape):
        return nc.dram_tensor(name, shape, F32, kind="Internal").ap()

    k.x_slots = dram("x_slots", (SLOTS, D))
    k.y_slots = dram("y_slots", (SLOTS, D))
    k.base = dram("base", (T, D))
    with ExitStack() as ctx:
        def sb(name, shape, dt=F32):
            return ctx.enter_context(nc.sbuf_tensor(name, shape, dt))

        k.pos = [sb(f"pos{j}", [P, TT], U32) for j in range(2)]
        k.gate = [sb(f"gate{j}", [P, TT]) for j in range(2)]
        k.tile_e = sb("tile_e", [P, NT], I32)
        with ExitStack() as inner:
            def sb(name, shape, dt=F32):
                return inner.enter_context(nc.sbuf_tensor(name, shape, dt))

            k.vec_sb = sb("vec_sb", [P, V_W])
            k.rows_sb = sb("rows_sb", [P, R_W])
            k.head_sb = sb("head_sb", [P, C_HEAD])
            k.attn_raw = sb("attn_raw", [P, W_W])
            k.c_sb = sb("c_sb", [P, B, C, S])
            stage_cond(nc, k)
            k.cst = sb("cst", [P, C_W])
            k.x2 = sb("x2", [P, C, B, S])
            k.lora_hi = sb("lora_hi", [P, W_W - W_B], F32R)
            k.lora_lo = sb("lora_lo", [P, W_W - W_B], F32R)
            k.sh_hi = sb("sh_hi", [P, 2, CHUNK], F32R)
            k.sh_lo = sb("sh_lo", [P, 2, CHUNK], F32R)
            stage_attention(nc, k)
            k.y_nat = sb("y_nat", [P, TT, D])
            k.y_hi = sb("y_hi", [P, C, T], F32R)
            k.y_lo = sb("y_lo", [P, C, T], F32R)
            k.dif = sb("dif", [P, TT])
            k.one_hot = [sb(f"one_hot{i}", [P, TT, E]) for i in range(2)]
            stage_lora(nc, k)
            stage_route(nc, k)
        stage_experts(nc, k)
        stage_combine(nc, k)


def constants():
    a = np.zeros((P, C_W), np.float32)
    a[:, C_ID:C_ID + P] = np.eye(P)
    theta = np.pi / 2 * np.arange(1, B + 1) / B
    ang = np.sin(theta)[:, None] * np.sin(theta)[None] + np.cos(theta)[:, None] * np.cos(theta)[None]
    a[:, C_MASK:C_MASK + P] = np.kron(ang, np.eye(GRP))
    a[:, C_TRI:C_TRI + P] = np.triu(np.ones((P, P)), 1)
    a[:, C_ONE:C_ONE + P] = 1
    a[:, C_SEG:C_SEG + TT * E] = np.tile(np.arange(TT) != 0, E)
    a[:, C_IOTA:C_IOTA + E] = np.arange(E)
    a[:, C_HEADS:C_HEAD] = np.arange(P)[:, None] // HD == np.arange(P // HD)
    a[:, C_J256:C_J256 + E * 8] = np.tile(np.arange(8) * ES, E)
    a[:, C_TILE:C_TILE + NT * E] = np.repeat(np.arange(NT), E)
    return a


def halves(w):
    return w.reshape(C, P, -1).transpose(1, 0, 2)


def packed(**i):
    f = {n: np.asarray(v) for n, v in i.items()}
    cat = lambda *a: np.concatenate([x.reshape(P, -1) for x in a], axis=1)

    def mlp(gate, up, down, pairs):
        out = []
        for j in range(pairs):
            cols = slice(j * PAIR, (j + 1) * PAIR)
            out.append(cat(halves(gate[:, cols]), halves(up[:, cols]), halves(down[cols])))
        return np.stack(out)

    g, u, d = (f["L0_cond_skill_" + n] for n in ("gate", "up", "down"))
    cond = [mlp(g[e], u[e], d[e], COND_PAIRS) for e in range(COND_E)]
    cond.append(mlp(f["L0_cond_shared_gate"], f["L0_cond_shared_up"], f["L0_cond_shared_down"], COND_PAIRS))
    w1, w2 = f["L0_ffn_We1"], f["L0_ffn_We2"]
    col = lambda v: v.reshape(-1, P).T
    qkv_b, bs1, be1 = f["L0_attn_in_proj_bias"], f["L0_ffn_bs1"], f["L0_ffn_be1"]
    bs = f["L0_cond2_Bs"].transpose(0, 2, 1).reshape(P, D)
    rows = np.concatenate([qkv_b[2 * D:], f["L0_ffn_bs2"], f["L0_ffn_br"]])
    arrays = {
        "xT": halves(f["x"].reshape(T, D).T),
        "cond_8": f["cond_8"],
        "cond_w": np.stack(cond),
        "ffn_w": np.stack([mlp(w1[e][:, :HR], w1[e][:, HR:], w2[e], FFN_PAIRS) for e in range(E)]),
        "shared_w": mlp(f["L0_ffn_Ws1"][:, :HS], f["L0_ffn_Ws1"][:, HS:], f["L0_ffn_Ws2"], HS // PAIR),
        "attn_w": cat(halves(f["L0_attn_in_proj_weight"].T), halves(f["L0_attn_out_w"].T),
                      halves(f["L0_cond2_W_base"].T), halves(f["L0_cond2_As"].reshape(P, D).T), bs),
        "vec": cat(col(qkv_b[:D]), col(qkv_b[D:2 * D]), col(f["L0_attn_out_b"]), col(f["L0_cond2_b_base"]),
                   col(bs1[:HS]), col(bs1[HS:])),
        "rows": np.broadcast_to(rows, (P, R_W)),
        "router": halves(f["L0_ffn_Wr"]),
        "lora_w": np.repeat(f["cond_8"].T, LR, axis=0),
        "be1": be1.reshape(E, 2 * HR // P, P).transpose(0, 2, 1),
        "be2": f["L0_ffn_be2"],
        "consts": constants(),
    }
    return {n: np.ascontiguousarray(a) for n, a in arrays.items()}


def kernel(**inputs):
    import concourse.bacc as _bacc
    from concourse.bass_utils import run_bass_kernel_spmd as _run

    nc = _bacc.Bacc("TRN2", target_bir_lowering=False, num_devices=1)
    arrays = packed(**inputs)
    ins = {n: nc.dram_tensor("in_" + n, a.shape, F32, kind="ExternalInput").ap() for n, a in arrays.items()}
    out = nc.dram_tensor("out", (T, D), F32, kind="ExternalOutput").ap()
    program(nc, ins, out)
    r = _run(nc, [{"in_" + n: a for n, a in arrays.items()}], core_ids=[0])
    return r.results[0]["out"].reshape(B, S, D)
```

```python
from contextlib import ExitStack

import numpy as np

import concourse.bass as bass
from concourse import mybir

F32 = mybir.dt.float32
F32R = mybir.dt.float32r
I32 = mybir.dt.int32
U32 = mybir.dt.uint32
ALU = mybir.AluOpType
ACT = mybir.ActivationFunctionType
AX_X = mybir.AxisListType.X
ds = bass.ds

P = 128
B, S, D = 8, 256, 256
T = B * S
C = D // P
TT = T // P
COND_E, COND_I, COND_K = 8, 1024, 2
PAIR = 2 * P
PIECE = C * PAIR
CHUNK = 3 * PIECE
B1 = 2 * PAIR // P
COND_PAIRS = COND_I // PAIR
MLPS = 1 + COND_K
H, HD = 16, 16
EPS = 1e-3
SG = 4
SGP = S // SG
GRP = 16
NG = SGP // GRP
SGT = SGP * B
LR = 16
LORA_SCALE = 2.0
E, HS, HR = 12, 512, 768
TAU = 1.5
ES = 256
NT = (2 * T + E * (ES - 1)) // ES
SLOTS = NT * ES
FFN_PAIRS = HR // PAIR
BLK = 512
NB = T // BLK

C_ID, C_MASK, C_HEADS = 0, P, 2 * P
C_PAD = C_HEADS + P // HD
C_HEAD = C_PAD + ES // P
C_TRI = C_HEAD
C_ONE = C_TRI + P
C_SEG = C_ONE + P
C_IOTA = C_SEG + TT * E
C_J256 = C_IOTA + E
C_TILE = C_J256 + E * 8
C_TOK = C_TILE + NT * E
C_W = C_TOK + TT

S_W, S_ROW, S_N = D, D + 1, D + 2

V_BQ, V_BK, V_OB, V_BB, V_BA, V_BG, V_W = 0, 2, 4, 6, 8, 12, 16
R_BV, R_BS2, R_BR, R_W = 0, D, 2 * D, 2 * D + E
W_QKV, W_O, W_B, W_A, W_L, W_W = 0, 1536, 2048, 2560, 2816, 3072


class Chip:

    def __init__(self, ins, out):
        self.xT = ins["xT"]
        self.cond_8 = ins["cond_8"]
        self.cond_w = ins["cond_w"]
        self.ffn_w = ins["ffn_w"]
        self.shared_w = ins["shared_w"]
        self.attn_w = ins["attn_w"]
        self.vec = ins["vec"]
        self.rows = ins["rows"]
        self.router = ins["router"]
        self.lora_w = ins["lora_w"]
        self.be2 = ins["be2"]
        self.consts = ins["consts"]
        self.out = out


def span(start, n):
    return slice(start, start + n) if isinstance(start, int) else ds(start, n)


def three(pe, o, sh, sl, mh, ml, first, last):
    pe.matmul(o, sh, mh, start=first, stop=False)
    pe.matmul(o, sh, ml, start=False, stop=False)
    return pe.matmul(o, sl, mh, start=False, stop=last)


def stage_cond(nc, k):
    with ExitStack() as ctx:
        def sb(name, shape, dt=F32):
            return ctx.enter_context(nc.sbuf_tensor("a_" + name, shape, dt))

        def ps(name, shape, dt=F32):
            return ctx.enter_context(nc.psum_tensor("a_" + name, shape, dt))

        def sem(name):
            return ctx.enter_context(nc.semaphore("a_" + name))

        RING = 4
        NQ = 2 * MLPS * COND_PAIRS
        BQ = NQ // 2
        XP = COND_PAIRS * COND_K
        STEPS = B // 2

        cond = sb("cond", [B, COND_E])
        neg_top = sb("neg_top", [B, 1])
        ex = sb("ex", [B, COND_E])
        ex_sum = sb("ex_sum", [B, 1])
        ex_rec = sb("ex_rec", [B, 1])
        prob = sb("prob", [B, COND_E])
        top = sb("top", [B, 8])
        top_i = sb("top_i", [B, 8], U32)
        pair_sum = sb("pair_sum", [B, 1])
        pair_rec = sb("pair_rec", [B, 1])
        wk = sb("wk", [B, COND_K])
        wk1 = sb("wk1", [B, COND_K])
        wk3 = sb("wk3", [B, MLPS])
        w_row = sb("w_row", [1, B * MLPS])
        i_row = sb("i_row", [1, B * COND_K], U32)
        w_col = sb("w_col", [P, B * MLPS])

        w_raw = [sb(f"w_raw{i}", [P, CHUNK]) for i in range(RING)]
        w_hi = sb("w_hi", [P, RING + COND_PAIRS, CHUNK], F32R)
        w_lo = sb("w_lo", [P, RING + COND_PAIRS, CHUNK], F32R)
        x_raw = [sb(f"x_raw{i}", [P, C, S]) for i in range(2)]
        x_hi = [sb(f"x_hi{i}", [P, C, S], F32R) for i in range(2)]
        x_lo = [sb(f"x_lo{i}", [P, C, S], F32R) for i in range(2)]
        g_act = [sb(f"g_act{i}", [P, 2 * S]) for i in range(2)]
        hid = [sb(f"hid{i}", [P, 2 * S]) for i in range(2)]
        h_hi = [sb(f"h_hi{i}", [P, 2 * S], F32R) for i in range(2)]
        h_lo = [sb(f"h_lo{i}", [P, 2 * S], F32R) for i in range(2)]

        ps_g = [ps(f"ps_g{i}", [P, 2 * S]) for i in range(2)]
        ps_u = [ps(f"ps_u{i}", [P, 2 * S]) for i in range(2)]
        ps_d = [ps(f"ps_d{i}", [P, C, S]) for i in range(2)]
        ps_w = ps("ps_w", [P, 512])

        cond_in = sem("cond_in")
        ones_in = sem("ones_in")
        route = sem("route")
        exped = sem("exped")
        rows_in = sem("rows_in")
        w_bc = sem("w_bc")
        w_col_ok = sem("w_col_ok")
        raw_in = [sem(f"raw_in{i}") for i in range(RING)]
        x_in = [sem(f"x_in{i}") for i in range(2)]
        w_hi_ok = sem("w_hi_ok")
        w_lo_ok = sem("w_lo_ok")
        x_hi_ok = sem("x_hi_ok")
        x_lo_ok = sem("x_lo_ok")
        gu_ok = sem("gu_ok")
        gelu_ok = sem("gelu_ok")
        hid_ok = sem("hid_ok")
        h_hi_ok = sem("h_hi_ok")
        h_lo_ok = sem("h_lo_ok")
        down_ok = sem("down_ok")
        c_ok = sem("c_ok")
        par_in = sem("par_in")
        head_in = sem("head_in")
        empty = sem("empty")
        x_out = sem("x_out")

        ident1 = sb("ident1", [1, P])
        U = ES // P
        slots = sb("slots", [P, U, S_N])

        block = ctx.enter_context(nc.Block())

        @block.sync
        def _(sp):
            sp.dma_start(cond[:, :], k.cond_8).then_inc(cond_in, 16)
            sp.dma_start(ident1[:, :], k.consts[0:1, C_ONE:C_ONE + P]).then_inc(ones_in, 16)
            def shared(m):
                sp.dma_start(w_raw[m][:, :], k.cond_w[COND_E, m]).then_inc(raw_in[m], 16)

            def first_x(b):
                sp.dma_start(x_raw[b][:, :, :], k.xT[:, :, b * S:(b + 1) * S]).then_inc(x_in[b], 16)

            shared(0)
            first_x(0)
            shared(1)
            shared(2)
            sp.wait_ge(rows_in, 32)
            shared(3)
            first_x(1)
            sp.dma_start(k.head_sb[:, :], k.consts[:, 0:C_HEAD]).then_inc(head_in, 16)

            def batch(it, half):
                for n in range(XP):
                    e = expert[n // COND_PAIRS]
                    at = half * XP + n
                    sp.wait_ge(w_lo_ok, it * (6 * XP) + 3 * (at + 1))
                    sp.dma_start(w_raw[n % RING][:, :], k.cond_w[ds(e, 1), n % COND_PAIRS].rearrange("e p n -> (e p) n")
                                 ).then_inc(raw_in[n % RING], 16)

            def next_x(b, half):
                sp.wait_ge(x_lo_ok, b - 1)
                sp.dma_start(x_raw[half][:, :, :], k.xT[:, :, ds(b * S, S)]).then_inc(x_in[half], 16)

            with sp.Fori(0, STEPS - 1) as it:
                for half in range(2):
                    expert = [sp.value_load(i_row[0:1, ds(it * 4 + half * 2 + j, 1)], min_val=0, max_val=COND_E - 1)
                              for j in range(COND_K)]
                    batch(it, half)
                    next_x(it * 2 + half + 2, half)
            sp.dma_start(k.attn_raw[:, :], k.attn_w).then_inc(par_in, 16)
            sp.dma_start(k.vec_sb[:, :], k.vec).then_inc(par_in, 16)
            sp.dma_start(k.rows_sb[:, :], k.rows).then_inc(par_in, 16)
            for half in range(2):
                b = 2 * (STEPS - 1) + half
                expert = [sp.value_load(i_row[0:1, 2 * b + j:2 * b + j + 1], min_val=0, max_val=COND_E - 1)
                          for j in range(COND_K)]
                batch(STEPS - 1, half)
            sp.wait_ge(par_in, 48)

        @block.gpsimd
        def _(pool):
            pool.wait_ge(route, 12)
            pool.dma_start(w_row[0:1, :].rearrange("o (b m) -> o b m", b=B), wk3[:, :]).then_inc(rows_in, 16)
            pool.dma_start(i_row[0:1, :].rearrange("o (b m) -> o b m", b=B), top_i[:, 0:COND_K]).then_inc(rows_in, 16)
            pool.wait_ge(down_ok, BQ)
            pool.memset(slots[:, :, 0:S_ROW], 0.0).then_inc(empty, 1)
            pool.wait_ge(head_in, 16)
            pool.tensor_copy(slots[:, :, S_ROW:S_N].bitcast(U32), k.head_sb[:, C_PAD:C_HEAD].unsqueeze(2)
                             ).then_inc(empty, 1)
            pool.wait_ge(empty, 2)
            x_v = k.x_slots.rearrange("(t u p) d -> p t u d", u=U, p=P)
            with pool.Fori(0, NT) as t:
                pool.dma_start(x_v[:, ds(t, 1), :, :].rearrange("p o u d -> p (o u) d"), slots[:, :, :]
                               ).then_inc(x_out, 16)
            pool.dma_start(k.out[T:T + ES, :].rearrange("(u p) d -> p u d", p=P), slots[:, :, 0:D]).then_inc(x_out, 16)
            pool.wait_ge(x_out, 16 * NT + 16)

        @block.scalar
        def _(act):
            act.wait_ge(route, 1)
            act.wait_ge(cond_in, 16)
            act.activation(ex[:, :], cond[:, :], ACT.Exp, bias=neg_top[:, 0:1], accum_out=ex_sum[:, 0:1]).then_inc(exped, 1)

            def weight_heads(slot, raw, landed):
                act.wait_ge(raw_in[raw], landed)
                for i in range(3):
                    act.activation(w_hi[:, slot, i * PIECE:(i + 1) * PIECE],
                                   w_raw[raw][:, i * PIECE:(i + 1) * PIECE], ACT.Copy).then_inc(w_hi_ok, 1)

            def x_heads(half, landed):
                act.wait_ge(x_in[half], landed)
                act.activation(x_hi[half][:, :, :], x_raw[half][:, :, :], ACT.Copy).then_inc(x_hi_ok, 1)

            def hidden(it, q):
                act.wait_ge(gu_ok, it * NQ + q + 1)
                act.activation(g_act[q % 2][:, :], ps_g[q % 2][:, :], ACT.Gelu_apprx_tanh).then_inc(gelu_ok, 1)
                act.wait_ge(hid_ok, it * NQ + q + 3)
                act.wait_ge(down_ok, it * NQ + q + 1)
                act.activation(h_hi[q % 2][:, :], hid[q % 2][:, :], ACT.Copy).then_inc(h_hi_ok, 1)

            weight_heads(RING, 0, 16)
            x_heads(0, 16)
            weight_heads(RING + 1, 1, 16)
            hidden(0, 0)
            for m in range(2, COND_PAIRS):
                weight_heads(RING + m, m, 16)

            def step(it, last):
                for q in range(NQ):
                    half, ql = divmod(q, BQ)
                    n = ql - 1
                    if 0 <= n < XP:
                        if n >= RING:
                            act.wait_ge(down_ok, it * NQ + half * BQ + n + 3)
                        weight_heads(n % RING, n % RING, it * (2 * XP // RING * 16) + 16 * (half * XP // RING + n // RING + 2))
                    if ql == BQ - 2 and not (last and half == 1):
                        x_heads(1 - half, it * 16 + 16 * (1 + half))
                    if not (last and q == NQ - 1):
                        hidden(it, q + 1)

            with act.Fori(0, STEPS - 1) as it:
                step(it, False)
            step(STEPS - 1, True)

        @block.vector
        def _(dve):
            done = [0]

            def then(ins):
                done[0] += 1
                ins.then_inc(route, 1)
                dve.wait_ge(route, done[0])

            dve.sem_inc(hid_ok, 2)
            dve.sem_inc(c_ok, 2)
            dve.wait_ge(cond_in, 16)
            then(dve.tensor_reduce(neg_top[:, :], cond[:, :], AX_X, ALU.max, negate=True))
            dve.wait_ge(exped, 1)
            then(dve.reciprocal(ex_rec[:, :], ex_sum[:, :]))
            then(dve.tensor_scalar(prob[:, :], ex[:, :], ex_rec[:, 0:1], None, ALU.mult))
            then(dve.max(top[:, :], prob[:, :]))
            then(dve.max_index(top_i[:, :], top[:, :], prob[:, :]))
            then(dve.tensor_tensor(pair_sum[:, :], top[:, 0:1], top[:, 1:2], ALU.add))
            then(dve.reciprocal(pair_rec[:, :], pair_sum[:, :]))
            then(dve.tensor_scalar(wk[:, :], top[:, 0:COND_K], pair_rec[:, 0:1], None, ALU.mult))
            then(dve.tensor_scalar(wk1[:, :], wk[:, :], 1.0 / 12, None, ALU.mult))
            then(dve.tensor_scalar(wk[:, :], wk[:, :], 1.0 - 1.0 / 12, None, ALU.mult))
            then(dve.memset(wk3[:, 0:1], 1.0))
            then(dve.tensor_tensor(wk3[:, 1:MLPS], wk1[:, :], wk[:, :], ALU.add))
            def weight_tails(slot, raw, heads):
                for i in range(3):
                    dve.wait_ge(w_hi_ok, heads + i + 1)
                    cols = slice(i * PIECE, (i + 1) * PIECE)
                    dve.tensor_tensor(w_lo[:, slot, cols], w_raw[raw][:, cols], w_hi[:, slot, cols].bitcast(F32),
                                      ALU.subtract).then_inc(w_lo_ok, 1)

            def x_tails(half, b):
                dve.wait_ge(x_hi_ok, b + 1)
                dve.tensor_tensor(x_lo[half][:, :, :], x_raw[half][:, :, :], x_hi[half][:, :, :].bitcast(F32),
                                  ALU.subtract).then_inc(x_lo_ok, 1)

            def hidden(it, q):
                half, ql = divmod(q, BQ)
                dve.wait_ge(gelu_ok, it * NQ + q + 1)
                w = w_col[:, span(it * (2 * MLPS) + half * MLPS + ql // COND_PAIRS, 1)]
                dve.scalar_tensor_tensor(hid[q % 2][:, :], ps_u[q % 2][:, :], w, g_act[q % 2][:, :],
                                         ALU.mult, ALU.mult).then_inc(hid_ok, 1)
                dve.wait_ge(h_hi_ok, it * NQ + q + 1)
                dve.tensor_tensor(h_lo[q % 2][:, :], hid[q % 2][:, :], h_hi[q % 2][:, :].bitcast(F32),
                                  ALU.subtract).then_inc(h_lo_ok, 1)

            weight_tails(RING, 0, 0)
            x_tails(0, 0)
            weight_tails(RING + 1, 1, 3)
            dve.wait_ge(w_bc, 1)
            dve.tensor_copy(w_col[:, :], ps_w[:, 0:B * MLPS]).then_inc(w_col_ok, 1)
            dve.wait_ge(w_col_ok, 1)
            hidden(0, 0)
            for m in range(2, COND_PAIRS):
                weight_tails(RING + m, m, 3 * m)

            def step(it, last):
                for q in range(NQ):
                    half, ql = divmod(q, BQ)
                    n = ql - 1
                    if 0 <= n < XP:
                        weight_tails(n % RING, n % RING, it * (6 * XP) + 3 * (COND_PAIRS + half * XP + n))
                    if ql == BQ - 2 and not (last and half == 1):
                        x_tails(1 - half, it * 2 + half + 1)
                    if ql == BQ - 1:
                        b = it * 2 + half
                        dve.wait_ge(down_ok, it * NQ + q + 3)
                        out = k.c_sb[:, b, :, :] if last else k.c_sb[:, ds(b, 1), :, :].rearrange("p o c s -> p (o c) s")
                        dve.tensor_copy(out, ps_d[half][:, :, :]).then_inc(c_ok, 1)
                    if not (last and q == NQ - 1):
                        hidden(it, q + 1)

            with dve.Fori(0, STEPS - 1) as it:
                step(it, False)
            step(STEPS - 1, True)

        @block.tensor
        def _(pe):
            pe.sem_inc(down_ok, 2)

            def gate_up(it, q):
                half, ql = divmod(q % NQ, BQ)
                if ql == 0:
                    pe.wait_ge(x_lo_ok, it * 2 + q // BQ + 1)
                if ql >= COND_PAIRS:
                    n = ql - COND_PAIRS
                    slot = n % RING
                    pe.wait_ge(w_lo_ok, it * (6 * XP) + 3 * (COND_PAIRS + half * XP + n + 1))
                else:
                    slot = RING + ql
                    pe.wait_ge(w_lo_ok, 3 * (ql + 1))
                pe.wait_ge(hid_ok, it * NQ + q + 1)
                for dst, off in ((ps_g[q % 2], 0), (ps_u[q % 2], PIECE)):
                    for i in range(2):
                        for c in range(C):
                            cols = slice(off + c * PAIR + i * P, off + c * PAIR + (i + 1) * P)
                            wh, wl = w_hi[:, slot, cols], w_lo[:, slot, cols]
                            o = dst[:, i * S:(i + 1) * S]
                            pe.matmul(o, wh, x_hi[half][:, c, :], start=(c == 0), stop=False)
                            pe.matmul(o, wh, x_lo[half][:, c, :], start=False, stop=False)
                            mm = pe.matmul(o, wl, x_hi[half][:, c, :], start=False, stop=(c == C - 1))
                mm.then_inc(gu_ok, 1)

            def down(it, q):
                half, ql = divmod(q, BQ)
                slot = (ql - COND_PAIRS) % RING if ql >= COND_PAIRS else RING + ql
                if ql == 0:
                    pe.wait_ge(c_ok, it * 2 + half + 1)
                pe.wait_ge(h_lo_ok, it * NQ + q + 1)
                for d in range(C):
                    for i in range(2):
                        cols = slice(2 * PIECE + i * D + d * P, 2 * PIECE + i * D + (d + 1) * P)
                        wh, wl = w_hi[:, slot, cols], w_lo[:, slot, cols]
                        hh, hl = h_hi[q % 2][:, i * S:(i + 1) * S], h_lo[q % 2][:, i * S:(i + 1) * S]
                        o = ps_d[half][:, d, :]
                        pe.matmul(o, wh, hh, start=(ql == 0 and d == 0 and i == 0), stop=False, skip_group_check=True)
                        pe.matmul(o, wh, hl, start=False, stop=False, skip_group_check=True)
                        mm = pe.matmul(o, wl, hh, start=False, stop=(ql == BQ - 1 and i == 1), skip_group_check=True)
                mm.then_inc(down_ok, 1)

            gate_up(0, 0)
            pe.wait_ge(ones_in, 16)
            pe.wait_ge(rows_in, 32)
            pe.matmul(ps_w[:, 0:B * MLPS], ident1[0:1, :], w_row[0:1, :], start=True, stop=True).then_inc(w_bc, 1)

            def step(it, last):
                for q in range(NQ):
                    if not (last and q == NQ - 1):
                        gate_up(it, q + 1)
                    down(it, q)

            with pe.Fori(0, STEPS - 1) as it:
                step(it, False)
            step(STEPS - 1, True)


def stage_attention(nc, k):
    with ExitStack() as ctx:
        def sb(name, shape, dt=F32):
            return ctx.enter_context(nc.sbuf_tensor("b_" + name, shape, dt))

        def ps(name, shape, dt=F32):
            return ctx.enter_context(nc.psum_tensor("b_" + name, shape, dt))

        def sem(name):
            return ctx.enter_context(nc.semaphore("b_" + name))

        ROWS = 32
        NJ = P // ROWS
        NS = NG * NJ
        LAG = 3
        assert SG > 2
        WN = W_B
        VW = 2 * ROWS
        PW = (W_W - W_B) // BLK
        SW = CHUNK // BLK
        w_hi = sb("w_hi", [P, WN], F32R)
        w_lo = sb("w_lo", [P, WN], F32R)
        sh_raw = sb("sh_raw", [P, CHUNK])
        c_hi = sb("c_hi", [P, C, SGT], F32R)
        c_lo = sb("c_lo", [P, C, SGT], F32R)
        x_raw = sb("x_raw", [P, C, B, SGP])
        qq = sb("qq", [P, C, SGT])
        qm = [sb(f"qm{i}", [P, C, 2, P]) for i in range(2)]
        kk = sb("kk", [P, C, SGT])
        v_raw = sb("v_raw", [P, NG, H // 2, 2, HD])
        v_hi = sb("v_hi", [P, NG, H // 2, 2, VW], F32R)
        v_lo = sb("v_lo", [P, NG, H // 2, 2, VW], F32R)
        sm = [sb(f"sm{i}", [P, 4, P]) for i in range(4)]
        sm_hi = [sb(f"sm_hi{i}", [P, 4, P], F32R) for i in range(4)]
        sm_lo = [sb(f"sm_lo{i}", [P, 4, P], F32R) for i in range(4)]
        frame = sb("frame", [P, 2, VW])
        num = sb("num", [P, C, P])
        den = sb("den", [P, C, P])
        rec = sb("rec", [P, C, P])
        an = [sb(f"an{i}", [P, C, P]) for i in range(2)]
        at_hi = sb("at_hi", [P, C, SGT], F32R)
        at_lo = sb("at_lo", [P, C, SGT], F32R)
        o_tmp = sb("o_tmp", [P, SGT])

        ps_a = [ps(f"ps_a{i}", [P, SGT]) for i in range(2)]
        ps_s = [ps(f"ps_s{i}", [P, 4 * P]) for i in range(2)]
        ps_o = [ps(f"ps_o{i}", [VW, NJ, C, P]) for i in range(2)]

        cst_in = sem("cst_in")
        sh_in = sem("sh_in")
        x_in = sem("x_in")
        w_hi_ok = sem("w_hi_ok")
        w_lo_ok = sem("w_lo_ok")
        late_hi_ok = sem("late_hi_ok")
        late_lo_ok = sem("late_lo_ok")
        qm_ok = [sem(f"qm{o}_ok") for o in range(2)]
        zero_ok = sem("zero_ok")
        lo_zero_ok = sem("lo_zero_ok")
        ones_ok = sem("ones_ok")
        c_hi_ok = sem("c_hi_ok")
        c_lo_ok = sem("c_lo_ok")
        pj_ok = sem("pj_ok")
        qk_ok = sem("qk_ok")
        v_ok = sem("v_ok")
        v_hi_ok = sem("v_hi_ok")
        v_lo_ok = sem("v_lo_ok")
        s_ok = sem("s_ok")
        m_ok = sem("m_ok")
        sm_hi_ok = sem("sm_hi_ok")
        sm_lo_ok = sem("sm_lo_ok")
        pv_ok = sem("pv_ok")
        den_ok = sem("den_ok")
        num_ok = sem("num_ok")
        rec_ok = sem("rec_ok")
        n_ok = sem("n_ok")
        ahi_ok = sem("ahi_ok")
        alo_ok = sem("alo_ok")
        op_ok = sem("op_ok")
        o_ok = sem("o_ok")
        x2_ok = sem("x2_ok")

        block = ctx.enter_context(nc.Block())

        @block.sync
        def _(sp):
            sp.dma_start(sh_raw[:, :], k.shared_w[0]).then_inc(sh_in, 16)
            sp.dma_start(k.cst[:, :], k.consts).then_inc(cst_in, 16)
            sp.wait_ge(late_lo_ok, PW + SW)
            sp.dma_start(sh_raw[:, :], k.shared_w[1]).then_inc(sh_in, 16)
            x_v = k.xT.rearrange("p c (b s) -> p c b s", b=B)
            with sp.Fori(0, SG) as it:
                sp.wait_ge(x2_ok, it * 2 + 2)
                for c in range(C):
                    sp.dma_start(x_raw[:, c, :, :], x_v[:, c, :, ds(it * SGP, SGP)]).then_inc(x_in, 16)
            sp.wait_ge(cst_in, 16)

        def grouped(ap):
            return ap.rearrange("p b (g s) -> p g b s", g=NG)

        def block_of(it, c):
            return grouped(k.c_sb[:, :, c, span(it * SGP, SGP)])

        def by_group(ap):
            return ap.rearrange("p (g b s) -> p g b s", g=NG, b=B)

        def late_piece(i):
            if i < PW:
                cols = slice(i * BLK, (i + 1) * BLK)
                return k.lora_hi[:, cols], k.lora_lo[:, cols], k.attn_raw[:, W_B + i * BLK:W_B + (i + 1) * BLK]
            j, t = divmod(i - PW, SW)
            cols = slice(t * BLK, (t + 1) * BLK)
            return k.sh_hi[:, j, cols], k.sh_lo[:, j, cols], sh_raw[:, cols]

        LATE = PW + 2 * SW

        def late_of(n):
            if 0 <= n < PW + SW:
                return n
            return n - 4 if PW + SW + 4 <= n < LATE + 4 else None

        def blocks(engine, step):
            step(0, None, False)
            with engine.Fori(1, SG - 1) as it:
                step(it, it - 1, False)
            step(SG - 1, SG - 2, True)

        @block.gpsimd
        def _(pool):
            pool.sem_inc(sm_lo_ok, 4)
            pool.sem_inc(alo_ok, 2)
            pool.wait_ge(zero_ok, 3)
            pool.tensor_scalar(v_lo[:, :, :, :, :].rearrange("p g h o d -> p (g h) (o d)"),
                               frame[:, :, :].rearrange("p o d -> p (o d)").unsqueeze(1).broadcast_to(
                                   [P, NG * H // 2, 2 * VW]), 0.0, None, ALU.mult).then_inc(lo_zero_ok, 1)
            pool.wait_ge(lo_zero_ok, 1)

            def value_tails(it):
                for g in range(NG):
                    pool.wait_ge(v_hi_ok, it * NG + g + 1)
                    for o in range(2):
                        cols = slice(o * HD, (o + 1) * HD)
                        ins = pool.tensor_tensor(v_lo[:, g, :, o, cols], v_raw[:, g, :, o, :],
                                                 v_hi[:, g, :, o, cols].bitcast(F32), ALU.subtract)
                    ins.then_inc(v_lo_ok, 1)

            def attended_tails(it, g):
                pool.wait_ge(ahi_ok, it * NG + g + 1)
                cols = slice(g * P, (g + 1) * P)
                pool.tensor_tensor(at_lo[:, :, cols], an[g % 2][:, :, :], at_hi[:, :, cols].bitcast(F32), ALU.subtract
                                   ).then_inc(alo_ok, 1)

            def step(it, before, last):
                for n in range(NS):
                    pool.wait_ge(sm_hi_ok, it * NS + n + 1)
                    pool.tensor_tensor(sm_lo[n % 4][:, :, :], sm[n % 4][:, :, :], sm_hi[n % 4][:, :, :].bitcast(F32),
                                       ALU.subtract).then_inc(sm_lo_ok, 1)
                    if n == 3 and before is not None:
                        attended_tails(before, NG - 1)
                    if n >= 2 * NJ + LAG and (n - LAG) % NJ == 0:
                        attended_tails(it, (n - LAG) // NJ - 2)
                attended_tails(it, NG - 2)
                if last:
                    attended_tails(it, NG - 1)
                else:
                    value_tails(it + 1)

            value_tails(0)
            blocks(pool, step)

        @block.scalar
        def _(act):
            def c_heads(it):
                for c in range(C):
                    act.activation(by_group(c_hi[:, c, :]), block_of(it, c), ACT.Copy).then_inc(c_hi_ok, 1)

            def masked(it, n):
                g, j = divmod(n, NJ)
                head = C_HEADS + 2 * j
                act.activation(qm[n % 2][:, :, 0, :], qq[:, :, g * P:(g + 1) * P], ACT.Copy,
                               scale=k.head_sb[:, head:head + 1]).then_inc(qm_ok[0], 1)

            def queries_keys(it):
                for e in range(C):
                    act.wait_ge(pj_ok, it * 8 + e + 1)
                    act.wait_ge(s_ok, it * NS + 1)
                    act.wait_ge(qm_ok[1], it * NS + 1)
                    act.activation(qq[:, e, :], ps_a[e][:, :], ACT.Relu, bias=k.vec_sb[:, V_BQ + e:V_BQ + e + 1]
                                   ).then_inc(qk_ok, 1)
                act.wait_ge(qk_ok, it * 4 + 2)
                masked(it, 0)
                masked(it, 1)
                for e in range(C):
                    act.wait_ge(pj_ok, it * 8 + e + 3)
                    act.activation(kk[:, e, :], ps_a[e][:, :], ACT.Relu, bias=k.vec_sb[:, V_BK + e:V_BK + e + 1]
                                   ).then_inc(qk_ok, 1)

            def value_heads(it):
                for g in range(NG):
                    act.wait_ge(v_ok, it * NG + g + 1)
                    for o in range(2):
                        ins = act.activation(v_hi[:, g, :, o, o * HD:(o + 1) * HD], v_raw[:, g, :, o, :], ACT.Copy)
                    ins.then_inc(v_hi_ok, 1)

            def numerators(it, g, half):
                act.wait_ge(pv_ok, it * NS + (g + 1) * NJ + 4)
                act.wait_ge(n_ok, it * NG + g + 1)
                for j in (2 * half, 2 * half + 1):
                    ins = act.activation(num[j * ROWS:(j + 1) * ROWS, :, :],
                                         ps_o[g % 2][0:ROWS, j, :, :], ACT.Copy)
                if half == 1:
                    ins.then_inc(num_ok, 1)

            def attended_heads(it, g):
                act.wait_ge(n_ok, it * NG + g + 2)
                act.activation(at_hi[:, :, g * P:(g + 1) * P], an[g % 2][:, :, :], ACT.Copy).then_inc(ahi_ok, 1)

            def output(it):
                for e in range(C):
                    act.wait_ge(op_ok, it * 2 + e + 1)
                    act.wait_ge(x2_ok, it * 2 + e + 2)
                    act.activation(o_tmp[:, :], ps_a[e][:, :], ACT.Identity, bias=k.vec_sb[:, V_OB + e:V_OB + e + 1]
                                   ).then_inc(o_ok, 1)

            def step(it, before, last):
                for n in range(NS):
                    if n + 2 < NS:
                        act.wait_ge(s_ok, it * NS + n + 2)
                        masked(it, n + 2)
                    act.wait_ge(m_ok, it * NS + n + 3)
                    act.wait_ge(pv_ok, it * NS + n + 1)
                    act.activation(sm_hi[n % 4][:, :, :], sm[n % 4][:, :, :], ACT.Copy).then_inc(sm_hi_ok, 1)
                    if n >= NJ + LAG and (n - LAG) % NJ == 0:
                        if n >= 2 * NJ + LAG:
                            attended_heads(it, (n - LAG) // NJ - 2)
                        numerators(it, (n - LAG) // NJ - 1, 0)
                    if n >= NJ + LAG + 1 and (n - LAG) % NJ == 1:
                        numerators(it, (n - LAG) // NJ - 1, 1)
                    if n < 2 and before is not None:
                        numerators(before, NG - 1, n)
                    if n == 3 and before is not None:
                        attended_heads(before, NG - 1)
                    if n == 7 and before is not None:
                        output(before)
                    if not last and n == 4:
                        act.wait_ge(pj_ok, it * 8 + 8)
                        c_heads(it + 1)
                    i = late_of(n)
                    if before is None and i is not None:
                        if i in (PW, PW + SW):
                            act.wait_ge(sh_in, 16 * ((i - PW) // SW + 1))
                        hi, _, raw = late_piece(i)
                        act.activation(hi, raw, ACT.Copy).then_inc(late_hi_ok, 1)
                numerators(it, NG - 2, 1)
                if not last:
                    queries_keys(it + 1)
                attended_heads(it, NG - 2)
                if last:
                    numerators(it, NG - 1, 0)
                    numerators(it, NG - 1, 1)
                    attended_heads(it, NG - 1)
                    output(it)
                else:
                    value_heads(it + 1)

            c_heads(0)
            for i in range(WN // BLK):
                cols = slice(i * BLK, (i + 1) * BLK)
                act.activation(w_hi[:, cols], k.attn_raw[:, cols], ACT.Copy).then_inc(w_hi_ok, 1)
            queries_keys(0)
            act.wait_ge(ones_ok, 1)
            value_heads(0)
            blocks(act, step)

        @block.vector
        def _(dve):
            dve.sem_inc(m_ok, 2)
            dve.sem_inc(n_ok, 1)
            dve.sem_inc(den_ok, 2)
            dve.sem_inc(x2_ok, 2)
            dve.sem_inc(qm_ok[1], 1)
            mask = k.head_sb[:, C_MASK:C_MASK + P].unsqueeze(1).broadcast_to([P, 4, P])

            def c_tails(it):
                for c in range(C):
                    dve.wait_ge(c_hi_ok, it * 2 + c + 1)
                    dve.tensor_tensor(by_group(c_lo[:, c, :]), block_of(it, c), by_group(c_hi[:, c, :]).bitcast(F32),
                                      ALU.subtract).then_inc(c_lo_ok, 1)

            def masked(it, n):
                g, j = divmod(n, NJ)
                head = C_HEADS + 2 * j + 1
                dve.tensor_scalar(qm[n % 2][:, :, 1, :], qq[:, :, g * P:(g + 1) * P], k.head_sb[:, head:head + 1],
                                  None, ALU.mult).then_inc(qm_ok[1], 1)

            def first_masked(it):
                dve.wait_ge(qk_ok, it * 4 + 2)
                dve.wait_ge(s_ok, it * NS + 1)
                masked(it, 0)
                masked(it, 1)

            def values(it):
                for g in range(NG):
                    dve.wait_ge(pj_ok, it * 8 + g + 5)
                    dve.tensor_tensor(v_raw[:, g, :, :, :].rearrange("p h o d -> p (h o d)"), ps_a[g % 2][:, 0:D],
                                      k.rows_sb[:, R_BV:R_BV + D], ALU.add).then_inc(v_ok, 1)

            def norm(it, g, part):
                if part == 0:
                    dve.wait_ge(pv_ok, it * NS + (g + 1) * NJ + 4)
                if part < 2:
                    for j in (2 * part, 2 * part + 1):
                        ins = dve.tensor_scalar(den[j * ROWS:(j + 1) * ROWS, :, :], ps_o[g % 2][ROWS:VW, j, :, :],
                                                EPS, None, ALU.max)
                    if part == 1:
                        ins.then_inc(den_ok, 1)
                    return
                if part == 2:
                    dve.wait_ge(den_ok, it * NG + g + 3)
                dve.reciprocal(rec[:, part - 2, :], den[:, part - 2, :]).then_inc(rec_ok, 1)
                if part == 3:
                    dve.wait_ge(rec_ok, it * (2 * NG) + 2 * g + 2)
                    dve.wait_ge(num_ok, it * NG + g + 3)
                    dve.wait_ge(alo_ok, it * NG + g + 1)
                    dve.tensor_tensor(an[g % 2][:, :, :], num[:, :, :], rec[:, :, :], ALU.mult).then_inc(n_ok, 1)

            def residual(it):
                dve.wait_ge(x_in, it * 32 + 32)
                for e in range(C):
                    dve.wait_ge(o_ok, it * 2 + e + 3)
                    dve.tensor_tensor(grouped(k.x2[:, e, :, span(it * SGP, SGP)]), by_group(o_tmp[:, :]),
                                      grouped(x_raw[:, e, :, :]), ALU.add).then_inc(x2_ok, 1)

            def step(it, before, last):
                for n in range(NS):
                    dve.wait_ge(s_ok, it * NS + n + 2)
                    dve.wait_ge(sm_lo_ok, it * NS + n + 1)
                    dve.tensor_tensor(sm[n % 4][:, :, :], ps_s[n % 2][:, :].rearrange("p (h t) -> p h t", h=4), mask,
                                      ALU.mult).then_inc(m_ok, 1)
                    if n + 2 < NS:
                        masked(it, n + 2)
                    if n >= NJ + LAG:
                        norm(it, *divmod(n - NJ - LAG, 4))
                    if n < 4 and before is not None:
                        norm(before, NG - 1, n)
                    if n == 8 and before is not None:
                        residual(before)
                    if not last and n == 5:
                        c_tails(it + 1)
                    i = late_of(n - 1)
                    if before is None and i is not None:
                        dve.wait_ge(late_hi_ok, i + 1)
                        hi, lo, raw = late_piece(i)
                        dve.tensor_tensor(lo, raw, hi.bitcast(F32), ALU.subtract).then_inc(late_lo_ok, 1)
                for m in range(NS - NJ - LAG, NS - 4):
                    norm(it, *divmod(m, 4))
                if last:
                    for part in range(4):
                        norm(it, NG - 1, part)
                    residual(it)
                else:
                    first_masked(it + 1)
                    values(it + 1)

            dve.memset(frame[:, :, :], 0.0).then_inc(zero_ok, 1)
            dve.wait_ge(zero_ok, 1)
            for o in range(2):
                dve.memset(frame[:, o, ROWS + o * HD:ROWS + (o + 1) * HD], 1.0).then_inc(zero_ok, 1)
            c_tails(0)
            for i in range(WN // BLK):
                cols = slice(i * BLK, (i + 1) * BLK)
                dve.wait_ge(w_hi_ok, i + 1)
                dve.tensor_tensor(w_lo[:, cols], k.attn_raw[:, cols], w_hi[:, cols].bitcast(F32), ALU.subtract
                                  ).then_inc(w_lo_ok, 1)
            first_masked(0)
            dve.wait_ge(zero_ok, 3)
            dve.tensor_copy(v_hi[:, :, :, :, :].rearrange("p g h o d -> p (g h) (o d)"),
                            frame[:, :, :].rearrange("p o d -> p (o d)").unsqueeze(1).broadcast_to(
                                [P, NG * H // 2, 2 * VW])).then_inc(ones_ok, 1)
            values(0)
            blocks(dve, step)

        @block.tensor
        def _(pe):
            pe.sem_inc(s_ok, 1)
            pe.sem_inc(pv_ok, 4)
            pe.sem_inc(o_ok, 2)
            pe.sem_inc(num_ok, 2)
            def query_key(it, n):
                e, base = n % 2, (n // 2) * D
                if n < 2:
                    if not (isinstance(it, int) and it == 0):
                        pe.wait_ge(o_ok, it * 2 + n - 1)
                else:
                    pe.wait_ge(qk_ok, it * 4 + n - 1)
                for c in range(C):
                    cols = slice(c * 3 * D + base + e * P, c * 3 * D + base + (e + 1) * P)
                    mm = three(pe, ps_a[n % 2][:, :], w_hi[:, cols], w_lo[:, cols], c_hi[:, c, :], c_lo[:, c, :],
                               c == 0, c == C - 1)
                mm.then_inc(pj_ok, 1)

            def value(it, g):
                if g < 2:
                    pe.wait_ge(qk_ok, it * 4 + g + 3)
                else:
                    pe.wait_ge(v_ok, it * NG + g - 1)
                tok = slice(g * P, (g + 1) * P)
                for c in range(C):
                    cols = slice(c * 3 * D + 2 * D, (c + 1) * 3 * D)
                    mm = three(pe, ps_a[g % 2][:, 0:D], c_hi[:, c, tok], c_lo[:, c, tok], w_hi[:, cols], w_lo[:, cols],
                               c == 0, c == C - 1)
                mm.then_inc(pj_ok, 1)

            def scores(it, n):
                g, j = divmod(n, NJ)
                tok = slice(g * P, (g + 1) * P)
                if n == 0:
                    pe.wait_ge(qk_ok, it * 4 + 4)
                pe.wait_ge(qm_ok[0], it * NS + n + 1)
                pe.wait_ge(qm_ok[1], it * NS + n + 2)
                pe.wait_ge(m_ok, it * NS + n + 1)
                for e in range(C):
                    mm = pe.matmul(ps_s[n % 2][:, e * 2 * P:(e + 1) * 2 * P], kk[:, e, tok], qm[n % 2][:, e, :, :],
                                   start=True, stop=True)
                mm.then_inc(s_ok, 1)

            def pv(it, n):
                g, j = divmod(n, NJ)
                if j == 0:
                    pe.wait_ge(num_ok, it * NG + g + 1)
                    pe.wait_ge(den_ok, it * NG + g + 1)
                    pe.wait_ge(v_lo_ok, it * NG + g + 1)
                pe.wait_ge(sm_lo_ok, it * NS + n + 5)
                for e in range(C):
                    for o in range(2):
                        s, pair = 2 * e + o, e * (H // 4) + j
                        out = ps_o[g % 2][:, j, e, :]
                        vh, vl = v_hi[:, g, pair, o, :], v_lo[:, g, pair, o, :]
                        pe.matmul(out, vh, sm_hi[n % 4][:, s, :], start=(j % 2 == 0 and s == 0), stop=False,
                                  skip_group_check=True)
                        pe.matmul(out, vh, sm_lo[n % 4][:, s, :], start=False, stop=False, skip_group_check=True)
                        mm = pe.matmul(out, vl, sm_hi[n % 4][:, s, :], start=False, stop=(o == 1),
                                       skip_group_check=True)
                mm.then_inc(pv_ok, 1)

            def output(it, last):
                pe.wait_ge(alo_ok, it * NG + NG + 2)
                for e in range(C):
                    if not last:
                        pe.wait_ge(v_ok, it * NG + NG + NG - 1 + e)
                    for c in range(C):
                        cols = slice(W_O + c * D + e * P, W_O + c * D + (e + 1) * P)
                        mm = three(pe, ps_a[e][:, :], w_hi[:, cols], w_lo[:, cols], at_hi[:, c, :], at_lo[:, c, :],
                                   c == 0, c == C - 1)
                    mm.then_inc(op_ok, 1)

            def step(it, before, last):
                for n in range(NS):
                    scores(it, n)
                    if n >= LAG:
                        pv(it, n - LAG)
                    if n == 6 and before is not None:
                        output(before, False)
                if not last:
                    pe.wait_ge(c_lo_ok, it * 2 + 4)
                    query_key(it + 1, 0)
                pv(it, NS - 3)
                if not last:
                    query_key(it + 1, 1)
                pv(it, NS - 2)
                pv(it, NS - 1)
                if not last:
                    query_key(it + 1, 2)
                    query_key(it + 1, 3)
                if not last:
                    for g in range(NG):
                        value(it + 1, g)
                else:
                    output(it, True)

            pe.wait_ge(c_lo_ok, 2)
            for n in range(4):
                pe.wait_ge(w_lo_ok, 2 + n // 2)
                query_key(0, n)
            for g in range(NG):
                value(0, g)
            pe.wait_ge(ones_ok, 1)
            pe.wait_ge(w_lo_ok, WN // BLK)
            blocks(pe, step)


def stage_lora(nc, k):
    with ExitStack() as ctx:
        def sb(name, shape, dt=F32):
            return ctx.enter_context(nc.sbuf_tensor("c_" + name, shape, dt))

        def ps(name, shape, dt=F32):
            return ctx.enter_context(nc.psum_tensor("c_" + name, shape, dt))

        def sem(name):
            return ctx.enter_context(nc.semaphore("c_" + name))

        A0, L0 = W_A - W_B, W_L - W_B
        U = BLK // P
        router = sb("router", [P, C, E])
        lora_raw = sb("lora_raw", [P, B])
        lora_w = sb("lora_w", [P, B])
        x_hi = sb("x_hi", [P, C, T], F32R)
        x_lo = sb("x_lo", [P, C, T], F32R)
        ha = sb("ha", [P, BLK])
        ha_hi = sb("ha_hi", [P, BLK], F32R)
        ha_lo = sb("ha_lo", [P, BLK], F32R)
        y = sb("y", [P, C, BLK])
        logit = sb("logit", [P, U, E])
        lt = sb("lt", [P, U, E])
        top = sb("top", [P, U, 8])
        top_i = sb("top_i", [P, U, 8], U32)
        idx = sb("idx", [P, U, 2])
        ps_h = ps("ps_h", [P, BLK])
        ps_y = [ps(f"ps_y{i}", [P, BLK]) for i in range(C)]
        ps_l = ps("ps_l", [P, U, E])
        ps_t = [ps(f"ps_t{i}", [P, 2, D]) for i in range(2)]

        par_in = sem("par_in")
        lw_ok = sem("lw_ok")
        x_hi_ok = sem("x_hi_ok")
        x_lo_ok = sem("x_lo_ok")
        h_ok = sem("h_ok")
        ha_ok = sem("ha_ok")
        ha_hi_ok = sem("ha_hi_ok")
        ha_lo_ok = sem("ha_lo_ok")
        ym_ok = sem("ym_ok")
        y_ok = sem("y_ok")
        y_hi_ok = sem("y_hi_ok")
        y_lo_ok = sem("y_lo_ok")
        lm_ok = sem("lm_ok")
        lg_ok = sem("lg_ok")
        t_ok = sem("t_ok")
        yn_ok = sem("yn_ok")
        yn2_ok = sem("yn2_ok")
        route = sem("route")
        block = ctx.enter_context(nc.Block())

        @block.sync
        def _(sp):
            sp.dma_start(lora_raw[:, :], k.lora_w).then_inc(par_in, 16)
            sp.dma_start(router[:, :, :], k.router).then_inc(par_in, 16)

        def cols_of(it):
            return span(it * BLK, BLK)

        def x2_of(it, c):
            return k.x2[:, c, it * 2:it * 2 + 2, :].rearrange("p b s -> p (b s)")

        @block.gpsimd
        def _(pool):
            pool.sem_inc(y_lo_ok, 2)
            with pool.Fori(0, NB) as it:
                for o in range(C):
                    pool.wait_ge(y_hi_ok, it * 2 + o + 1)
                    cols = ds(it * BLK, BLK)
                    pool.tensor_tensor(k.y_lo[:, o, cols], y[:, o, :], k.y_hi[:, o, cols].bitcast(F32), ALU.subtract
                                       ).then_inc(y_lo_ok, 1)

        @block.scalar
        def _(act):
            def x_heads(it):
                for c in range(C):
                    act.activation(x_hi[:, c, cols_of(it)], x2_of(it, c), ACT.Copy).then_inc(x_hi_ok, 1)

            def hidden_heads(it):
                act.wait_ge(ha_ok, it * 2 + 2)
                act.activation(ha_hi[:, :], ha[:, :], ACT.Copy).then_inc(ha_hi_ok, 1)

            def outputs(it):
                for o in range(C):
                    act.wait_ge(ym_ok, it * 2 + o + 1)
                    act.wait_ge(y_lo_ok, it * 2 + o + 1)
                    act.activation(y[:, o, :], ps_y[o][:, :], ACT.Identity, bias=k.vec_sb[:, V_BB + o:V_BB + o + 1]
                                   ).then_inc(y_ok, 1)
                for o in range(C):
                    act.wait_ge(y_ok, it * 2 + o + 1)
                    act.activation(k.y_hi[:, o, span(it * BLK, BLK)], y[:, o, :], ACT.Copy).then_inc(y_hi_ok, 1)

            def second_copy(it):
                for i in range(2):
                    act.wait_ge(yn_ok, it * 2 + i + 3)
                    tiles = span(it * U + 2 * i, 2)
                    act.activation(k.y_nat[1][:, tiles, 0:D], k.y_nat[0][:, tiles, 0:D], ACT.Copy).then_inc(yn2_ok, 1)

            for n in range(NB - 1):
                x_heads(n)
            hidden_heads(0)
            x_heads(NB - 1)
            with act.Fori(0, NB - 1) as it:
                outputs(it)
                hidden_heads(it + 1)
                second_copy(it)
            outputs(NB - 1)
            second_copy(NB - 1)

        @block.vector
        def _(dve):
            R = 4
            dve.sem_inc(lg_ok, 1)
            dve.sem_inc(yn_ok, 2)

            def x_tails(it):
                for c in range(C):
                    dve.wait_ge(x_hi_ok, it * 2 + c + 1)
                    dve.tensor_tensor(x_lo[:, c, cols_of(it)], x2_of(it, c), x_hi[:, c, cols_of(it)].bitcast(F32),
                                      ALU.subtract).then_inc(x_lo_ok, 1)

            def hidden(it):
                dve.wait_ge(h_ok, it + 1)
                for b in range(2):
                    cols = slice(b * S, (b + 1) * S)
                    dve.tensor_scalar(ha[:, cols], ps_h[:, cols], lora_w[:, span(it * 2 + b, 1)], None, ALU.mult
                                      ).then_inc(ha_ok, 1)
                dve.wait_ge(ha_hi_ok, it + 1)
                dve.tensor_tensor(ha_lo[:, :], ha[:, :], ha_hi[:, :].bitcast(F32), ALU.subtract).then_inc(ha_lo_ok, 1)

            def turned(it):
                for i in range(2):
                    dve.wait_ge(t_ok, it * 2 + i + 1)
                    dve.tensor_copy(k.y_nat[0][:, span(it * U + 2 * i, 2), 0:D], ps_t[i][:, :, :]).then_inc(yn_ok, 1)

            def choices(it):
                tiles = span(it * U, U)
                dve.wait_ge(lm_ok, it + 1)
                dve.tensor_tensor(logit[:, :, :], ps_l[:, :, :],
                                  k.rows_sb[:, R_BR:R_BR + E].unsqueeze(1).broadcast_to([P, U, E]), ALU.add
                                  ).then_inc(route, 1)
                dve.wait_ge(route, it * R + 1)
                dve.tensor_scalar(lt[:, :, :], logit[:, :, :], 1.0 / TAU, None, ALU.mult).then_inc(lg_ok, 1)
                dve.wait_ge(lg_ok, it + 2)
                turned(it)
                for u in range(U):
                    ins = dve.max(top[:, u, :], lt[:, u, :])
                ins.then_inc(route, 1)
                dve.wait_ge(route, it * R + 2)
                dve.tensor_tensor(k.dif[:, tiles], top[:, :, 1], top[:, :, 0], ALU.subtract)
                for u in range(U):
                    ins = dve.max_index(top_i[:, u, :], top[:, u, :], lt[:, u, :])
                ins.then_inc(route, 1)
                dve.wait_ge(route, it * R + 3)
                dve.tensor_copy(idx[:, :, :], top_i[:, :, 0:2]).then_inc(route, 1)
                dve.wait_ge(route, it * R + 4)
                iota = k.cst[:, C_IOTA:C_IOTA + E].unsqueeze(1).broadcast_to([P, U, E])
                for j in range(2):
                    dve.tensor_tensor(k.one_hot[j][:, tiles, :], iota, idx[:, :, j:j + 1].broadcast_to([P, U, E]),
                                      ALU.is_equal)

            x_tails(0)
            dve.wait_ge(par_in, 32)
            dve.tensor_scalar(lora_w[:, :], lora_raw[:, :], LORA_SCALE, None, ALU.mult).then_inc(lw_ok, 1)
            dve.wait_ge(lw_ok, 1)
            x_tails(1)
            hidden(0)
            x_tails(2)
            x_tails(3)
            with dve.Fori(0, NB - 1) as it:
                hidden(it + 1)
                choices(it)
            choices(NB - 1)

        @block.tensor
        def _(pe):
            def base(it):
                for c in range(C):
                    pe.wait_ge(x_lo_ok, it * 2 + c + 1)
                    cols = slice(A0 + c * P, A0 + (c + 1) * P)
                    mm = three(pe, ps_h[:, :], k.lora_hi[:, cols], k.lora_lo[:, cols], x_hi[:, c, cols_of(it)],
                               x_lo[:, c, cols_of(it)], c == 0, c == C - 1)
                mm.then_inc(h_ok, 1)
                for o in range(C):
                    if not (isinstance(it, int) and it == 0):
                        pe.wait_ge(y_ok, it * 2 + o - 1)
                    for c in range(C):
                        cols = slice(c * D + o * P, c * D + (o + 1) * P)
                        three(pe, ps_y[o][:, :], k.lora_hi[:, cols], k.lora_lo[:, cols], x_hi[:, c, cols_of(it)],
                                   x_lo[:, c, cols_of(it)], c == 0, False)

            def lora(it):
                pe.wait_ge(ha_lo_ok, it + 1)
                for o in range(C):
                    cols = slice(L0 + o * P, L0 + (o + 1) * P)
                    three(pe, ps_y[o][:, :], k.lora_hi[:, cols], k.lora_lo[:, cols], ha_hi[:, :], ha_lo[:, :], False,
                          True).then_inc(ym_ok, 1)

            def finish(it):
                pe.wait_ge(y_ok, it * 2 + 2)
                pe.wait_ge(lg_ok, it + 1)
                for u in range(U):
                    for c in range(C):
                        mm = pe.matmul(ps_l[:, u, :], y[:, c, u * P:(u + 1) * P], router[:, c, :],
                                       start=(c == 0), stop=(c == C - 1))
                mm.then_inc(lm_ok, 1)
                for i in range(2):
                    pe.wait_ge(yn_ok, it * 2 + i + 1)
                    for u in range(2):
                        for c in range(C):
                            tok = slice((2 * i + u) * P, (2 * i + u + 1) * P)
                            mm = pe.transpose(ps_t[i][:, u, c * P:(c + 1) * P], y[:, c, tok],
                                              k.head_sb[:, C_ID:C_ID + P])
                    mm.then_inc(t_ok, 1)

            base(0)
            lora(0)
            pe.wait_ge(par_in, 32)
            with pe.Fori(0, NB - 1) as it:
                base(it + 1)
                finish(it)
                lora(it + 1)
            finish(NB - 1)


def stage_route(nc, k):
    with ExitStack() as ctx:
        def sb(name, shape, dt=F32):
            return ctx.enter_context(nc.sbuf_tensor("d_" + name, shape, dt))

        def ps(name, shape, dt=F32):
            return ctx.enter_context(nc.psum_tensor("d_" + name, shape, dt))

        def sem(name):
            return ctx.enter_context(nc.semaphore("d_" + name))

        NI = HS // P
        U = BLK // P
        ITP = 2
        cst, vec, rows, one_hot = k.cst, k.vec_sb, k.rows_sb, k.one_hot
        ex = sb("ex", [P, TT])
        ex1 = sb("ex1", [P, TT])
        both = sb("both", [P, TT, E])
        tot = sb("tot", [P, E, TT])
        inc = sb("inc", [P, E, TT])
        exc = sb("exc", [P, E, TT])
        more = sb("more", [P, E, 8])
        tiles = sb("tiles", [P, E])
        tend = sb("tend", [P, E])
        tbeg = sb("tbeg", [P, E])
        sbase = sb("sbase", [P, E])
        slot = sb("slot", [P, TT, E])
        slot2 = sb("slot2", [P, TT, E])
        mine = [sb(f"mine{i}", [P, TT, E]) for i in range(2)]
        posf = [sb(f"posf{i}", [P, TT]) for i in range(2)]
        past = sb("past", [P, NT, E])
        npast = sb("npast", [P, NT])
        w_hi, w_lo = k.sh_hi, k.sh_lo
        x_raw = sb("x_raw", [P, C, BLK])
        base = [sb(f"base{i}", [P, 2, D]) for i in range(2)]
        gate0 = sb("gate0", [P, TT])
        gate1 = sb("gate1", [P, TT])
        pos = [sb(f"pos{j}", [P, TT], U32) for j in range(2)]
        g_act = [sb(f"g_act{i}", [P, BLK]) for i in range(2)]
        hid = [sb(f"hid{i}", [P, BLK]) for i in range(2)]
        h_hi = [sb(f"h_hi{i}", [P, BLK], F32R) for i in range(2)]
        h_lo = [sb(f"h_lo{i}", [P, BLK], F32R) for i in range(2)]
        ps_a = [ps(f"ps_a{i}", [P, BLK]) for i in range(2)]
        ps_g = [ps(f"ps_g{i}", [P, BLK]) for i in range(2)]
        ps_o = [ps(f"ps_o{i}", [P, 2, D]) for i in range(2)]
        ps_r = [ps(f"ps_r{i}", [P, TT, E]) for i in range(2)]

        x_in = sem("x_in")
        route = sem("route")
        exped = sem("exped")
        ranks = sem("ranks")
        both_ok = sem("both_ok")
        pos_ok = sem("pos_ok")
        moved = sem("moved")
        ag_ok = sem("ag_ok")
        gelu_ok = sem("gelu_ok")
        hid_ok = sem("hid_ok")
        h_hi_ok = sem("h_hi_ok")
        h_lo_ok = sem("h_lo_ok")
        down_ok = sem("down_ok")
        res_ok = sem("res_ok")
        base_ok = sem("base_ok")
        base_out = [sem(f"base_out{i}") for i in range(2)]
        block = ctx.enter_context(nc.Block())

        @block.sync
        def _(sp):
            out_v = k.out[0:T, :].rearrange("(t p) d -> p t d", p=P)

            def load(it):
                for c in range(C):
                    sp.dma_start(x_raw[:, c, :], k.x2[:, c, span(it * 2, 2), :].rearrange("p b s -> p (b s)")
                                 ).then_inc(x_in, 16)

            def store(it):
                for i in range(2):
                    sp.wait_ge(base_ok, it * 2 + i + 3)
                    sp.dma_start(out_v[:, span(it * U + 2 * i, 2), :], base[i][:, :, :]).then_inc(base_out[i], 16)

            for i in range(2):
                sp.sem_inc(base_out[i], 16)
            load(0)
            with sp.Fori(0, NB - 1) as it:
                sp.wait_ge(res_ok, it + 1)
                load(it + 1)
                store(it)
            store(NB - 1)
            for i in range(2):
                sp.wait_ge(base_out[i], 16 * NB + 16)

        @block.gpsimd
        def _(pool):
            pool.wait_ge(pos_ok, 2)
            for n in range(TT):
                for j in range(2):
                    pool.indirect_dma_start(out=k.x_slots, out_offset=bass.IndirectOffsetOnAxis(ap=pos[j][:, n:n + 1], axis=0),
                                            in_=k.y_nat[j][:, n, :], in_offset=None).then_inc(moved, 16)
            pool.wait_ge(moved, 16 * 2 * TT)

        @block.scalar
        def _(act):
            act.activation(ex[:, :], k.dif[:, :], ACT.Exp).then_inc(exped, 1)
            with act.Fori(0, NB) as it:
                for i in range(NI):
                    act.wait_ge(ag_ok, it * NI + i + 1)
                    act.activation(g_act[i % 2][:, :], ps_g[i % 2][:, :], ACT.Gelu, bias=vec[:, V_BG + i:V_BG + i + 1]
                                   ).then_inc(gelu_ok, 1)
                    act.wait_ge(hid_ok, it * NI + i + 3)
                    act.wait_ge(down_ok, it * NI + i + 1)
                    act.activation(h_hi[i % 2][:, :], hid[i % 2][:, :], ACT.Copy).then_inc(h_hi_ok, 1)

        @block.vector
        def _(dve):
            done = [0]

            def then(ins):
                done[0] += 1
                ins.then_inc(route, 1)
                dve.wait_ge(route, done[0])

            dve.sem_inc(hid_ok, 2)
            dve.sem_inc(base_ok, 2)
            dve.tensor_tensor(both[:, :, :], one_hot[0][:, :, :], one_hot[1][:, :, :], ALU.add).then_inc(both_ok, 1)
            dve.wait_ge(exped, 1)
            then(dve.tensor_scalar(ex1[:, :], ex[:, :], 1.0, None, ALU.add))
            then(dve.reciprocal(gate0[:, :], ex1[:, :]))
            then(dve.tensor_tensor(gate1[:, :], ex[:, :], gate0[:, :], ALU.mult))
            for j, gate in enumerate((gate0, gate1)):
                dve.tensor_copy(k.y_nat[j][:, :, S_W:S_ROW], gate[:, :].unsqueeze(2))
                dve.tensor_copy(k.y_nat[j][:, :, S_ROW:S_N].bitcast(U32), cst[:, C_TOK:C_TOK + TT].unsqueeze(2))
            dve.wait_ge(ranks, 1)
            then(dve.tensor_copy(tot[:, :, :], ps_r[1][:, :, :].rearrange("p t e -> p e t")))
            then(dve.tensor_tensor_scan(inc[:, :, :].rearrange("p e t -> p (e t)"), cst[:, C_SEG:C_SEG + TT * E],
                                        tot[:, :, :].rearrange("p e t -> p (e t)"), 0.0, ALU.mult, ALU.add))
            then(dve.tensor_tensor(exc[:, :, :], inc[:, :, :], tot[:, :, :], ALU.subtract))
            then(dve.tensor_tensor(more[:, :, :], inc[:, :, TT - 1:TT].broadcast_to([P, E, 8]),
                                   cst[:, C_J256:C_J256 + E * 8].rearrange("p (e j) -> p e j", e=E), ALU.is_gt))
            then(dve.tensor_reduce(tiles[:, :], more[:, :, :], AX_X, ALU.add))
            then(dve.tensor_tensor_scan(tend[:, :], cst[:, C_ONE:C_ONE + E], tiles[:, :], 0.0, ALU.mult, ALU.add))
            then(dve.tensor_tensor(tbeg[:, :], tend[:, :], tiles[:, :], ALU.subtract))
            then(dve.tensor_scalar(sbase[:, :], tbeg[:, :], float(ES), None, ALU.mult))
            then(dve.tensor_tensor(slot[:, :, :], ps_r[0][:, :, :], exc[:, :, :].rearrange("p e t -> p t e"), ALU.add))
            then(dve.tensor_tensor(slot2[:, :, :], slot[:, :, :], sbase[:, :].unsqueeze(1).broadcast_to([P, TT, E]), ALU.add))
            for j in range(2):
                ins = dve.tensor_tensor(mine[j][:, :, :], one_hot[j][:, :, :], slot2[:, :, :], ALU.mult)
            then(ins)
            for j in range(2):
                ins = dve.tensor_reduce(posf[j][:, :], mine[j][:, :, :], AX_X, ALU.add)
            then(ins)
            for j in range(2):
                dve.tensor_copy(pos[j][:, :], posf[j][:, :]).then_inc(pos_ok, 1)
            then(dve.tensor_tensor(past[:, :, :], tend[:, :].unsqueeze(1).broadcast_to([P, NT, E]),
                                   cst[:, C_TILE:C_TILE + NT * E].rearrange("p (t e) -> p t e", t=NT), ALU.is_le))
            then(dve.tensor_reduce(npast[:, :], past[:, :, :], AX_X, ALU.add))
            then(dve.tensor_scalar(k.tile_e[:, :], npast[:, :], float(E - 1), None, ALU.min))
            with dve.Fori(0, NB) as it:
                for i in range(NI):
                    dve.wait_ge(gelu_ok, it * NI + i + 1)
                    dve.scalar_tensor_tensor(hid[i % 2][:, :], ps_a[i % 2][:, :], vec[:, V_BA + i:V_BA + i + 1],
                                             g_act[i % 2][:, :], ALU.add, ALU.mult).then_inc(hid_ok, 1)
                    dve.wait_ge(h_hi_ok, it * NI + i + 1)
                    dve.tensor_tensor(h_lo[i % 2][:, :], hid[i % 2][:, :], h_hi[i % 2][:, :].bitcast(F32), ALU.subtract
                                      ).then_inc(h_lo_ok, 1)
                dve.wait_ge(down_ok, it * NI + NI + 2)
                for i in range(2):
                    dve.wait_ge(base_out[i], it * 16 + 16)
                    dve.tensor_tensor(base[i][:, :, :], ps_o[i][:, :, :],
                                      rows[:, R_BS2:R_BS2 + D].unsqueeze(1).broadcast_to([P, 2, D]), ALU.add
                                      ).then_inc(base_ok, 1)

        @block.tensor
        def _(pe):
            pe.sem_inc(down_ok, 2)
            def act_gate(it, i):
                j, t = divmod(i, ITP)
                pe.wait_ge(hid_ok, it * NI + i + 1)
                tok = span((it + i // NI) * BLK, BLK)
                i, j = i % NI, j % (NI // ITP)
                for dst, off in ((ps_a[i % 2], 0), (ps_g[i % 2], PIECE)):
                    for c in range(C):
                        cols = slice(off + c * PAIR + t * P, off + c * PAIR + (t + 1) * P)
                        wh, wl = w_hi[:, j, cols], w_lo[:, j, cols]
                        pe.matmul(dst[:, :], wh, k.y_hi[:, c, tok], start=(c == 0), stop=False)
                        pe.matmul(dst[:, :], wh, k.y_lo[:, c, tok], start=False, stop=False)
                        mm = pe.matmul(dst[:, :], wl, k.y_hi[:, c, tok], start=False, stop=(c == C - 1))
                mm.then_inc(ag_ok, 1)

            def down(it, i):
                j, t = divmod(i, ITP)
                pe.wait_ge(h_lo_ok, it * NI + i + 1)
                cols = slice(2 * PIECE + t * D, 2 * PIECE + (t + 1) * D)
                wh, wl = w_hi[:, j, cols], w_lo[:, j, cols]
                for u in range(U):
                    tok = slice(u * P, (u + 1) * P)
                    hh, hl = h_hi[i % 2][:, tok], h_lo[i % 2][:, tok]
                    o = ps_o[u // 2][:, u % 2, :]
                    last = i == NI - 1
                    pe.matmul(o, hh, wh, start=False, stop=False, skip_group_check=True)
                    pe.matmul(o, hh, wl, start=False, stop=False, skip_group_check=True)
                    mm = pe.matmul(o, hl, wh, start=False, stop=last, skip_group_check=True)
                mm.then_inc(down_ok, 1)

            def residual(it):
                pe.wait_ge(x_in, it * 32 + 32)
                pe.wait_ge(base_ok, it * 2 + 2)
                for u in range(U):
                    for c in range(C):
                        mm = pe.matmul(ps_o[u // 2][:, u % 2, c * P:(c + 1) * P], x_raw[:, c, u * P:(u + 1) * P],
                                       cst[:, C_ID:C_ID + P], start=(u % 2 == 0 and c == 0), stop=False,
                                       skip_group_check=True)
                mm.then_inc(res_ok, 1)

            pe.wait_ge(both_ok, 1)
            flat = both[:, :, :].rearrange("p t e -> p (t e)")
            pe.matmul(ps_r[0][:, :, :].rearrange("p t e -> p (t e)"), cst[:, C_TRI:C_TRI + P], flat, start=True, stop=True)
            pe.matmul(ps_r[1][:, :, :].rearrange("p t e -> p (t e)"), cst[:, C_ONE:C_ONE + P], flat, start=True, stop=True
                      ).then_inc(ranks, 1)
            act_gate(0, 0)

            def step(it, last):
                for i in range(NI):
                    if not (last and i == NI - 1):
                        act_gate(it, i + 1)
                    if i == 0:
                        residual(it)
                    down(it, i)

            with pe.Fori(0, NB - 1) as it:
                step(it, False)
            step(NB - 1, True)


def stage_experts(nc, k):
    with ExitStack() as ctx:
        def sb(name, shape, dt=F32):
            return ctx.enter_context(nc.sbuf_tensor("e_" + name, shape, dt))

        def ps(name, shape, dt=F32):
            return ctx.enter_context(nc.psum_tensor("e_" + name, shape, dt))

        def sem(name):
            return ctx.enter_context(nc.semaphore("e_" + name))

        NP = FFN_PAIRS
        RING = 2 * NP
        NQ = 2 * NP
        STEPS = NT // 2
        U = ES // P
        assert NT == 2 * STEPS + 1
        w_raw = [sb(f"w_raw{i}", [P, CHUNK + B1]) for i in range(RING)]
        w_hi = sb("w_hi", [P, RING, CHUNK], F32R)
        w_lo = sb("w_lo", [P, RING, CHUNK], F32R)
        ident = k.head_sb[:, C_ID:C_ID + P]
        b1 = sb("b1", [P, RING, B1])
        b2 = [sb(f"b2_{i}", [P, D]) for i in range(2)]
        x_raw = [sb(f"x_raw{i}", [P, U, S_N]) for i in range(2)]
        wgt = [sb(f"wgt{i}", [P, U]) for i in range(2)]
        row = [sb(f"row{i}", [P, U], U32) for i in range(2)]
        b2w = [sb(f"b2w{i}", [P, U, D]) for i in range(2)]
        x_hi = [sb(f"x_hi{i}", [P, C, ES], F32R) for i in range(2)]
        x_lo = [sb(f"x_lo{i}", [P, C, ES], F32R) for i in range(2)]
        g_act = [sb(f"g_act{i}", [P, 2, ES]) for i in range(2)]
        hid = [sb(f"hid{i}", [P, 2, ES]) for i in range(2)]
        h_hi = [sb(f"h_hi{i}", [P, 2, ES], F32R) for i in range(2)]
        h_lo = [sb(f"h_lo{i}", [P, 2, ES], F32R) for i in range(2)]
        yo = [sb(f"yo{i}", [P, U, D]) for i in range(2)]
        ps_a = [ps(f"ps_a{i}", [P, 2, ES]) for i in range(2)]
        ps_g = [ps(f"ps_g{i}", [P, 2, ES]) for i in range(2)]
        ps_o = [ps(f"ps_o{i}", [P, U, D]) for i in range(2)]
        ps_t = ps("ps_t", [P, C, ES])

        raw_in = [sem(f"raw_in{i}") for i in range(RING)]
        b_in = [sem(f"b_in{i}") for i in range(2)]
        x_in = [sem(f"x_in{i}") for i in range(2)]
        w_hi_ok = sem("w_hi_ok")
        w_lo_ok = sem("w_lo_ok")
        wd_lo_ok = sem("wd_lo_ok")
        t_ok = sem("t_ok")
        x_hi_ok = sem("x_hi_ok")
        x_lo_ok = sem("x_lo_ok")
        meta_ok = sem("meta_ok")
        g_ok = sem("g_ok")
        a_ok = sem("a_ok")
        gelu_ok = sem("gelu_ok")
        hid_ok = sem("hid_ok")
        h_hi_ok = sem("h_hi_ok")
        h_lo_ok = sem("h_lo_ok")
        down_ok = sem("down_ok")
        b2w_ok = sem("b2w_ok")
        yo_ok = sem("yo_ok")
        added = sem("added")
        yo_free = sem("yo_free")
        block = ctx.enter_context(nc.Block())
        x_v = k.x_slots.rearrange("(t u p) d -> p t u d", u=U, p=P)

        def peeled(engine, pair):
            for q in range(NP):
                pair(0, q)
            with engine.Fori(0, STEPS - 1) as it:
                for q in range(NP, NP + NQ):
                    pair(it, q)
            for q in range(NP, NP + NQ):
                pair(STEPS - 1, q)

        def is_last(it, q, tiles=1):
            return isinstance(it, int) and it == STEPS - 1 and q >= NP + NQ - tiles * NP

        def is_first(it, q):
            return isinstance(it, int) and it == 0 and q < NP

        @block.sync
        def _(sp):
            def tile(it, half):
                t = it * 2 + half
                tt = span(t, 1)
                e = sp.value_load(k.tile_e[0:1, tt], min_val=0, max_val=E - 1)
                sp.wait_ge(meta_ok, t + 1)
                sp.dma_start(x_raw[half][:, :, :], x_v[:, tt, :, :].rearrange("p o u d -> p (o u) d")
                             ).then_inc(x_in[half], 16)
                for j in range(NP):
                    n = half * NP + j
                    sp.wait_ge(wd_lo_ok, it * RING + n + 1)
                    sp.dma_start(w_raw[n][:, :], k.ffn_w[ds(e, 1), j].rearrange("e p n -> (e p) n")
                                 ).then_inc(raw_in[n], 16)

            with sp.Fori(0, STEPS) as it:
                for half in range(2):
                    tile(it, half)
            tile(STEPS, 0)

        @block.gpsimd
        def _(pool):
            pool.sem_inc(wd_lo_ok, RING)
            pool.sem_inc(meta_ok, 2)
            pool.sem_inc(yo_free, 2)

            def bias(it, half):
                e = pool.value_load(k.tile_e[0:1, span(it * 2 + half, 1)], min_val=0, max_val=E - 1)
                pool.dma_start(b2[half % 2][:, :], k.be2[ds(e, 1), :].broadcast_to([P, D])
                               ).then_inc(b_in[half % 2], 16)

            def may_take(it, half):
                pool.wait_ge(x_in[half % 2], it * 16 + 16 * (1 + half // 2))
                pool.wait_ge(t_ok, it * 2 + half + 3)

            def take(it, half):
                b = half % 2
                pool.tensor_copy(wgt[b][:, :].unsqueeze(2), x_raw[b][:, :, S_W:S_ROW])
                pool.tensor_copy(row[b][:, :].unsqueeze(2), x_raw[b][:, :, S_ROW:S_N].bitcast(U32)
                                 ).then_inc(meta_ok, 1)

            def may_weight(it, half):
                pool.wait_ge(meta_ok, it * 2 + half + 3)
                pool.wait_ge(b_in[half % 2], it * 16 + 16 * (1 + half // 2))
                pool.wait_ge(yo_ok, it * 2 + half + 1)

            def weighted_bias(it, half):
                b = half % 2
                for u in range(U):
                    ins = pool.tensor_scalar(b2w[b][:, u, :], b2[b][:, :], wgt[b][:, u:u + 1], None, ALU.mult)
                ins.then_inc(b2w_ok, 1)

            def may_add(it, half):
                pool.wait_ge(yo_ok, it * 2 + half + 3)

            def add(it, half):
                b = half % 2
                for u in range(U):
                    pool.indirect_dma_start(out=k.out, out_offset=bass.IndirectOffsetOnAxis(ap=row[b][:, u:u + 1], axis=0),
                                            in_=yo[b][:, u, :], in_offset=None, compute_op=ALU.add).then_inc(added, 16)

            def down_tails(n, it):
                slot, cols = n % RING, slice(2 * PIECE, 3 * PIECE)
                pool.wait_ge(w_hi_ok, it * (3 * NQ) + 3 * n + 3)
                pool.wait_ge(w_lo_ok, it * (2 * NQ) + 2 * (n + 1))
                pool.tensor_tensor(w_lo[:, slot, cols], w_raw[slot][:, cols], w_hi[:, slot, cols].bitcast(F32),
                                   ALU.subtract)
                pool.tensor_copy(b1[:, slot, :], w_raw[slot][:, CHUNK:CHUNK + B1]).then_inc(wd_lo_ok, 1)

            def pair(it, q):
                half, j = divmod(q, NP)
                if j == 0:
                    may_weight(it, half)
                if j == 1 and not is_first(it, q):
                    may_add(it, half - 1)
                if j == 2 and not is_first(it, q):
                    pool.wait_ge(added, it * 64 + half * 32)
                if j == 2 and not is_last(it, q):
                    may_take(it, half + 1)
                if not is_last(it, q):
                    down_tails(q + NP, it)
                if j == 0:
                    weighted_bias(it, half)
                    if not is_last(it, q):
                        if not is_first(it, q):
                            pool.wait_ge(b2w_ok, it * 2 + half)
                        bias(it, half + 1)
                if j == 1 and not is_first(it, q):
                    add(it, half - 1)
                if j == 2 and not is_first(it, q):
                    pool.sem_inc(yo_free, 1)
                if j == 2 and not is_last(it, q):
                    take(it, half + 1)

            bias(0, 0)
            may_take(0, 0)
            take(0, 0)
            for n in range(NP):
                down_tails(n, 0)
            peeled(pool, pair)
            may_add(STEPS, 0)
            add(STEPS, 0)
            pool.wait_ge(added, NT * 32)

        @block.scalar
        def _(act):
            def weight_heads(slot, landed, pieces=range(3)):
                act.wait_ge(raw_in[slot], landed)
                for i in pieces:
                    cols = slice(i * PIECE, (i + 1) * PIECE)
                    act.activation(w_hi[:, slot, cols], w_raw[slot][:, cols], ACT.Copy).then_inc(w_hi_ok, 1)

            def x_heads(it, half):
                act.wait_ge(t_ok, it * 2 + half + 3)
                act.activation(x_hi[half % 2][:, :, :], ps_t[:, :, :], ACT.Copy).then_inc(x_hi_ok, 1)

            def pair(it, q):
                half, j = divmod(q, NP)
                act.wait_ge(g_ok, it * NQ + q + 1)
                act.wait_ge(wd_lo_ok, it * NQ + q + 1 + RING)
                for i in range(2):
                    act.activation(g_act[q % 2][:, i, :], ps_g[q % 2][:, i, :], ACT.Gelu,
                                   bias=b1[:, q % RING, 2 + i:3 + i]).then_inc(gelu_ok, 1)
                if not is_last(it, q):
                    n = q + NP
                    weight_heads(n % RING, it * 16 + 16 * (1 + n // RING), (0,))
                act.wait_ge(down_ok, it * NQ + q + 1)
                for i in range(2):
                    act.wait_ge(hid_ok, it * (2 * NQ) + 2 * q + i + 5)
                    act.activation(h_hi[q % 2][:, i, :], hid[q % 2][:, i, :], ACT.Copy).then_inc(h_hi_ok, 1)
                if not is_last(it, q):
                    if j == 1:
                        x_heads(it, half + 1)
                    weight_heads(n % RING, it * 16 + 16 * (1 + n // RING), (1, 2))

            x_heads(0, 0)
            for n in range(NP):
                weight_heads(n, 16)
            peeled(act, pair)

        @block.vector
        def _(dve):
            dve.sem_inc(x_lo_ok, 1)
            dve.sem_inc(hid_ok, 4)
            dve.sem_inc(yo_ok, 2)

            def weight_tails(n, it):
                slot = n % RING
                for i in range(2):
                    cols = slice(i * PIECE, (i + 1) * PIECE)
                    dve.wait_ge(w_hi_ok, it * (3 * NQ) + 3 * n + i + 1)
                    dve.tensor_tensor(w_lo[:, slot, cols], w_raw[slot][:, cols], w_hi[:, slot, cols].bitcast(F32),
                                      ALU.subtract).then_inc(w_lo_ok, 1)

            def x_tails(it, half):
                dve.wait_ge(x_hi_ok, it * 2 + half + 1)
                dve.tensor_tensor(x_lo[half % 2][:, :, :], ps_t[:, :, :], x_hi[half % 2][:, :, :].bitcast(F32),
                                  ALU.subtract).then_inc(x_lo_ok, 1)

            def copy_out(it, half):
                b = half % 2
                dve.wait_ge(down_ok, it * NQ + (half + 1) * NP + 2)
                dve.wait_ge(b2w_ok, it * 2 + half + 1)
                dve.wait_ge(yo_free, it * 2 + half + 1)
                for u in range(U):
                    ins = dve.scalar_tensor_tensor(yo[b][:, u, :], ps_o[b][:, u, :], wgt[b][:, u:u + 1], b2w[b][:, u, :],
                                                   ALU.mult, ALU.add)
                ins.then_inc(yo_ok, 1)

            def pair(it, q):
                half, j = divmod(q, NP)
                dve.wait_ge(a_ok, it * NQ + q + 1)
                for i in range(2):
                    dve.wait_ge(gelu_ok, it * (2 * NQ) + 2 * q + i + 1)
                    dve.scalar_tensor_tensor(hid[q % 2][:, i, :], ps_a[q % 2][:, i, :], b1[:, q % RING, i:i + 1],
                                             g_act[q % 2][:, i, :], ALU.add, ALU.mult).then_inc(hid_ok, 1)
                for i in range(2):
                    dve.wait_ge(h_hi_ok, it * (2 * NQ) + 2 * q + i + 1)
                    dve.tensor_tensor(h_lo[q % 2][:, i, :], hid[q % 2][:, i, :], h_hi[q % 2][:, i, :].bitcast(F32),
                                      ALU.subtract).then_inc(h_lo_ok, 1)
                if j == 0 and not is_first(it, q):
                    copy_out(it, half - 1)
                if not is_last(it, q):
                    if j == 1:
                        x_tails(it, half + 1)
                    weight_tails(q + NP, it)

            x_tails(0, 0)
            for n in range(NP):
                weight_tails(n, 0)
            peeled(dve, pair)
            copy_out(STEPS, 0)

        @block.tensor
        def _(pe):
            pe.sem_inc(t_ok, 2)
            pe.sem_inc(down_ok, 2)

            def turn(it, half):
                pe.wait_ge(x_in[half % 2], it * 16 + 16 * (1 + half // 2))
                pe.wait_ge(x_lo_ok, it * 2 + half + 1)
                for u in range(U):
                    for c in range(C):
                        mm = pe.transpose(ps_t[:, c, u * P:(u + 1) * P], x_raw[half % 2][:, u, c * P:(c + 1) * P], ident)
                mm.then_inc(t_ok, 1)

            def gate_up(it, q):
                half, j = divmod(q, NP)
                slot, x = q % RING, half % 2
                if j == 0:
                    pe.wait_ge(x_lo_ok, it * 2 + half + 2)
                pe.wait_ge(w_lo_ok, it * (2 * NQ) + 2 * (q + 1))
                pe.wait_ge(hid_ok, it * (2 * NQ) + 2 * q + 2)
                for dst, off, ok in ((ps_g[q % 2], PIECE, g_ok), (ps_a[q % 2], 0, a_ok)):
                    for i in range(2):
                        for c in range(C):
                            cols = slice(off + c * PAIR + i * P, off + c * PAIR + (i + 1) * P)
                            wh, wl = w_hi[:, slot, cols], w_lo[:, slot, cols]
                            mm = three(pe, dst[:, i, :], wh, wl, x_hi[x][:, c, :], x_lo[x][:, c, :], c == 0, c == C - 1)
                    mm.then_inc(ok, 1)

            def down(it, q):
                half, j = divmod(q, NP)
                slot = q % RING
                if j == 0:
                    pe.wait_ge(yo_ok, it * 2 + half + 1)
                pe.wait_ge(wd_lo_ok, it * NQ + q + 1 + RING)
                for i in range(2):
                    pe.wait_ge(h_lo_ok, it * (2 * NQ) + 2 * q + i + 1)
                    cols = slice(2 * PIECE + i * D, 2 * PIECE + (i + 1) * D)
                    wh, wl = w_hi[:, slot, cols], w_lo[:, slot, cols]
                    for u in range(U):
                        tok = slice(u * P, (u + 1) * P)
                        hh, hl = h_hi[q % 2][:, i, tok], h_lo[q % 2][:, i, tok]
                        o = ps_o[half % 2][:, u, :]
                        pe.matmul(o, hh, wh, start=(j == 0 and u == 0 and i == 0), stop=False, skip_group_check=True)
                        pe.matmul(o, hh, wl, start=False, stop=False, skip_group_check=True)
                        mm = pe.matmul(o, hl, wh, start=False, stop=(j == NP - 1 and i == 1), skip_group_check=True)
                mm.then_inc(down_ok, 1)

            def pair(it, q):
                if not (is_last(it, q) and q % NP == NP - 1):
                    gate_up(it, q + 1)
                down(it, q)
                if q % NP == 0 and not is_last(it, q):
                    turn(it, q // NP + 1)

            turn(0, 0)
            gate_up(0, 0)
            peeled(pe, pair)


def program(nc, ins, out):
    k = Chip(ins, out)

    def dram(name, shape):
        return nc.dram_tensor(name, shape, F32, kind="Internal").ap()

    k.x_slots = dram("x_slots", (SLOTS, S_N))
    with ExitStack() as ctx:
        def sb(name, shape, dt=F32):
            return ctx.enter_context(nc.sbuf_tensor(name, shape, dt))

        k.tile_e = sb("tile_e", [P, NT], I32)
        k.head_sb = sb("head_sb", [P, C_HEAD])
        with ExitStack() as inner:
            def sb(name, shape, dt=F32):
                return inner.enter_context(nc.sbuf_tensor(name, shape, dt))

            k.vec_sb = sb("vec_sb", [P, V_W])
            k.rows_sb = sb("rows_sb", [P, R_W])
            k.attn_raw = sb("attn_raw", [P, W_W])
            k.c_sb = sb("c_sb", [P, B, C, S])
            stage_cond(nc, k)
            k.cst = sb("cst", [P, C_W])
            k.x2 = sb("x2", [P, C, B, S])
            k.lora_hi = sb("lora_hi", [P, W_W - W_B], F32R)
            k.lora_lo = sb("lora_lo", [P, W_W - W_B], F32R)
            k.sh_hi = sb("sh_hi", [P, 2, CHUNK], F32R)
            k.sh_lo = sb("sh_lo", [P, 2, CHUNK], F32R)
            stage_attention(nc, k)
            k.y_nat = [sb(f"y_nat{j}", [P, TT, S_N]) for j in range(2)]
            k.y_hi = sb("y_hi", [P, C, T], F32R)
            k.y_lo = sb("y_lo", [P, C, T], F32R)
            k.dif = sb("dif", [P, TT])
            k.one_hot = [sb(f"one_hot{i}", [P, TT, E]) for i in range(2)]
            stage_lora(nc, k)
            stage_route(nc, k)
        stage_experts(nc, k)


def constants():
    a = np.zeros((P, C_W), np.float32)
    a[:, C_ID:C_ID + P] = np.eye(P)
    theta = np.pi / 2 * np.arange(1, B + 1) / B
    ang = np.sin(theta)[:, None] * np.sin(theta)[None] + np.cos(theta)[:, None] * np.cos(theta)[None]
    a[:, C_MASK:C_MASK + P] = np.kron(ang, np.eye(GRP))
    a[:, C_TRI:C_TRI + P] = np.triu(np.ones((P, P)), 1)
    a[:, C_ONE:C_ONE + P] = 1
    a[:, C_SEG:C_SEG + TT * E] = np.tile(np.arange(TT) != 0, E)
    a[:, C_IOTA:C_IOTA + E] = np.arange(E)
    a[:, C_HEADS:C_PAD] = np.arange(P)[:, None] // HD == np.arange(P // HD)
    a[:, C_J256:C_J256 + E * 8] = np.tile(np.arange(8) * ES, E)
    a[:, C_TILE:C_TILE + NT * E] = np.repeat(np.arange(NT), E)
    a[:, C_TOK:C_TOK + TT] = np.arange(T).reshape(TT, P).T
    a[:, C_PAD:C_HEAD] = T + np.arange(ES).reshape(-1, P).T
    return a


def halves(w):
    return w.reshape(C, P, -1).transpose(1, 0, 2)


def packed(**i):
    f = {n: np.asarray(v) for n, v in i.items()}
    cat = lambda *a: np.concatenate([x.reshape(P, -1) for x in a], axis=1)

    def mlp(gate, up, down, pairs):
        out = []
        for j in range(pairs):
            cols = slice(j * PAIR, (j + 1) * PAIR)
            out.append(cat(halves(gate[:, cols]), halves(up[:, cols]), halves(down[cols])))
        return np.stack(out)

    g, u, d = (f["L0_cond_skill_" + n] for n in ("gate", "up", "down"))
    cond = [mlp(g[e], u[e], d[e], COND_PAIRS) for e in range(COND_E)]
    cond.append(mlp(f["L0_cond_shared_gate"], f["L0_cond_shared_up"], f["L0_cond_shared_down"], COND_PAIRS))
    w1, w2 = f["L0_ffn_We1"], f["L0_ffn_We2"]
    col = lambda v: v.reshape(-1, P).T
    qkv_b, bs1, be1 = f["L0_attn_in_proj_bias"], f["L0_ffn_bs1"], f["L0_ffn_be1"]
    bs = f["L0_cond2_Bs"].transpose(0, 2, 1).reshape(P, D)
    ffn = np.stack([mlp(w1[e][:, :HR], w1[e][:, HR:], w2[e], FFN_PAIRS) for e in range(E)])
    rows = np.concatenate([qkv_b[2 * D:], f["L0_ffn_bs2"], f["L0_ffn_br"]])
    arrays = {
        "xT": halves(f["x"].reshape(T, D).T),
        "cond_8": f["cond_8"],
        "cond_w": np.stack(cond),
        "ffn_w": np.concatenate([ffn, be1.reshape(E, 2, FFN_PAIRS, PAIR // P, P).transpose(0, 2, 4, 1, 3).reshape(
            E, FFN_PAIRS, P, B1)], axis=3),
        "shared_w": mlp(f["L0_ffn_Ws1"][:, :HS], f["L0_ffn_Ws1"][:, HS:], f["L0_ffn_Ws2"], HS // PAIR),
        "attn_w": cat(halves(f["L0_attn_in_proj_weight"].T), halves(f["L0_attn_out_w"].T),
                      halves(f["L0_cond2_W_base"].T), halves(f["L0_cond2_As"].reshape(P, D).T), bs),
        "vec": cat(col(qkv_b[:D]), col(qkv_b[D:2 * D]), col(f["L0_attn_out_b"]), col(f["L0_cond2_b_base"]),
                   col(bs1[:HS]), col(bs1[HS:])),
        "rows": np.broadcast_to(rows, (P, R_W)),
        "router": halves(f["L0_ffn_Wr"]),
        "lora_w": np.repeat(f["cond_8"].T, LR, axis=0),
        "be2": f["L0_ffn_be2"],
        "consts": constants(),
    }
    return {n: np.ascontiguousarray(a) for n, a in arrays.items()}


def kernel(**inputs):
    import concourse.bacc as _bacc
    from concourse.bass_utils import run_bass_kernel_spmd as _run

    nc = _bacc.Bacc("TRN2", target_bir_lowering=False, num_devices=1)
    arrays = packed(**inputs)
    ins = {n: nc.dram_tensor("in_" + n, a.shape, F32, kind="ExternalInput").ap() for n, a in arrays.items()}
    out = nc.dram_tensor("out", (T + ES, D), F32, kind="ExternalOutput").ap()
    program(nc, ins, out)
    r = _run(nc, [{"in_" + n: a for n, a in arrays.items()}], core_ids=[0])
    return r.results[0]["out"][:T].reshape(B, S, D)
```
